# Optimizing a Trainium2 kernel written in Bass

```python
import numpy as np
import jax
import jax.numpy as jnp

def _softmax(x, axis=-1):
    return jax.nn.softmax(x, axis=axis)

def _gelu(x):
    return jax.nn.gelu(x, approximate=True)

def _silu(x):
    return jax.nn.silu(x)

def _sigmoid(x):
    return jax.nn.sigmoid(x)

def _layernorm(x, axis=-1, eps=1e-05):
    m = jnp.mean(x, axis=axis, keepdims=True)
    v = jnp.var(x, axis=axis, keepdims=True)
    return (x - m) / jnp.sqrt(v + eps)

def _scatter_add(tgt, idx, src, axis=0):
    return tgt.at[idx].add(src)

def _segment_sum(src, seg, n):
    return jax.ops.segment_sum(src, seg, n)
kernel_name = 'mk_conv_preact_d4_conv_nchw512_r2_907f02'

def setup_inputs(seed: int=0):
    np.random.seed(seed)
    _w = jnp.asarray

    def _rec_inputs():
        import jax
        import jax.numpy as jnp
        _gk = jax.random.key(seed)
        x = -0.000125 + 0.9999 * jax.random.normal(jax.random.fold_in(_gk, 1), (16, 256, 32, 32), jnp.float32)
        return x
    x = _rec_inputs()

    def _L0_conv_setup():
        import jax, jax.numpy as jnp
        import numpy as np
        B, C, H, W = (16, 256, 32, 32)
        key = jax.random.key(seed)
        k1, k2, k3 = jax.random.split(key, 3)
        x = jax.random.normal(k1, (B, C, H, W), dtype=jnp.float32)
        fan_in = C
        bound = 1.0 / np.sqrt(fan_in)
        w = jax.random.uniform(k2, (C, C), minval=-bound, maxval=bound, dtype=jnp.float32)
        bias = jax.random.uniform(k3, (C,), minval=-bound, maxval=bound, dtype=jnp.float32)
        return {'x': x, 'w': w, 'bias': bias}
    _L0_conv_all = _L0_conv_setup()
    _L0_conv_in = {k: v for k, v in _L0_conv_all.items() if k in ('w', 'bias')}
    del _L0_conv_all

    def _L1_conv_setup():
        import jax, jax.numpy as jnp
        import numpy as np
        import math
        PERMS = ((0, 1, 2, 3, 4, 5, 6, 7), (3, 0, 1, 2, 5, 6, 7, 4), (2, 3, 0, 1, 6, 7, 4, 5), (1, 2, 3, 0, 7, 4, 5, 6), (4, 5, 6, 7, 0, 1, 2, 3), (5, 6, 7, 4, 3, 0, 1, 2), (6, 7, 4, 5, 2, 3, 0, 1), (7, 4, 5, 6, 1, 2, 3, 0))

        def d4_1x1(x, w):
            b, C, h, ww = x.shape
            cout, cin, _ = w.shape
            W = jnp.stack([w[..., jnp.array(p)] for p in PERMS], axis=1)
            xr = x.reshape(b, cin, 8, h, ww)
            y = jnp.einsum('ogif,bifhw->boghw', W, xr)
            return y.reshape(b, cout * 8, h, ww)

        def group_norm(x, gamma, beta, num_groups, eps=1e-05):
            b, C, h, w = x.shape
            xg = x.reshape(b, num_groups, C // num_groups, h, w)
            mean = xg.mean(axis=(2, 3, 4), keepdims=True)
            var = xg.var(axis=(2, 3, 4), keepdims=True)
            xn = ((xg - mean) / jnp.sqrt(var + eps)).reshape(b, C, h, w)
            return xn * gamma[None, :, None, None] + beta[None, :, None, None]

        def unfold_patches(x, k):
            b, C, h, w = x.shape
            p = (k - 1) // 2
            xp = jnp.pad(x, ((0, 0), (0, 0), (p, p), (p, p)))
            pats = jnp.stack([xp[:, :, i:i + h, j:j + w] for i in range(k) for j in range(k)], axis=2)
            return pats
        key = jax.random.key(seed)
        ks = jax.random.split(key, 4)
        b, H, W = (8, 56, 56)
        cin, cout, rr, k, gc = (32, 32, 2, 3, 16)
        cmid = cin // rr
        G = cout // gc
        x = jax.random.normal(ks[0], (b, cin * 8, H, W), jnp.float32)
        w_v = jax.random.normal(ks[1], (cout, cin, 8), jnp.float32) / math.sqrt(8 * cin / 2)
        w1 = jax.random.normal(ks[2], (cmid, cin, 8), jnp.float32) / math.sqrt(8 * cin / 2)
        gn_gamma = jnp.ones((cmid * 8,), jnp.float32)
        gn_beta = jnp.zeros((cmid * 8,), jnp.float32)
        w2 = jax.random.normal(ks[3], (k * k * G, cmid), jnp.float32) / math.sqrt(cmid)
        b2 = jnp.zeros((k * k * G,), jnp.float32)
        return {'x': x, 'w_v': w_v, 'w1': w1, 'gn_gamma': gn_gamma, 'gn_beta': gn_beta, 'w2': w2, 'b2': b2}
    _L1_conv_all = _L1_conv_setup()
    _L1_conv_in = {k: v for k, v in _L1_conv_all.items() if k in ('w_v', 'w1', 'gn_gamma', 'gn_beta', 'w2', 'b2')}
    del _L1_conv_all

    def _L2_conv_setup():
        import jax, jax.numpy as jnp
        import numpy as np
        from jax import lax
        EPS = 1e-05
        DW_THRESH = 4.0
        PW_THRESH = 0.001
        C_IN = 256
        C_OUT = 256

        def _bn(x, g, b, m, v):
            inv = g * lax.rsqrt(v + EPS)
            return x * inv[None, :, None, None] + (b - m * inv)[None, :, None, None]

        def _prune(x, thresh):
            amax = jnp.max(jnp.abs(x), axis=(2, 3), keepdims=True)
            return jnp.where(amax < thresh, jnp.zeros_like(x), x)
        key = jax.random.key(seed)
        ks = jax.random.split(key, 8)
        B, H, W = (32, 28, 28)
        x = jax.random.normal(ks[0], (B, C_IN, H, W), dtype=jnp.float32)
        dw_w = jax.random.normal(ks[1], (C_IN, 1, 3, 3), dtype=jnp.float32) * 0.1
        dw_b = jax.random.normal(ks[2], (C_IN,), dtype=jnp.float32) * 0.1
        bn1_g = jnp.ones((C_IN,), jnp.float32)
        bn1_b = jnp.zeros((C_IN,), jnp.float32)
        bn1_m = jnp.zeros((C_IN,), jnp.float32)
        bn1_v = jnp.ones((C_IN,), jnp.float32)
        pw_w = jax.random.normal(ks[3], (C_OUT, C_IN, 1, 1), dtype=jnp.float32) * 0.05
        pw_b = jax.random.normal(ks[4], (C_OUT,), dtype=jnp.float32) * 0.1
        bn2_g = jnp.ones((C_OUT,), jnp.float32)
        bn2_b = jnp.zeros((C_OUT,), jnp.float32)
        bn2_m = jnp.zeros((C_OUT,), jnp.float32)
        bn2_v = jnp.ones((C_OUT,), jnp.float32)
        return dict(x=x, dw_w=dw_w, dw_b=dw_b, bn1_g=bn1_g, bn1_b=bn1_b, bn1_m=bn1_m, bn1_v=bn1_v, pw_w=pw_w, pw_b=pw_b, bn2_g=bn2_g, bn2_b=bn2_b, bn2_m=bn2_m, bn2_v=bn2_v)
    _L2_conv_all = _L2_conv_setup()
    _L2_conv_in = {k: v for k, v in _L2_conv_all.items() if k in ('dw_w', 'dw_b', 'bn1_g', 'bn1_b', 'bn1_m', 'bn1_v', 'pw_w', 'pw_b', 'bn2_g', 'bn2_b', 'bn2_m', 'bn2_v')}
    del _L2_conv_all

    def _L3_conv_setup():
        import jax, jax.numpy as jnp
        import numpy as np
        C = 256
        G = 16
        Cg = C // G
        K = 3
        P = K * K
        PAD = 1
        STRIDE = 1
        DIL = 1
        DWK = 3
        OFFSET_SCALE = 1.0
        LN_EPS = 1e-05

        def _dcnv3_core(x, offset, mask):
            N, H, W, _ = x.shape
            Hin, Win = (H + 2 * PAD, W + 2 * PAD)
            Hout, Wout = (H, W)
            xpad = jnp.pad(x, ((0, 0), (PAD, PAD), (PAD, PAD), (0, 0)))
            base = DIL * (K - 1) // 2 + 0.5
            ref_y = (base + jnp.arange(Hout, dtype=jnp.float32) * STRIDE) / Hin
            ref_x = (base + jnp.arange(Wout, dtype=jnp.float32) * STRIDE) / Win
            ref = jnp.stack(jnp.broadcast_arrays(ref_x[None, :], ref_y[:, None]), -1)
            g1 = jnp.arange(K, dtype=jnp.float32) * DIL - DIL * (K - 1) // 2
            gxx, gyy = jnp.meshgrid(g1 / Win, g1 / Hin, indexing='ij')
            grid = jnp.stack([gxx, gyy], -1).reshape(P, 2)
            off = offset.reshape(N, Hout, Wout, G, P, 2)
            norm = jnp.array([Win, Hin], jnp.float32)
            loc = ref[None, :, :, None, None, :] + grid * OFFSET_SCALE + off * OFFSET_SCALE / norm
            px = loc[..., 0] * Win - 0.5
            py = loc[..., 1] * Hin - 0.5
            xg = xpad.reshape(N, Hin, Win, G, Cg).transpose(0, 3, 1, 2, 4).reshape(N * G, Hin, Win, Cg)
            pxg = px.transpose(0, 3, 1, 2, 4).reshape(N * G, Hout, Wout, P)
            pyg = py.transpose(0, 3, 1, 2, 4).reshape(N * G, Hout, Wout, P)
            mg = mask.transpose(0, 3, 1, 2, 4).reshape(N * G, Hout, Wout, P)

            def bilin(img, bx, by, m):
                x0 = jnp.floor(bx)
                y0 = jnp.floor(by)
                wx = (bx - x0)[..., None]
                wy = (by - y0)[..., None]
                x0i = x0.astype(jnp.int32)
                y0i = y0.astype(jnp.int32)

                def g(yy, xx):
                    valid = (yy >= 0) & (yy < Hin) & (xx >= 0) & (xx < Win)
                    v = img[jnp.clip(yy, 0, Hin - 1), jnp.clip(xx, 0, Win - 1)]
                    return v * valid[..., None]
                v00 = g(y0i, x0i)
                v01 = g(y0i, x0i + 1)
                v10 = g(y0i + 1, x0i)
                v11 = g(y0i + 1, x0i + 1)
                samp = (v00 * (1 - wx) + v01 * wx) * (1 - wy) + (v10 * (1 - wx) + v11 * wx) * wy
                return jnp.einsum('hwpc,hwp->hwc', samp, m)
            out = jax.vmap(bilin)(xg, pxg, pyg, mg)
            return out.reshape(N, G, Hout, Wout, Cg).transpose(0, 2, 3, 1, 4).reshape(N, Hout, Wout, C)
        key = jax.random.key(seed)
        ks = jax.random.split(key, 10)
        N, H, W = (2, 32, 32)
        sc = 1.0 / np.sqrt(C)
        return {'x': jax.random.normal(ks[0], (N, C, H, W), jnp.float32), 'dw_w': jax.random.normal(ks[1], (C, 1, DWK, DWK), jnp.float32) * 0.1, 'dw_b': jax.random.normal(ks[2], (C,), jnp.float32) * 0.02, 'ln_g': jnp.ones((C,), jnp.float32), 'ln_b': jnp.zeros((C,), jnp.float32), 'off_w': jax.random.normal(ks[3], (C, G * P * 2), jnp.float32) * 0.01, 'off_b': jax.random.normal(ks[4], (G * P * 2,), jnp.float32) * 0.01, 'mask_w': jax.random.normal(ks[5], (C, G * P), jnp.float32) * 0.01, 'mask_b': jnp.zeros((G * P,), jnp.float32), 'in_w': jax.random.normal(ks[6], (C, C), jnp.float32) * sc, 'in_b': jnp.zeros((C,), jnp.float32), 'out_w': jax.random.normal(ks[7], (C, C), jnp.float32) * sc, 'out_b': jnp.zeros((C,), jnp.float32)}
    _L3_conv_all = _L3_conv_setup()
    _L3_conv_in = {k: v for k, v in _L3_conv_all.items() if k in ('dw_w', 'dw_b', 'ln_g', 'ln_b', 'off_w', 'off_b', 'mask_w', 'mask_b', 'in_w', 'in_b', 'out_w', 'out_b')}
    del _L3_conv_all
    return {'x': x, 'L0_conv_w': _L0_conv_in['w'], 'L0_conv_bias': _L0_conv_in['bias'], 'L1_conv_w_v': _L1_conv_in['w_v'], 'L1_conv_w1': _L1_conv_in['w1'], 'L1_conv_gn_gamma': _L1_conv_in['gn_gamma'], 'L1_conv_gn_beta': _L1_conv_in['gn_beta'], 'L1_conv_w2': _L1_conv_in['w2'], 'L1_conv_b2': _L1_conv_in['b2'], 'L2_conv_dw_w': _L2_conv_in['dw_w'], 'L2_conv_dw_b': _L2_conv_in['dw_b'], 'L2_conv_bn1_g': _L2_conv_in['bn1_g'], 'L2_conv_bn1_b': _L2_conv_in['bn1_b'], 'L2_conv_bn1_m': _L2_conv_in['bn1_m'], 'L2_conv_bn1_v': _L2_conv_in['bn1_v'], 'L2_conv_pw_w': _L2_conv_in['pw_w'], 'L2_conv_pw_b': _L2_conv_in['pw_b'], 'L2_conv_bn2_g': _L2_conv_in['bn2_g'], 'L2_conv_bn2_b': _L2_conv_in['bn2_b'], 'L2_conv_bn2_m': _L2_conv_in['bn2_m'], 'L2_conv_bn2_v': _L2_conv_in['bn2_v'], 'L3_conv_dw_w': _L3_conv_in['dw_w'], 'L3_conv_dw_b': _L3_conv_in['dw_b'], 'L3_conv_ln_g': _L3_conv_in['ln_g'], 'L3_conv_ln_b': _L3_conv_in['ln_b'], 'L3_conv_off_w': _L3_conv_in['off_w'], 'L3_conv_off_b': _L3_conv_in['off_b'], 'L3_conv_mask_w': _L3_conv_in['mask_w'], 'L3_conv_mask_b': _L3_conv_in['mask_b'], 'L3_conv_in_w': _L3_conv_in['in_w'], 'L3_conv_in_b': _L3_conv_in['in_b'], 'L3_conv_out_w': _L3_conv_in['out_w'], 'L3_conv_out_b': _L3_conv_in['out_b']}

def reference(x, L0_conv_w, L0_conv_bias, L1_conv_w_v, L1_conv_w1, L1_conv_gn_gamma, L1_conv_gn_beta, L1_conv_w2, L1_conv_b2, L2_conv_dw_w, L2_conv_dw_b, L2_conv_bn1_g, L2_conv_bn1_b, L2_conv_bn1_m, L2_conv_bn1_v, L2_conv_pw_w, L2_conv_pw_b, L2_conv_bn2_g, L2_conv_bn2_b, L2_conv_bn2_m, L2_conv_bn2_v, L3_conv_dw_w, L3_conv_dw_b, L3_conv_ln_g, L3_conv_ln_b, L3_conv_off_w, L3_conv_off_b, L3_conv_mask_w, L3_conv_mask_b, L3_conv_in_w, L3_conv_in_b, L3_conv_out_w, L3_conv_out_b):
    import jax
    import jax.numpy as jnp

    def _L0_conv_ref(x, w, bias):
        import jax, jax.numpy as jnp
        import numpy as np
        B, C, H, W = (16, 256, 32, 32)
        b, c, h, wid = x.shape
        query = jnp.einsum('oc,bchw->bohw', w, x) + bias[None, :, None, None]
        query = query.reshape(b, c, h * wid)
        scores = jnp.einsum('bcn,bdn->bcd', query, query)
        attn = jax.nn.softmax(scores, axis=-1)
        out = jnp.einsum('bcd,bdn->bcn', attn, query).reshape(b, c, h, wid)
        return out

    def _L1_conv_ref(x, w_v, w1, gn_gamma, gn_beta, w2, b2):
        import jax, jax.numpy as jnp
        import numpy as np
        import math
        PERMS = ((0, 1, 2, 3, 4, 5, 6, 7), (3, 0, 1, 2, 5, 6, 7, 4), (2, 3, 0, 1, 6, 7, 4, 5), (1, 2, 3, 0, 7, 4, 5, 6), (4, 5, 6, 7, 0, 1, 2, 3), (5, 6, 7, 4, 3, 0, 1, 2), (6, 7, 4, 5, 2, 3, 0, 1), (7, 4, 5, 6, 1, 2, 3, 0))

        def d4_1x1(x, w):
            b, C, h, ww = x.shape
            cout, cin, _ = w.shape
            W = jnp.stack([w[..., jnp.array(p)] for p in PERMS], axis=1)
            xr = x.reshape(b, cin, 8, h, ww)
            y = jnp.einsum('ogif,bifhw->boghw', W, xr)
            return y.reshape(b, cout * 8, h, ww)

        def group_norm(x, gamma, beta, num_groups, eps=1e-05):
            b, C, h, w = x.shape
            xg = x.reshape(b, num_groups, C // num_groups, h, w)
            mean = xg.mean(axis=(2, 3, 4), keepdims=True)
            var = xg.var(axis=(2, 3, 4), keepdims=True)
            xn = ((xg - mean) / jnp.sqrt(var + eps)).reshape(b, C, h, w)
            return xn * gamma[None, :, None, None] + beta[None, :, None, None]

        def unfold_patches(x, k):
            b, C, h, w = x.shape
            p = (k - 1) // 2
            xp = jnp.pad(x, ((0, 0), (0, 0), (p, p), (p, p)))
            pats = jnp.stack([xp[:, :, i:i + h, j:j + w] for i in range(k) for j in range(k)], axis=2)
            return pats
        k, gc = (3, 16)
        b, _, h, w = x.shape
        cmid = w1.shape[0]
        G = w2.shape[0] // (k * k)
        t = jax.nn.relu(group_norm(d4_1x1(x, w1), gn_gamma, gn_beta, cmid))
        tr = t.reshape(b, cmid, 8, h, w)
        wgt = jnp.einsum('oi,bighw->boghw', w2, tr) + b2[None, :, None, None, None]
        wv = wgt.reshape(b, G, k, k, 8, h, w)
        s = [wv[:, :, :, :, g] for g in range(8)]
        sw = [jnp.swapaxes(s[g], 2, 3) for g in range(4, 8)]
        trans = [s[0], jnp.rot90(s[1], 1, (2, 3)), jnp.rot90(s[2], 2, (2, 3)), jnp.rot90(s[3], 3, (2, 3)), jnp.rot90(sw[0], 3, (2, 3)), jnp.rot90(sw[1], 2, (2, 3)), jnp.rot90(sw[2], 1, (2, 3)), sw[3]]
        wv = jnp.stack(trans, axis=4)
        wv = wv.reshape(b, G, k * k, 8, h, w)[:, :, None]
        wv = jnp.swapaxes(wv, 3, 4)
        xv = d4_1x1(x, w_v)
        pats = unfold_patches(xv, k).reshape(b, G, gc, 8, k * k, h, w)
        out = (wv * pats).sum(axis=4)
        return out.reshape(b, G * gc * 8, h, w)

    def _L2_conv_ref(x, dw_w, dw_b, bn1_g, bn1_b, bn1_m, bn1_v, pw_w, pw_b, bn2_g, bn2_b, bn2_m, bn2_v):
        import jax, jax.numpy as jnp
        import numpy as np
        from jax import lax
        EPS = 1e-05
        DW_THRESH = 4.0
        PW_THRESH = 0.001
        C_IN = 256
        C_OUT = 256

        def _bn(x, g, b, m, v):
            inv = g * lax.rsqrt(v + EPS)
            return x * inv[None, :, None, None] + (b - m * inv)[None, :, None, None]

        def _prune(x, thresh):
            amax = jnp.max(jnp.abs(x), axis=(2, 3), keepdims=True)
            return jnp.where(amax < thresh, jnp.zeros_like(x), x)
        dn = ('NCHW', 'OIHW', 'NCHW')
        h = lax.conv_general_dilated(x, dw_w, window_strides=(1, 1), padding=((1, 1), (1, 1)), feature_group_count=C_IN, dimension_numbers=dn)
        h = h + dw_b[None, :, None, None]
        h = jax.nn.relu(_bn(h, bn1_g, bn1_b, bn1_m, bn1_v))
        h = _prune(h, DW_THRESH)
        h = lax.conv_general_dilated(h, pw_w, window_strides=(1, 1), padding=((0, 0), (0, 0)), dimension_numbers=dn)
        h = h + pw_b[None, :, None, None]
        h = jax.nn.relu(_bn(h, bn2_g, bn2_b, bn2_m, bn2_v))
        h = _prune(h, PW_THRESH)
        return h

    def _L3_conv_ref(x, dw_w, dw_b, ln_g, ln_b, off_w, off_b, mask_w, mask_b, in_w, in_b, out_w, out_b):
        import jax, jax.numpy as jnp
        import numpy as np
        C = 256
        G = 16
        Cg = C // G
        K = 3
        P = K * K
        PAD = 1
        STRIDE = 1
        DIL = 1
        DWK = 3
        OFFSET_SCALE = 1.0
        LN_EPS = 1e-05

        def _dcnv3_core(x, offset, mask):
            N, H, W, _ = x.shape
            Hin, Win = (H + 2 * PAD, W + 2 * PAD)
            Hout, Wout = (H, W)
            xpad = jnp.pad(x, ((0, 0), (PAD, PAD), (PAD, PAD), (0, 0)))
            base = DIL * (K - 1) // 2 + 0.5
            ref_y = (base + jnp.arange(Hout, dtype=jnp.float32) * STRIDE) / Hin
            ref_x = (base + jnp.arange(Wout, dtype=jnp.float32) * STRIDE) / Win
            ref = jnp.stack(jnp.broadcast_arrays(ref_x[None, :], ref_y[:, None]), -1)
            g1 = jnp.arange(K, dtype=jnp.float32) * DIL - DIL * (K - 1) // 2
            gxx, gyy = jnp.meshgrid(g1 / Win, g1 / Hin, indexing='ij')
            grid = jnp.stack([gxx, gyy], -1).reshape(P, 2)
            off = offset.reshape(N, Hout, Wout, G, P, 2)
            norm = jnp.array([Win, Hin], jnp.float32)
            loc = ref[None, :, :, None, None, :] + grid * OFFSET_SCALE + off * OFFSET_SCALE / norm
            px = loc[..., 0] * Win - 0.5
            py = loc[..., 1] * Hin - 0.5
            xg = xpad.reshape(N, Hin, Win, G, Cg).transpose(0, 3, 1, 2, 4).reshape(N * G, Hin, Win, Cg)
            pxg = px.transpose(0, 3, 1, 2, 4).reshape(N * G, Hout, Wout, P)
            pyg = py.transpose(0, 3, 1, 2, 4).reshape(N * G, Hout, Wout, P)
            mg = mask.transpose(0, 3, 1, 2, 4).reshape(N * G, Hout, Wout, P)

            def bilin(img, bx, by, m):
                x0 = jnp.floor(bx)
                y0 = jnp.floor(by)
                wx = (bx - x0)[..., None]
                wy = (by - y0)[..., None]
                x0i = x0.astype(jnp.int32)
                y0i = y0.astype(jnp.int32)

                def g(yy, xx):
                    valid = (yy >= 0) & (yy < Hin) & (xx >= 0) & (xx < Win)
                    v = img[jnp.clip(yy, 0, Hin - 1), jnp.clip(xx, 0, Win - 1)]
                    return v * valid[..., None]
                v00 = g(y0i, x0i)
                v01 = g(y0i, x0i + 1)
                v10 = g(y0i + 1, x0i)
                v11 = g(y0i + 1, x0i + 1)
                samp = (v00 * (1 - wx) + v01 * wx) * (1 - wy) + (v10 * (1 - wx) + v11 * wx) * wy
                return jnp.einsum('hwpc,hwp->hwc', samp, m)
            out = jax.vmap(bilin)(xg, pxg, pyg, mg)
            return out.reshape(N, G, Hout, Wout, Cg).transpose(0, 2, 3, 1, 4).reshape(N, Hout, Wout, C)
        N, _, H, W = x.shape
        inp = jnp.transpose(x, (0, 2, 3, 1))
        xproj = inp @ in_w + in_b
        x1 = jax.lax.conv_general_dilated(x, dw_w, (1, 1), [((DWK - 1) // 2, (DWK - 1) // 2)] * 2, feature_group_count=C, dimension_numbers=('NCHW', 'OIHW', 'NCHW'))
        x1 = jnp.transpose(x1, (0, 2, 3, 1)) + dw_b
        mu = x1.mean(-1, keepdims=True)
        var = ((x1 - mu) ** 2).mean(-1, keepdims=True)
        x1 = (x1 - mu) / jnp.sqrt(var + LN_EPS) * ln_g + ln_b
        x1 = jax.nn.gelu(x1, approximate=False)
        offset = x1 @ off_w + off_b
        mask = jax.nn.softmax((x1 @ mask_w + mask_b).reshape(N, H, W, G, P), -1)
        out = _dcnv3_core(xproj, offset, mask)
        out = out @ out_w + out_b
        return jnp.transpose(out, (0, 3, 1, 2))

    def _gn(v, G=32, eps=1e-05):
        B_, C_, H_, W_ = v.shape
        g = v.reshape(B_, G, C_ // G, H_, W_)
        m = jnp.mean(g, axis=(2, 3, 4), keepdims=True)
        s = jnp.var(g, axis=(2, 3, 4), keepdims=True)
        return ((g - m) / jnp.sqrt(s + eps)).reshape(v.shape)

    def _ln_c(v, eps=1e-06):
        m = jnp.mean(v, axis=1, keepdims=True)
        s = jnp.var(v, axis=1, keepdims=True)
        return (v - m) / jnp.sqrt(s + eps)

    def _ln_t(v, eps=1e-05):
        m = jnp.mean(v, axis=-1, keepdims=True)
        s = jnp.var(v, axis=-1, keepdims=True)
        return (v - m) / jnp.sqrt(s + eps)

    def _to_tokens(v):
        B_, C_, H_, W_ = v.shape
        return v.reshape(B_, C_, H_ * W_).transpose(0, 2, 1)

    def _from_tokens(t, like):
        B_, C_, H_, W_ = like.shape
        return t.transpose(0, 2, 1).reshape(B_, C_, H_, W_)
    x = x + _L0_conv_ref(_gn(x), L0_conv_w, L0_conv_bias)
    x = x + _L1_conv_ref(_gn(x), L1_conv_w_v, L1_conv_w1, L1_conv_gn_gamma, L1_conv_gn_beta, L1_conv_w2, L1_conv_b2)
    x = x + _L2_conv_ref(_gn(x), L2_conv_dw_w, L2_conv_dw_b, L2_conv_bn1_g, L2_conv_bn1_b, L2_conv_bn1_m, L2_conv_bn1_v, L2_conv_pw_w, L2_conv_pw_b, L2_conv_bn2_g, L2_conv_bn2_b, L2_conv_bn2_m, L2_conv_bn2_v)
    x = x + _L3_conv_ref(_gn(x), L3_conv_dw_w, L3_conv_dw_b, L3_conv_ln_g, L3_conv_ln_b, L3_conv_off_w, L3_conv_off_b, L3_conv_mask_w, L3_conv_mask_b, L3_conv_in_w, L3_conv_in_b, L3_conv_out_w, L3_conv_out_b)
    return x

_drawn_inputs = setup_inputs


def setup_inputs(seed=0):
    import zlib

    import numpy as np

    out = dict(_drawn_inputs(seed))
    spreads = {'L1_conv_gn_gamma': (1.0, 0.2),
     'L1_conv_gn_beta': (0.0, 0.1),
     'L1_conv_b2': (0.0, 0.1),
     'L2_conv_bn1_g': (1.0, 0.2),
     'L2_conv_bn1_b': (0.0, 0.309),
     'L2_conv_bn1_m': (0.0, 0.402),
     'L2_conv_bn1_v': (1.0, 0.2),
     'L2_conv_bn2_g': (1.0, 0.6),
     'L2_conv_bn2_b': (0.0, 0.396),
     'L2_conv_bn2_m': (0.0, 0.348),
     'L2_conv_bn2_v': (1.0, 0.6),
     'L3_conv_ln_g': (1.0, 0.6),
     'L3_conv_ln_b': (0.0, 0.8),
     'L3_conv_in_b': (0.0, 0.281),
     'L3_conv_out_b': (0.0, 0.285)}
    factors = {'L2_conv_dw_w': 8.0,
     'L3_conv_dw_w': 3.559,
     'L3_conv_dw_b': 21.834,
     'L3_conv_off_w': 3.789,
     'L3_conv_off_b': 26.762,
     'L3_conv_mask_w': 6.374,
     'L2_conv_dw_b': 2.789}
    for name, (base, spread) in spreads.items():
        noise = np.random.default_rng([zlib.crc32(name.encode()), seed]).standard_normal(out[name].shape)
        drawn = base * np.exp(spread * noise) if base else spread * noise
        out[name] = jnp.asarray(drawn.astype(out[name].dtype))
    for name, factor in factors.items():
        out[name] = (out[name] * factor).astype(out[name].dtype)
    return out
```

```python
from contextlib import ExitStack

import concourse.bass as bass
import numpy as np
from concourse import mybir

F32 = mybir.dt.float32
I32 = mybir.dt.int32
ALU = mybir.AluOpType
ACT = mybir.ActivationFunctionType
AX = mybir.AxisListType

P = 128
B, C, H, W = 16, 256, 32, 32
K = C // P
N = H * W
HALF = N // 2
HR = H // 2
TILES = N // P
TR = P // W
GN_EPS, LN_EPS, BN_EPS = 1e-5, 1e-5, 1e-5
DW_THRESH, PW_THRESH = 4.0, 0.001
TAPS = 9
G = 16
CG = C // G
OM = G * 3 * TAPS
R = 4
D = 2 * R + 1
PADW = W + 2 * R
PADH = H + 2 * R
ROWF = PADW * CG
IMGR = TR + 2 * R
PIX = P
CORNERS = 4
PE_SUMMED = 4

COLS = {}
_at = 0
for _name, _n in (("q_bias", K), ("dw2_b", K), ("bn1_g", K), ("bn1_b", K), ("bn1_m", K), ("bn1_v", K),
                  ("pw_b", K), ("bn2_g", K), ("bn2_b", K), ("bn2_m", K), ("bn2_v", K), ("dw3_b", K),
                  ("ln_g", K), ("ln_b", K), ("out_b", K), ("t_gamma", 1), ("t_beta", 1),
                  ("dw2", K * TAPS), ("dw3", K * TAPS), ("b2", K * TAPS)):
    COLS[_name] = (_at, _n)
    _at += _n
NCOLS = _at
WTS = {}
_at = 0
for _name, _n in (("w0", C), ("wv", C), ("w1", P), ("pw", C), ("in_w", C), ("om_w", OM), ("out_w", C)):
    WTS[_name] = (_at, _n)
    _at += _n
NWTS = _at
CST = {}
_at = 0
for _name, _n in (("ident", P), ("group8", P), ("mean256", P), ("code", G * TAPS), ("group_of", G * TAPS),
                  ("group_iota", G), ("pixel_xy", TILES * 2), ("corner", CORNERS), ("minus_d", D),
                  ("grid", OM), ("half", 2), ("eps", 1)):
    CST[_name] = (_at, _n)
    _at += _n
NCST = _at


def build(nc, x_in, weights_in, w2x_in, cols_in, rows_in, consts_in, out, batches=B, layers=4):
    ctx = ExitStack()
    with ctx:
        def sb(name, shape, dt=F32):
            return ctx.enter_context(nc.sbuf_tensor(name, shape, dt))

        def sem(name):
            return ctx.enter_context(nc.semaphore(name))

        def dram(name, shape):
            return nc.dram_tensor(name, shape, F32, kind="Internal").ap()

        img_dram = dram("img_dram", [G * PADH * PADW, CG])
        om_dram = dram("om_dram", [G, TILES, PIX, 3 * TAPS])
        samp_dram = dram("samp_dram", [G, TILES, PIX, CG])

        wts = sb("wts", [P, K, NWTS])
        w2x = sb("w2x", [P, K, TAPS, P])
        cols = sb("cols", [P, NCOLS])
        rows = sb("rows", [P, C + OM])
        cst = sb("cst", [P, NCST])
        x = sb("x", [P, K, N])
        img = sb("img", [P, IMGR * ROWF])
        tb = sb("tb", [P, PIX, 3 * TAPS])
        hatx = sb("hatx", [P, D, TAPS, PIX])
        haty = sb("haty", [P, 2, TAPS, PIX])
        wy = sb("wy", [P, TAPS, PIX])
        prod = sb("prod", [P, 3, TAPS, PIX])
        tapped = sb("tapped", [P, 2, PIX * CG])
        om = sb("om", [P, TILES, OM])
        big = sb("big", [P, TILES, C])
        stats = sb("stats", [P, K, 2, 6])
        small = sb("small", [P, 64])
        keys = sb("keys", [P, TILES, G * TAPS])
        mout = sb("mout", [P, TILES, G * TAPS])
        onehot = sb("onehot", [P, G * TAPS])
        junk = sb("junk", [P, G * TAPS])
        rs = sb("rs", [P, 96])
        idx4 = sb("idx4", [P, CORNERS], I32)
        fli = sb("fli", [P, 2], I32)
        gat = sb("gat", [P, CORNERS, CG])
        tick = sb("tick", [1, 32])
        pdone = sb("pdone", [1, 1])
        gmix = sb("gmix", [P, G, CG])
        runs = sb("runs", [P, 2 * TILES + 2])
        runs_i = sb("runs_i", [1, TILES + 1], I32)

        flat = hatx[:, :, :, :].rearrange("p d t n -> p (d t n)")
        q = flat[:, 0:K * N].rearrange("p (k n) -> p k n", k=K)
        e = flat[:, K * N:K * N + K * C].rearrange("p (k n) -> p k n", k=K)
        et = flat[:, K * N + K * C:K * N + 2 * K * C].rearrange("p (k n) -> p k n", k=K)
        late = K * N + 2 * K * C
        xvp_n = K * (H + 2) * (W + 2)
        xvp = flat[:, late:late + xvp_n].rearrange("p (k h w) -> p k h w", k=K, h=H + 2)
        tr = flat[:, late + xvp_n:late + xvp_n + N]
        late = late + xvp_n + N
        acc = flat[:, late:late + K * N].rearrange("p (k n) -> p k n", k=K)
        pwm = flat[:, late + K * N:late + K * N + K * C].rearrange("p (k n) -> p k n", k=K)
        assert late + K * N + K * C <= D * TAPS * PIX
        tmp = tapped[:, 0, :].rearrange("p (b n) -> p b n", b=4)
        qT = big
        samp = big[:, :, :].rearrange("p t c -> p (t c)")
        flag = tapped[:, 1, 0:TILES * G * TAPS].rearrange("p (t m) -> p t m", t=TILES)
        xp = img[:, 0:xvp_n].rearrange("p (k h w) -> p k h w", k=K, h=H + 2)

        def cst_(name):
            a, n = CST[name]
            return cst[:, a:a + n]

        def col(name, i=0, n=1):
            return cols[:, COLS[name][0] + i:COLS[name][0] + i + n]

        def wt(name, k, a=0, n=None):
            s, m = WTS[name]
            return wts[:, k, s + a:s + a + (m if n is None else n)]

        ident = cst_("ident")
        ps = ctx.enter_context(nc.psum_tensor("ps", [P, 8, 512], F32))

        s_load = sem("s_weights_loaded")
        s_x = sem("s_x_loaded")
        s_stored = sem("s_x_stored")
        s_zero = sem("s_border_zeroed")
        s_zeroed_dram = sem("s_dram_border_zeroed")
        s_xpz = sem("s_xp_border_zeroed")
        s_gz = sem("s_samp_zeroed")
        s_vset = sem("s_vector_setup")
        s_gset = sem("s_pool_setup")
        s_v = sem("s_vector_chain")
        s_a = sem("s_scalar_chain")
        s_gstat = sem("s_channel_stats")
        s_gsum = sem("s_group_stats")
        s_var = sem("s_group_variance")
        s_rstd = sem("s_group_rstd")
        s_norm = sem("s_normed")
        s_q = sem("s_q_psum")
        s_qs = sem("s_q_sbuf")
        s_qt = sem("s_qT_psum")
        s_qtv = sem("s_qT_sbuf_by_vector")
        s_qta = sem("s_qT_sbuf_by_scalar")
        s_sc = sem("s_scores_psum")
        s_mx = sem("s_score_max")
        s_e = sem("s_exp_scores")
        s_et = sem("s_eT_psum")
        s_ets = sem("s_eT_sbuf")
        s_att = sem("s_attention_psum")
        s_t1 = sem("s_t_psum")
        s_tsc = sem("s_t_scale")
        s_tr = sem("s_t_relu")
        s_xv = sem("s_xv_psum")
        s_xvs = sem("s_xv_sbuf")
        s_xvz = sem("s_xv_border_zeroed")
        s_w = sem("s_kernel_psum")
        s_wu = sem("s_kernel_used")
        s_dw = sem("s_depthwise_done")
        s_h = sem("s_h_relu")
        s_pwm = sem("s_pruned_pointwise_weights")
        s_pw = sem("s_pointwise_psum")
        s_h2 = sem("s_h2_relu")
        s_flat = sem("s_normed_unbordered")
        s_xpr = sem("s_xproj_psum")
        s_xprs = sem("s_xproj_sbuf")
        s_imgw = sem("s_img_in_dram")
        s_dw3 = sem("s_depthwise3_done")
        s_mean = sem("s_ln_mean_psum")
        s_cent = sem("s_ln_centered")
        s_sq = sem("s_ln_squared")
        s_lvar = sem("s_ln_var_psum")
        s_sd = sem("s_ln_sd")
        s_xhat = sem("s_ln_normed")
        s_gelu = sem("s_gelu")
        s_om = sem("s_om_psum")
        s_oms = sem("s_om_sbuf")
        s_msub = sem("s_mask_minus_max")
        s_mexp = sem("s_mask_exp")
        s_omr = sem("s_om_final")
        s_omw = sem("s_om_in_dram")
        s_tb = sem("s_om_by_group_loaded")
        s_img = sem("s_img_by_group_loaded")
        s_cnt = sem("s_sparse_counts")
        s_cntr = sem("s_sparse_count_max")
        s_runs = sem("s_sparse_runs")
        s_hx = sem("s_hat_x")
        s_hy = sem("s_hat_y")
        s_wyd = sem("s_wy")
        s_prod = sem("s_hat_products")
        s_wd = sem("s_tap_weight_psum")
        s_tap = sem("s_tapped_for_sum")
        s_tapv = sem("s_tap_weight_used")
        s_vacc = sem("s_vector_sum")
        s_vmul = sem("s_vector_tap")
        s_psum = sem("s_tensor_sum")
        s_samp = sem("s_sampled")
        s_sampw = sem("s_sampled_in_dram")
        s_sampp = sem("s_sampled_by_pixel")
        s_rv = sem("s_sparse_chain")
        s_idx = sem("s_sparse_indices")
        s_gat = sem("s_sparse_gathered")
        s_gatu = sem("s_sparse_gathered_used")
        s_gd = sem("s_sparse_gather_done")
        s_mixed = sem("s_sparse_added")
        s_oT = sem("s_outT_psum")
        s_oTs = sem("s_outT_sbuf")
        s_fin = sem("s_out_psum")
        s_xdone = sem("s_x_final")

        N_LOAD = 5
        block = ctx.enter_context(nc.Block())

        def bank(b, n=512, at=0):
            return ps[:, b, at:at + n]

        def rows_of(t3, k, half):
            return t3[:, k, 1 + half * HR:1 + (half + 1) * HR, 1:1 + W]

        def shifted(t3, k, i, j, r0=0, nr=H):
            return t3[:, k, r0 + i:r0 + i + nr, j:j + W]

        cells = iter(range(32))

        def wait_apart(eng, semaphore, value):
            i = next(cells)
            cell = tick[:, i:i + 1]
            if eng is nc.tensor:
                value = eng.snap(value)
                eng.wait_ge(s_load, 16 * N_LOAD)
            eng.wait_ge(semaphore, value)
            if eng is nc.vector:
                eng.memset(cell, 0.0)
            elif eng is nc.gpsimd:
                eng.tensor_tensor(cell, cst_("half")[0:1, 0:1], cst_("half")[0:1, 0:1], ALU.add)

        @block.sync
        def _(sp):
            sp.dma_start(wts[:, :, :], weights_in.rearrange("k p n -> p k n")).then_inc(s_load, 16)
            sp.dma_start(w2x[:, :, :, :].rearrange("p k t n -> p (k t n)"), w2x_in).then_inc(s_load, 16)
            sp.dma_start(cols[:, :], cols_in).then_inc(s_load, 16)
            sp.dma_start(rows[:, :], rows_in).then_inc(s_load, 16)
            sp.dma_start(cst[:, :], consts_in).then_inc(s_load, 16)
            sp.wait_ge(s_zero, 1)
            sp.dma_start(img_dram.rearrange("(p n) c -> p (n c)", p=P), img[:, 0:G * PADH * PADW * CG // P])\
                .then_inc(s_zeroed_dram, 16)
            sp.wait_ge(s_zeroed_dram, 16)
            with sp.Fori(0, batches) as n:
                sp.wait_ge(s_stored, n * 16)
                sp.dma_start(x[:, :, :], x_in[bass.ds(n, 1)].rearrange("o (k p) n -> p (o k) n", p=P))\
                    .then_inc(s_x, 16)
                if layers > 3:
                    grouped = img_dram.rearrange("(g y x) c -> y x g c", g=G, y=PADH)
                    for t in range(TILES):
                        sp.wait_ge(s_xprs, n * TILES + t + 1)
                        for r in range(TR):
                            y = R + t * TR + r
                            sp.dma_start(grouped[y, R:R + W], big[r * W:(r + 1) * W, t, :].rearrange(
                                "p (g c) -> p g c", g=G)).then_inc(s_imgw, 16)
                    sp.wait_ge(s_imgw, (n + 1) * 16 * TILES * TR)
                    sp.wait_ge(s_dw3, n * 2 + 2)
                    gs = img_dram.rearrange("(g y x) c -> g (y x c)", g=G, y=PADH)
                    for g in range(G):
                        src = bass.AP(gs.tensor, g * PADH * ROWF, [[TR * ROWF, TILES], [1, IMGR * ROWF]])
                        sp.dma_start(img[g * TILES:(g + 1) * TILES, :], src).then_inc(s_img, 16)
                    sp.wait_ge(s_omr, n + 1)
                    for t in range(TILES):
                        sp.dma_start(om_dram[:, t].rearrange("g n m -> n g m"),
                                     om[:, t, :].rearrange("p (g m) -> p g m", g=G)).then_inc(s_omw, 16)
                    sp.wait_ge(s_omw, (n + 1) * 16 * TILES)
                    sp.dma_start(tb[:, :, :].rearrange("p n m -> p (n m)"),
                                 om_dram.rearrange("g t n m -> (g t) (n m)")).then_inc(s_tb, 16)
                    sp.wait_ge(s_samp, n + 1)
                    sp.dma_start(samp_dram.rearrange("g t n c -> (g t) (n c)"), samp).then_inc(s_sampw, 16)
                    sp.wait_ge(s_sampw, (n + 1) * 16)
                    for t in range(TILES):
                        sp.dma_start(big[:, t, :].rearrange("p (g c) -> p g c", g=G),
                                     samp_dram[:, t].rearrange("g n c -> n g c")).then_inc(s_sampp, 16)
                sp.wait_ge(s_xdone, n + 1)
                sp.dma_start(out[bass.ds(n, 1)].rearrange("o (k p) n -> p (o k) n", p=P), x[:, :, :])\
                    .then_inc(s_stored, 16)
            sp.wait_ge(s_stored, 16 * batches)

        @block.tensor
        def _(pe):
            pe.wait_ge(s_load, 16 * N_LOAD)

            def group_stats(j, c):
                pe.wait_ge(s_gstat, j)
                pe.matmul(bank(7, c), cst_("group8"), small[:, 0:c], start=True, stop=True).then_inc(s_gsum, 1)

            with pe.Fori(0, batches) as n:
                stat0 = n * (5 if layers > 1 else 1) if layers < 4 else n * 5
                if layers in (1, 2, 3):
                    stat0 = n * {1: 1, 2: 3, 3: 4}[layers]
                group_stats(stat0 + 1, 4)
                pe.wait_ge(s_norm, n * layers + 1)
                for m in range(K):
                    for h in range(2):
                        for k in range(K):
                            mm = pe.matmul(bank(2 * m + h), wt("w0", k, m * P, P), rows_of(xp, k, h),
                                           start=(k == 0), stop=(k == K - 1))
                        mm.then_inc(s_q, 1)
                pe.wait_ge(s_qs, n * 4 + 4)
                for j in range(4):
                    for t in (2 * j, 2 * j + 1):
                        for m in range(K):
                            mm = pe.transpose(bank(j, P, (t % 2) * C + m * P), q[:, m, t * P:(t + 1) * P], ident)
                    mm.then_inc(s_qt, 1)
                pe.wait_ge(s_qtv, n * 2 + 2)
                pe.wait_ge(s_qta, n * 2 + 2)
                for m in range(K):
                    for t in range(TILES):
                        mm = pe.matmul(bank(4, C, m * C), qT[:, t, m * P:(m + 1) * P], qT[:, t, :],
                                       start=(t == 0), stop=(t == TILES - 1))
                mm.then_inc(s_sc, 1)
                pe.wait_ge(s_e, n * 2 + 2)
                for d in range(K):
                    for m in range(K):
                        mm = pe.transpose(bank(5, P, d * C + m * P), e[:, m, d * P:(d + 1) * P], ident)
                mm.then_inc(s_et, 1)
                pe.wait_ge(s_ets, n + 1)
                for m in range(K):
                    for h in range(2):
                        for d in range(K):
                            mm = pe.matmul(bank(2 * m + h), et[:, d, m * P:(m + 1) * P],
                                           q[:, d, h * HALF:(h + 1) * HALF], start=(d == 0), stop=(d == K - 1))
                        mm.then_inc(s_att, 1)

                if layers > 1:
                    group_stats(stat0 + 2, 4)
                    pe.wait_ge(s_norm, n * layers + 2)
                    for h in range(2):
                        for k in range(K):
                            mm = pe.matmul(bank(h), wt("w1", k), rows_of(xp, k, h), start=(k == 0), stop=(k == K - 1))
                        mm.then_inc(s_t1, 1)
                    for m in range(K):
                        for h in range(2):
                            for k in range(K):
                                mm = pe.matmul(bank(2 + 2 * m + h), wt("wv", k, m * P, P), rows_of(xp, k, h),
                                               start=(k == 0), stop=(k == K - 1))
                            mm.then_inc(s_xv, 1)
                    group_stats(stat0 + 3, 2)
                    pe.wait_ge(s_tr, n + 1)
                    pe.wait_ge(s_xvs, n * 4 + 4)
                    for i in range(K * TAPS * 2):
                        m, tap, h = i // (2 * TAPS), i // 2 % TAPS, i % 2
                        if i >= 4:
                            pe.wait_ge(s_wu, n * 2 * K * TAPS + i - 3)
                        pe.matmul(bank(i % 4), w2x[:, m, tap, :], tr[:, h * HALF:(h + 1) * HALF],
                                  start=True, stop=True).then_inc(s_w, 1)
                if layers > 2:
                    group_stats(stat0 + 4, 4)
                    pe.wait_ge(s_h, n * 2 + 2)
                    pe.wait_ge(s_pwm, n * 2 + 2)
                    for m in range(K):
                        for h in range(2):
                            for k in range(K):
                                mm = pe.matmul(bank(2 * m + h), pwm[:, k, m * P:(m + 1) * P],
                                               q[:, k, h * HALF:(h + 1) * HALF], start=(k == 0), stop=(k == K - 1))
                            mm.then_inc(s_pw, 1)
                if layers > 3:
                    group_stats(stat0 + 5, 4)
                    pe.wait_ge(s_flat, n * 2 + 2)
                    for t in range(TILES):
                        for k in range(K):
                            mm = pe.matmul(bank(t // 2, C, t % 2 * C), acc[:, k, t * P:(t + 1) * P],
                                           wt("in_w", k), start=(k == 0), stop=(k == K - 1))
                        if t % 2:
                            mm.then_inc(s_xpr, 1)
                    pe.wait_ge(s_dw3, n * 2 + 2)
                    for h in range(2):
                        for k in range(K):
                            mm = pe.matmul(bank(4 + h), cst_("mean256"), q[:, k, h * HALF:(h + 1) * HALF],
                                           start=(k == 0), stop=(k == K - 1))
                        mm.then_inc(s_mean, 1)
                    pe.wait_ge(s_sq, n * 2 + 2)
                    for h in range(2):
                        for k in range(K):
                            mm = pe.matmul(bank(4 + h), cst_("mean256"), acc[:, k, h * HALF:(h + 1) * HALF],
                                           start=(k == 0), stop=(k == K - 1))
                        mm.then_inc(s_lvar, 1)
                    pe.wait_ge(s_gelu, n * 2 + 2)
                    pe.wait_ge(s_xprs, n * TILES + TILES)
                    for t in range(TILES):
                        if t >= 4:
                            pe.wait_ge(s_oms, n * TILES + t - 3)
                        for k in range(K):
                            mm = pe.matmul(bank(t % 4, OM), q[:, k, t * P:(t + 1) * P], wt("om_w", k),
                                           start=(k == 0), stop=(k == K - 1))
                        mm.then_inc(s_om, 1)
                    wait_apart(pe, s_oms, n * TILES + TILES)

                    def weight(dy, d):
                        u = n * (D * D) + dy * D + d
                        pe.wait_ge(s_prod, u + 1)
                        if d >= 2:
                            pe.wait_ge(s_tapv, u - 1)
                        for p in range(TAPS):
                            mm = pe.matmul(bank(4 + d % 2, PIX), ident, prod[:, d % 3, p, :],
                                           start=(p == 0), stop=(p == TAPS - 1))
                        mm.then_inc(s_wd, 1)

                    with pe.Fori(0, D) as dy:
                        pe.wait_ge(s_tapv, n * (D * D) + dy * D)
                        weight(dy, 0)
                        for d in range(D):
                            if d + 1 < D:
                                weight(dy, d + 1)
                            if d < PE_SUMMED:
                                v = (n * D + dy) * PE_SUMMED + d
                                pe.wait_ge(s_tap, v + 1)
                                for b in range(4):
                                    mm = pe.matmul(bank(b), ident, tapped[:, d % 2, b * 512:(b + 1) * 512],
                                                   start=False, stop=False, skip_group_check=True)
                                mm.then_inc(s_psum, 1)
                    pe.wait_ge(s_mixed, n + 1)
                    for k in range(K):
                        for t in range(TILES):
                            mm = pe.transpose(bank(4 + 2 * k + t // 4, P, t % 4 * P), big[:, t, k * P:(k + 1) * P], ident)
                        mm.then_inc(s_oT, 1)
                    pe.wait_ge(s_oTs, n * 4 + 4)
                    for m in range(K):
                        for h in range(2):
                            for k in range(K):
                                mm = pe.matmul(bank(2 * m + h), wt("out_w", k, m * P, P),
                                               q[:, k, h * HALF:(h + 1) * HALF], start=(k == 0), stop=(k == K - 1))
                            mm.then_inc(s_fin, 1)

        @block.vector
        def _(ve):
            vec = nc.vector
            vec.memset(img[:, :], 0.0).then_inc(s_zero, 1)
            ve.wait_ge(s_load, 16 * N_LOAD)
            for i, bn in enumerate(("bn1", "bn2")):
                vec.tensor_scalar(col(bn + "_v", 0, K), col(bn + "_v", 0, K), BN_EPS, None, ALU.add)\
                    .then_inc(s_vset, 1)
            vec.tensor_tensor(rows[:, C:C + OM], rows[:, C:C + OM], cst_("grid"), ALU.add).then_inc(s_vset, 1)
            vec.memset(runs[:, :], 0.0).then_inc(s_vset, 1)
            ve.wait_ge(s_gset, 2)
            for i, (bn, bias) in enumerate((("bn1", "dw2_b"), ("bn2", "pw_b"))):
                at = 4 + 4 * i
                vec.tensor_tensor(col(bn + "_g", 0, K), col(bn + "_g", 0, K), col(bn + "_v", 0, K), ALU.mult)\
                    .then_inc(s_vset, 1)
                vec.tensor_tensor(col(bias, 0, K), col(bias, 0, K), col(bn + "_m", 0, K), ALU.subtract)\
                    .then_inc(s_vset, 1)
                ve.wait_ge(s_vset, at + 2)
                vec.tensor_tensor(col(bias, 0, K), col(bias, 0, K), col(bn + "_g", 0, K), ALU.mult)\
                    .then_inc(s_vset, 1)
                ve.wait_ge(s_vset, at + 3)
                vec.tensor_tensor(col(bias, 0, K), col(bias, 0, K), col(bn + "_b", 0, K), ALU.add)\
                    .then_inc(s_vset, 1)

            chain = {"k": 0}

            with ve.Fori(0, batches) as n:
                per = VLINKS[layers]

                def link(ins, alone=False):
                    chain["k"] += 1
                    ins.then_inc(s_v, 1)
                    if alone:
                        wait_apart(ve, s_v, n * per + chain["k"])
                    else:
                        ve.wait_ge(s_v, n * per + chain["k"])

                def moments(src, c, stat):
                    for k in range(c):
                        for h in range(2):
                            last = vec.bn_stats(stats[:, k, h, :], src(k, h))
                    link(last, alone=True)
                    for k in range(c):
                        last = vec.bn_aggr(small[:, 2 * k:2 * k + 2], stats[:, k, :, :].rearrange("p a b -> p (a b)"))
                    link(last)
                    mean, var = small[:, 0:2 * c:2], small[:, 1:2 * c:2]
                    link(vec.tensor_tensor(small[:, 8:8 + c], mean, mean, ALU.mult))
                    vec.tensor_tensor(var, var, small[:, 8:8 + c], ALU.add).then_inc(s_gstat, 1)
                    ve.wait_ge(s_gsum, stat)
                    link(vec.tensor_copy(small[:, 12:12 + 2 * c], bank(7, 2 * c)))
                    mean, msq = small[:, 12:12 + 2 * c:2], small[:, 13:12 + 2 * c:2]
                    link(vec.tensor_tensor(small[:, 20:20 + c], mean, mean, ALU.mult))
                    link(vec.tensor_tensor(small[:, 24:24 + c], msq, small[:, 20:20 + c], ALU.subtract))
                    vec.tensor_scalar(small[:, 24:24 + c], small[:, 24:24 + c], GN_EPS, None, ALU.add)\
                        .then_inc(s_var, 1)
                    ve.wait_ge(s_rstd, stat)
                    return mean

                def group_norm(stat):
                    mean = moments(lambda k, h: x[:, k, h * HALF:(h + 1) * HALF], K, stat)
                    for k in range(K):
                        last = vec.tensor_scalar(xp[:, k, 1:1 + H, 1:1 + W], x[:, k, :].rearrange("p (h w) -> p h w", h=H),
                                                 mean[:, k:k + 1], small[:, 28 + k:29 + k], ALU.subtract, ALU.mult)
                    last.then_inc(s_norm, 1)

                def depthwise(dst, w, bias):
                    for k in range(K):
                        o = dst[:, k, :].rearrange("p (h w) -> p h w", h=H)
                        wcol = lambda tap: col(w, k * TAPS + tap)
                        if bias is None:
                            link(vec.tensor_scalar(o, shifted(xp, k, 0, 0), wcol(0), None, ALU.mult))
                        else:
                            link(vec.tensor_scalar(o, shifted(xp, k, 0, 0), wcol(0), col(bias, k), ALU.mult, ALU.add))
                        for tap in range(1, TAPS):
                            last = vec.scalar_tensor_tensor(out=o, in0=shifted(xp, k, tap // 3, tap % 3), scalar=wcol(tap),
                                                            in1=o, op0=ALU.mult, op1=ALU.add)
                            if tap < TAPS - 1:
                                link(last)
                        last.then_inc(s_dw if w == "dw2" else s_dw3, 1)

                nst = {1: 1, 2: 3, 3: 4, 4: 5}[layers]
                ve.wait_ge(s_x, n * 16 + 16)
                ve.wait_ge(s_xpz, n + 1)
                group_norm(n * nst + 1)
                for j in (0, 2):
                    ve.wait_ge(s_qt, n * 4 + j + 1)
                    vec.tensor_copy(qT[:, 2 * j:2 * j + 2, :].rearrange("p t c -> p (t c)"), bank(j)).then_inc(s_qtv, 1)
                ve.wait_ge(s_sc, n + 1)
                vec.tensor_reduce(small[:, 32:34], bank(4).rearrange("p (m d) -> p m d", m=K), AX.X, ALU.max,
                                  negate=True).then_inc(s_mx, 1)
                ve.wait_ge(s_et, n + 1)
                vec.tensor_copy(et[:, :, :].rearrange("p k n -> p (k n)"), bank(5)).then_inc(s_ets, 1)
                link(vec.reciprocal(small[:, 36:38], small[:, 34:36]))
                for m in range(K):
                    for h in range(2):
                        ve.wait_ge(s_att, n * 4 + 2 * m + h + 1)
                        o = x[:, m, h * HALF:(h + 1) * HALF]
                        last = vec.scalar_tensor_tensor(out=o, in0=bank(2 * m + h), scalar=small[:, 36 + m:37 + m],
                                                        in1=o, op0=ALU.mult, op1=ALU.add)
                link(last)
                if layers > 1:
                    group_norm(n * nst + 2)
                    ve.wait_ge(s_t1, n * 2 + 2)
                    mean = moments(lambda k, h: bank(h), 1, n * nst + 3)
                    link(vec.tensor_tensor(small[:, 40:41], col("t_gamma"), small[:, 28:29], ALU.mult))
                    link(vec.tensor_tensor(small[:, 42:43], mean, small[:, 40:41], ALU.mult))
                    vec.tensor_tensor(small[:, 41:42], col("t_beta"), small[:, 42:43], ALU.subtract).then_inc(s_tsc, 1)
                    ve.wait_ge(s_xvz, n + 1)
                    ve.wait_ge(s_xvs, n * 4 + 4)
                    for i in range(K * TAPS * 2):
                        m, tap, h = i // (2 * TAPS), i // 2 % TAPS, i % 2
                        ve.wait_ge(s_w, n * 2 * K * TAPS + i + 1)
                        o = acc[:, m, h * HALF:(h + 1) * HALF]
                        t = o if tap == 0 else tmp[:, h, :]
                        vec.scalar_tensor_tensor(
                            out=t.rearrange("p (h w) -> p h w", w=W), in0=bank(i % 4).rearrange("p (h w) -> p h w", w=W),
                            scalar=col("b2", m * TAPS + tap), in1=shifted(xvp, m, tap // 3, tap % 3, h * HR, HR),
                            op0=ALU.add, op1=ALU.mult).then_inc(s_wu, 1)
                        if tap > 0:
                            ve.wait_ge(s_wu, n * 2 * K * TAPS + i + 1)
                            last = vec.tensor_tensor(o, o, t, ALU.add)
                            if h == 1:
                                link(last)
                    for m in range(K):
                        last = vec.tensor_tensor(x[:, m, :], x[:, m, :], acc[:, m, :], ALU.add)
                    link(last)
                if layers > 2:
                    group_norm(n * nst + 4)
                    link_norm = ve.wait_ge(s_norm, n * layers + 3)
                    depthwise(acc, "dw2", None)
                    ve.wait_ge(s_h, n * 2 + 2)
                    for k in range(K):
                        last = vec.tensor_reduce(small[:, 44 + k:45 + k], q[:, k, :], AX.X, ALU.max)
                    link(last)
                    link(vec.tensor_scalar(small[:, 46:48], small[:, 44:46], DW_THRESH, None, ALU.is_ge))
                    for k in range(K):
                        vec.tensor_scalar(pwm[:, k, :], wt("pw", k), small[:, 46 + k:47 + k], None, ALU.mult)\
                            .then_inc(s_pwm, 1)
                    ve.wait_ge(s_h2, n * 4 + 4)
                    for k in range(K):
                        last = vec.tensor_reduce(small[:, 48 + k:49 + k], acc[:, k, :], AX.X, ALU.max)
                    link(last)
                    link(vec.tensor_scalar(small[:, 50:52], small[:, 48:50], PW_THRESH, None, ALU.is_ge))
                    for k in range(K):
                        last = vec.scalar_tensor_tensor(out=x[:, k, :], in0=acc[:, k, :], scalar=small[:, 50 + k:51 + k],
                                                        in1=x[:, k, :], op0=ALU.mult, op1=ALU.add)
                    link(last)
                if layers > 3:
                    group_norm(n * nst + 5)
                    ve.wait_ge(s_norm, n * layers + 4)
                    for t in range(TILES):
                        if t % 2 == 0:
                            ve.wait_ge(s_xpr, n * 4 + t // 2 + 1)
                        vec.tensor_tensor(big[:, t, :], bank(t // 2, C, t % 2 * C), rows[:, 0:C], ALU.add)\
                            .then_inc(s_xprs, 1)
                    depthwise(q, "dw3", "dw3_b")
                    ve.wait_ge(s_mean, n * 2 + 2)
                    for k in range(K):
                        for h in range(2):
                            o = q[:, k, h * HALF:(h + 1) * HALF]
                            last = vec.tensor_tensor(o, o, bank(4 + h), ALU.subtract)
                        last.then_inc(s_cent, 1)
                    ve.wait_ge(s_sd, n * 2 + 2)
                    link(vec.reciprocal(tr, tr))
                    for k in range(K):
                        vec.tensor_tensor(q[:, k, :], q[:, k, :], tr, ALU.mult).then_inc(s_xhat, 1)
                    for t in range(TILES):
                        ve.wait_ge(s_om, n * TILES + t + 1)
                        vec.tensor_tensor(om[:, t, :], bank(t % 4, OM), rows[:, C:C + OM], ALU.add).then_inc(s_oms, 1)
                    ve.wait_ge(s_oms, n * TILES + TILES)
                    for b in range(4):
                        vec.memset(bank(b), 0.0)
                    planes = om[:, :, :].rearrange("p t (g c m) -> p (t g) c m", g=G, c=3)
                    tx, ty, mask = planes[:, :, 0, :], planes[:, :, 1, :], planes[:, :, 2, :]
                    red = junk[:, 0:TILES * G]
                    wide = red.rearrange("p (a o) -> p a o", o=1).broadcast_to([P, TILES * G, TAPS])
                    link(vec.tensor_reduce(red, mask, AX.X, ALU.max))
                    vec.tensor_tensor(mask, mask, wide, ALU.subtract).then_inc(s_msub, 1)
                    ve.wait_ge(s_mexp, n + 1)
                    link(vec.tensor_reduce(red, mask, AX.X, ALU.add))
                    link(vec.reciprocal(red, red))
                    link(vec.tensor_tensor(mask, mask, wide, ALU.mult))
                    f3 = flag[:, :, :].rearrange("p t (g m) -> p (t g) m", g=G)
                    m3 = mout[:, :, :].rearrange("p t (g m) -> p (t g) m", g=G)
                    for o, t in ((f3, tx), (m3, ty)):
                        last = vec.scalar_tensor_tensor(out=o, in0=t, scalar=-1.0, in1=t, op0=ALU.mult, op1=ALU.max)
                    link(last)
                    link(vec.tensor_tensor(f3, f3, m3, ALU.max))
                    link(vec.tensor_scalar(f3, f3, float(R), None, ALU.is_gt))
                    link(vec.tensor_tensor(m3, mask, f3, ALU.mult))
                    vec.tensor_tensor(mask, mask, m3, ALU.subtract).then_inc(s_omr, 1)
                    code = cst_("code").rearrange("p (o m) -> p o m", o=1).broadcast_to([P, TILES, G * TAPS])
                    link(vec.tensor_tensor(keys[:, :, :], flag[:, :, :], code, ALU.mult))
                    vec.tensor_reduce(runs[:, 0:TILES], flag[:, :, :], AX.X, ALU.add).then_inc(s_cnt, 1)
                    ve.wait_ge(s_cntr, n + 1)
                    base = 2 * TILES
                    link(vec.tensor_scalar(runs[:, TILES:2 * TILES], runs[:, TILES:2 * TILES], 1.0, None, ALU.max))
                    for t in range(TILES):
                        prev = runs[:, base:base + 1] if t == 0 else runs[:, TILES + t - 1:TILES + t]
                        link(vec.tensor_tensor(runs[:, TILES + t:TILES + t + 1], prev, runs[:, TILES + t:TILES + t + 1], ALU.add))
                    vec.tensor_copy(runs_i[0:1, 0:1], runs[0:1, base:base + 1])
                    vec.tensor_copy(runs_i[0:1, 1:TILES + 1], runs[0:1, TILES:2 * TILES]).then_inc(s_runs, 1)
                    ve.wait_ge(s_runs, n + 1)
                    link(vec.tensor_copy(runs[:, base:base + 1], runs[:, 2 * TILES - 1:2 * TILES]))

                    wait_apart(ve, s_img, (n + 1) * 16 * G)
                    wait_apart(ve, s_gz, n + 1)
                    imgv = img[:, :].rearrange("p (y x) -> p y x", y=IMGR)
                    spread = [TR, W, CG]

                    with ve.Fori(0, D) as dy:
                        for d in range(D):
                            u = n * (D * D) + dy * D + d
                            ve.wait_ge(s_wd, u + 1)
                            wtap = bank(4 + d % 2, PIX).rearrange("p (r x o) -> p r x o", r=TR, o=1)\
                                .broadcast_to([P] + spread)
                            src = imgv[:, bass.ds(dy, TR), d * CG:(d + W) * CG].rearrange("p r (x c) -> p r x c", c=CG)
                            if d < PE_SUMMED:
                                v = (n * D + dy) * PE_SUMMED + d
                                if d >= 2:
                                    ve.wait_ge(s_psum, v - 1)
                                else:
                                    ve.wait_ge(s_psum, (n * D + dy) * PE_SUMMED)
                                dst = tapped[:, d % 2, :].rearrange("p (r x c) -> p r x c", r=TR, c=CG)
                                vec.tensor_tensor(dst, wtap, src, ALU.mult).then_inc(s_tap, 1)
                                ve.wait_ge(s_tap, v + 1)
                                vec.memset(small[0:1, 63:64], 0.0).then_inc(s_tapv, 1)
                            else:
                                for b in range(2):
                                    rr = slice(b * TR // 2, (b + 1) * TR // 2)
                                    v2 = ((n * D + dy) * (D - PE_SUMMED) + d - PE_SUMMED) * 2 + b
                                    dst = ps[:, 6:8, :].rearrange("p b n -> p (b n)")
                                    ins = vec.tensor_tensor(dst.rearrange("p (r x c) -> p r x c", r=TR // 2, c=CG),
                                                            wtap[:, rr], src[:, rr], ALU.mult)
                                    ins.then_inc(s_vmul, 1)
                                    ve.wait_ge(s_vmul, v2 + 1)
                                    o = samp[:, b * 1024:(b + 1) * 1024]
                                    last = vec.tensor_tensor(o, o, dst, ALU.add)
                                    last.then_inc(s_vacc, 1)
                                    ve.wait_ge(s_vacc, v2 + 1)
                                vec.memset(small[0:1, 63:64], 0.0).then_inc(s_tapv, 1)
                    ve.wait_ge(s_psum, (n + 1) * D * PE_SUMMED)
                    vec.tensor_tensor(samp, samp, ps[:, 0:4, :].rearrange("p b n -> p (b n)"), ALU.add)\
                        .then_inc(s_samp, 1)
                    wait_apart(ve, s_sampp, (n + 1) * 16 * TILES)
                    with ve.Fori(0, TILES) as t:
                        first = ve.value_load(runs_i[0:1, bass.ds(t, 1)], min_val=0, max_val=1 << 20)
                        end = ve.value_load(runs_i[0:1, bass.ds(t + 1, 1)], min_val=0, max_val=1 << 20)
                        omt = om[:, bass.ds(t, 1), :].rearrange("p o (g c m) -> p (o g) c m", g=G, c=3)
                        key = keys[:, bass.ds(t, 1), :].rearrange("p o m -> p (o m)")
                        mo = mout[:, bass.ds(t, 1), :].rearrange("p o m -> p (o m)")
                        g3 = lambda ap: ap.rearrange("p (g m) -> p g m", g=G)
                        with ve.Fori(first, end) as it:
                            rk = {"k": 0}

                            def rlink(ins):
                                rk["k"] += 1
                                ins.then_inc(s_rv, 1)
                                ve.wait_ge(s_rv, it * RLINKS + rk["k"])

                            top, sel, pos, flr, frac = rs[:, 0:8], rs[:, 8:12], rs[:, 12:14], rs[:, 14:16], rs[:, 16:18]
                            wxa, wya, w4 = rs[:, 18:20], rs[:, 20:22], rs[:, 22:26]
                            lin, gsel = rs[:, 26:28], rs[:, 28:44]
                            val, up = rs[:, 44:60], rs[:, 60:62]
                            rlink(vec.tensor_reduce(top[:, 0:1], key, AX.X, ALU.max))
                            rlink(vec.tensor_scalar(top[:, 0:1], top[:, 0:1], 0.5, None, ALU.max))
                            rlink(vec.tensor_scalar(onehot[:, :], key, top[:, 0:1], None, ALU.is_equal))
                            for c, table in enumerate((omt[:, :, 0, :], omt[:, :, 1, :], g3(mo), g3(cst_("group_of")))):
                                last = vec.scalar_tensor_tensor(out=g3(junk[:, :]), in0=g3(onehot[:, :]), scalar=1.0, in1=table,
                                                                op0=ALU.mult, op1=ALU.mult, accum_out=sel[:, c:c + 1])
                                rlink(last)
                            vec.scalar_tensor_tensor(out=key, in0=key, scalar=top[:, 0:1], in1=key,
                                                     op0=ALU.not_equal, op1=ALU.mult)
                            rlink(vec.tensor_tensor(pos, sel[:, 0:2], cst_("pixel_xy")[:, bass.ds(t * 2, 2)], ALU.add))
                            rlink(vec.tensor_scalar(pos, pos, -2.0, float(H), ALU.max, ALU.min))
                            rlink(vec.tensor_copy(fli[:, :], pos))
                            rlink(vec.tensor_copy(flr, fli[:, :]))
                            rlink(vec.tensor_tensor(up, flr, pos, ALU.is_gt))
                            rlink(vec.tensor_tensor(flr, flr, up, ALU.subtract))
                            rlink(vec.tensor_scalar(lin[:, 0:1], sel[:, 3:4], float(PADH * PADW), flr[:, 0:1], ALU.mult, ALU.add))
                            rlink(vec.scalar_tensor_tensor(out=lin[:, 1:2], in0=flr[:, 1:2], scalar=float(PADW), in1=lin[:, 0:1],
                                                           op0=ALU.mult, op1=ALU.add))
                            vec.tensor_scalar(idx4[:, :], cst_("corner"), lin[:, 1:2], None, ALU.add).then_inc(s_idx, 1)
                            rlink(vec.tensor_tensor(frac, pos, flr, ALU.subtract))
                            vec.tensor_copy(wxa[:, 1:2], frac[:, 0:1])
                            vec.tensor_scalar(wxa[:, 0:1], frac[:, 0:1], -1.0, 1.0, ALU.mult, ALU.add)
                            vec.tensor_scalar(wya[:, 1:2], frac[:, 1:2], sel[:, 2:3], None, ALU.mult)
                            rlink(vec.tensor_scalar(up[:, 0:1], frac[:, 1:2], -1.0, 1.0, ALU.mult, ALU.add))
                            rlink(vec.tensor_scalar(wya[:, 0:1], up[:, 0:1], sel[:, 2:3], None, ALU.mult))
                            for c in range(2):
                                last = vec.tensor_scalar(w4[:, 2 * c:2 * c + 2], wxa, wya[:, c:c + 1], None, ALU.mult)
                            vec.tensor_scalar(gsel, cst_("group_iota"), sel[:, 3:4], None, ALU.is_equal)
                            rlink(last)
                            ve.wait_ge(s_gd, it + 1)
                            vec.tensor_tensor(gat[:, :, :], gat[:, :, :], w4.rearrange("p (k o) -> p k o", o=1)
                                              .broadcast_to([P, CORNERS, CG]), ALU.mult).then_inc(s_gatu, 1)
                            ve.wait_ge(s_gatu, it + 1)
                            rlink(vec.tensor_reduce(val, gat[:, :, :].rearrange("p k c -> p c k"), AX.X, ALU.add))
                            rlink(vec.tensor_tensor(gmix[:, :, :], gsel.rearrange("p (g o) -> p g o", o=1).broadcast_to([P, G, CG]),
                                                    val.rearrange("p (o c) -> p o c", o=1).broadcast_to([P, G, CG]), ALU.mult))
                            o = big[:, bass.ds(t, 1), :].rearrange("p o c -> p (o c)")
                            rlink(vec.tensor_tensor(o, o, gmix[:, :, :].rearrange("p g c -> p (g c)"), ALU.add))
                            assert rk["k"] == RLINKS, rk
                    vec.memset(small[0:1, 62:63], 0.0).then_inc(s_mixed, 1)
                    for j in range(4):
                        if j % 2 == 0:
                            ve.wait_ge(s_oT, n * 2 + j // 2 + 1)
                        vec.tensor_copy(q[:, j // 2, j % 2 * HALF:(j % 2 + 1) * HALF], bank(4 + j)).then_inc(s_oTs, 1)
                    for m in range(K):
                        for h in range(2):
                            ve.wait_ge(s_fin, n * 4 + 2 * m + h + 1)
                            o = x[:, m, h * HALF:(h + 1) * HALF]
                            last = vec.scalar_tensor_tensor(out=o, in0=bank(2 * m + h), scalar=col("out_b", m),
                                                            in1=o, op0=ALU.add, op1=ALU.add)
                    link(last)
                vec.memset(small[0:1, 61:62], 0.0).then_inc(s_xdone, 1)
                assert chain["k"] == per, chain

        @block.scalar
        def _(ac):
            act = nc.scalar
            ac.wait_ge(s_load, 16 * N_LOAD)
            ac.wait_ge(s_vset, 12)
            with ac.Fori(0, batches) as n:
                for m in range(K):
                    for h in range(2):
                        ac.wait_ge(s_q, n * 4 + 2 * m + h + 1)
                        act.activation(q[:, m, h * HALF:(h + 1) * HALF], bank(2 * m + h), ACT.Identity,
                                       bias=col("q_bias", m)).then_inc(s_qs, 1)
                for j in (1, 3):
                    ac.wait_ge(s_qt, n * 4 + j + 1)
                    act.activation(qT[:, 2 * j:2 * j + 2, :].rearrange("p t c -> p (t c)"), bank(j), ACT.Copy)\
                        .then_inc(s_qta, 1)
                ac.wait_ge(s_mx, n + 1)
                for m in range(K):
                    act.activation(e[:, m, :], bank(4, C, m * C), ACT.Exp, bias=small[:, 32 + m:33 + m],
                                   accum_out=small[:, 34 + m:35 + m]).then_inc(s_e, 1)
                if layers > 1:
                    ac.wait_ge(s_xvz, n + 1)
                    for m in range(K):
                        for h in range(2):
                            ac.wait_ge(s_xv, n * 4 + 2 * m + h + 1)
                            act.activation(rows_of(xvp, m, h), bank(2 + 2 * m + h).rearrange("p (h w) -> p h w", w=W),
                                           ACT.Copy).then_inc(s_xvs, 1)
                    ac.wait_ge(s_tsc, n + 1)
                    act.activation(tr, ps[:, 0:2, :].rearrange("p b n -> p (b n)"), ACT.Relu, bias=small[:, 41:42],
                                   scale=small[:, 40:41]).then_inc(s_tr, 1)
                if layers > 2:
                    for k in range(K):
                        ac.wait_ge(s_dw, n * 2 + k + 1)
                        act.activation(q[:, k, :], acc[:, k, :], ACT.Relu, bias=col("dw2_b", k), scale=col("bn1_g", k))\
                            .then_inc(s_h, 1)
                    for m in range(K):
                        for h in range(2):
                            ac.wait_ge(s_pw, n * 4 + 2 * m + h + 1)
                            act.activation(acc[:, m, h * HALF:(h + 1) * HALF], bank(2 * m + h), ACT.Relu,
                                           bias=col("pw_b", m), scale=col("bn2_g", m)).then_inc(s_h2, 1)
                if layers > 3:
                    ac.wait_ge(s_norm, n * layers + 4)
                    for k in range(K):
                        act.activation(acc[:, k, :].rearrange("p (h w) -> p h w", h=H), xp[:, k, 1:1 + H, 1:1 + W], ACT.Copy)\
                            .then_inc(s_flat, 1)
                    ac.wait_ge(s_xpr, n * 4 + 4)
                    for k in range(K):
                        ac.wait_ge(s_cent, n * 2 + k + 1)
                        act.activation(acc[:, k, :], q[:, k, :], ACT.Square).then_inc(s_sq, 1)
                    for h in range(2):
                        ac.wait_ge(s_lvar, n * 2 + h + 1)
                        act.activation(tr[:, h * HALF:(h + 1) * HALF], bank(4 + h), ACT.Sqrt, bias=cst_("eps"))\
                            .then_inc(s_sd, 1)
                    for k in range(K):
                        ac.wait_ge(s_xhat, n * 2 + k + 1)
                        act.activation(q[:, k, :], q[:, k, :], ACT.Gelu, bias=col("ln_b", k), scale=col("ln_g", k))\
                            .then_inc(s_gelu, 1)
                    ac.wait_ge(s_msub, n + 1)
                    mask = om[:, :, :].rearrange("p t (g c m) -> p (t g) c m", g=G, c=3)[:, :, 2, :]
                    act.activation(mask, mask, ACT.Exp).then_inc(s_mexp, 1)
                    ac.wait_ge(s_tb, n * 16 + 16)
                    tv = tb[:, :, :].rearrange("p n (c m) -> p c m n", c=3)
                    tx, ty = tv[:, 0], tv[:, 1]
                    ac.wait_ge(s_om, n * TILES + TILES)
                    for d in range(D):
                        act.activation(hatx[:, d], tx, ACT.Abs, bias=cst_("minus_d")[:, d:d + 1]).then_inc(s_a, 1)
                    for d in range(D):
                        ac.wait_ge(s_a, n * 2 * D + d + 1)
                        act.activation(hatx[:, d], hatx[:, d], ACT.Relu, bias=1.0, scale=-1.0).then_inc(s_hx, 1)
                    for dy in range(D):
                        if dy >= 2:
                            ac.wait_ge(s_wyd, n * D + dy - 1)
                        act.activation(haty[:, dy % 2], ty, ACT.Abs, bias=cst_("minus_d")[:, dy:dy + 1]).then_inc(s_a, 1)
                        ac.wait_ge(s_a, n * 2 * D + D + dy + 1)
                        act.activation(haty[:, dy % 2], haty[:, dy % 2], ACT.Relu, bias=1.0, scale=-1.0).then_inc(s_hy, 1)

        @block.gpsimd
        def _(po):
            pool = nc.gpsimd
            po.wait_ge(s_vset, 2)
            po.wait_ge(s_load, 16 * N_LOAD)
            for bn in ("bn1", "bn2"):
                pool.tensor_tensor(col(bn + "_v", 0, K), col(bn + "_v", 0, K), cst_("half")[:, 0:K], ALU.pow)\
                    .then_inc(s_gset, 1)
            with po.Fori(0, batches) as n:
                nst = {1: 1, 2: 3, 3: 4, 4: 5}[layers]

                def rstd(stat, c):
                    po.wait_ge(s_var, stat)
                    pool.tensor_tensor(small[:, 28:28 + c], small[:, 24:24 + c], cst_("half")[:, 0:c], ALU.pow)\
                        .then_inc(s_rstd, 1)

                wait_apart(po, s_zeroed_dram, 16)
                if layers > 3:
                    wait_apart(po, s_samp, n)
                else:
                    wait_apart(po, s_xdone, n)
                pool.memset(xp[:, :, :, :], 0.0).then_inc(s_xpz, 1)
                rstd(n * nst + 1, K)
                if layers > 1:
                    if layers > 3:
                        wait_apart(po, s_prod, n * (D * D))
                    pool.memset(xvp[:, :, :, :], 0.0).then_inc(s_xvz, 1)
                    rstd(n * nst + 2, K)
                    rstd(n * nst + 3, 1)
                if layers > 2:
                    rstd(n * nst + 4, K)
                if layers > 3:
                    rstd(n * nst + 5, K)
                    wait_apart(po, s_cnt, n + 1)
                    pool.partition_all_reduce(runs[:, TILES:2 * TILES], runs[:, 0:TILES], P,
                                              bass.bass_isa.ReduceOp.max).then_inc(s_cntr, 1)
                    mk = tb[:, :, :].rearrange("p n (c m) -> p c m n", c=3)[:, 2]
                    wait_apart(po, s_imgw, (n + 1) * 16 * TILES * TR)
                    pool.memset(samp, 0.0).then_inc(s_gz, 1)
                    wait_apart(po, s_hx, n * D + D)
                    with po.Fori(0, D) as dy:
                        po.wait_ge(s_hy, n * D + dy + 1)
                        po.wait_ge(s_prod, (n * D + dy) * D)
                        hy = haty[:, bass.ds(dy % 2, 1)].rearrange("p o m n -> p (o m) n")
                        pool.tensor_tensor(wy[:, :, :], hy, mk, ALU.mult).then_inc(s_wyd, 1)
                        po.wait_ge(s_wyd, n * D + dy + 1)
                        for d in range(D):
                            u = n * (D * D) + dy * D + d
                            if d >= 3:
                                po.wait_ge(s_wd, u - 2)
                            else:
                                po.wait_ge(s_wd, n * (D * D) + dy * D)
                            pool.tensor_tensor(prod[:, d % 3], wy[:, :, :], hatx[:, d], ALU.mult).then_inc(s_prod, 1)
                    wait_apart(po, s_runs, n + 1)
                    with po.Fori(0, TILES) as t:
                        first = po.value_load(runs_i[0:1, bass.ds(t, 1)], min_val=0, max_val=1 << 20)
                        end = po.value_load(runs_i[0:1, bass.ds(t + 1, 1)], min_val=0, max_val=1 << 20)
                        with po.Fori(first, end) as it:
                            wait_apart(po, s_idx, it + 1)
                            for c in range(CORNERS):
                                pool.indirect_dma_start(
                                    out=gat[:, c, :], out_offset=None, in_=img_dram,
                                    in_offset=bass.IndirectOffsetOnAxis(ap=idx4[:, c:c + 1], axis=0)).then_inc(s_gat, 16)
                            po.wait_ge(s_gat, 16 * CORNERS)
                            pool.memset(pdone[:, :], 0.0).then_inc(s_gd, 1)
                            po.inc_swdge_sem([s_gat], [16 * CORNERS], mode="sub")
                            po.wait_ge(s_gd, it + 1)


VLINKS = {1: 8, 2: 39, 3: 66, 4: 109}
RLINKS = 22


def consts():
    out = np.zeros((P, NCST), np.float32)

    def put(name, value):
        a, n = CST[name]
        out[:, a:a + n] = value

    put("ident", np.eye(P))
    put("group8", np.kron(np.eye(P // 8), np.full((8, 8), 1 / 8)))
    put("mean256", 1 / C)
    put("code", G * TAPS - np.arange(G * TAPS))
    put("group_of", np.arange(G * TAPS) // TAPS)
    put("group_iota", np.arange(G))
    pix = np.arange(P)
    put("pixel_xy", np.stack([v for t in range(TILES) for v in (pix % W, t * TR + pix // W)], 1))
    put("corner", R * PADW + R + np.array([0, 1, PADW, PADW + 1]))
    put("minus_d", R - np.arange(D))
    grid = np.zeros((G, 3, TAPS))
    grid[:, 0], grid[:, 1] = np.arange(TAPS) // 3 - 1, np.arange(TAPS) % 3 - 1
    put("grid", grid.reshape(-1))
    put("half", -0.5)
    put("eps", LN_EPS)
    return out


PERMS = ((0, 1, 2, 3, 4, 5, 6, 7), (3, 0, 1, 2, 5, 6, 7, 4), (2, 3, 0, 1, 6, 7, 4, 5), (1, 2, 3, 0, 7, 4, 5, 6),
         (4, 5, 6, 7, 0, 1, 2, 3), (5, 6, 7, 4, 3, 0, 1, 2), (6, 7, 4, 5, 2, 3, 0, 1), (7, 4, 5, 6, 1, 2, 3, 0))


def tap_perms():
    a = np.arange(TAPS).reshape(3, 3)
    turned = [a, np.rot90(a, 1), np.rot90(a, 2), np.rot90(a, 3),
              np.rot90(a.T, 3), np.rot90(a.T, 2), np.rot90(a.T, 1), a.T]
    return np.stack([t.reshape(-1) for t in turned])


def lay_out(inp):
    a = {k: np.asarray(v) for k, v in inp.items()}

    def chunks(w):
        return w.reshape(K, P, -1)

    def d4(w):
        perms = np.array(PERMS)
        full = w[:, :, perms]
        return full.transpose(1, 3, 0, 2).reshape(w.shape[1] * 8, w.shape[0] * 8)

    off = a["L3_conv_off_w"].reshape(C, G, TAPS, 2)
    offb = a["L3_conv_off_b"].reshape(G, TAPS, 2)
    om_w = np.stack([off[..., 0], off[..., 1], a["L3_conv_mask_w"].reshape(C, G, TAPS)], 2).reshape(C, OM)
    om_b = np.stack([offb[..., 0], offb[..., 1], a["L3_conv_mask_b"].reshape(G, TAPS)], 1).reshape(OM)
    parts = {"w0": a["L0_conv_w"].T, "wv": d4(a["L1_conv_w_v"]), "w1": d4(a["L1_conv_w1"]),
             "pw": a["L2_conv_pw_w"].reshape(C, C).T, "in_w": a["L3_conv_in_w"], "om_w": om_w, "out_w": a["L3_conv_out_w"]}
    weights = np.concatenate([chunks(parts[name]) for name in WTS], 2)

    perm = tap_perms()
    w2 = a["L1_conv_w2"].reshape(K, TAPS, P // 8)
    w2x = np.zeros((P // 8, 8, K, TAPS, P // 8, 8), np.float32)
    for g in range(8):
        for c in range(P // 8):
            w2x[:, g, :, :, c, g] = w2[:, perm[g], :].transpose(2, 0, 1)
    b2 = a["L1_conv_b2"].reshape(K, TAPS)[:, perm]
    b2 = np.tile(b2.transpose(1, 0, 2).reshape(8, K * TAPS), (P // 8, 1))

    def two(v):
        return v.reshape(K, P).T

    def taps(w):
        return w.reshape(K, P, TAPS).transpose(1, 0, 2).reshape(P, K * TAPS)

    c = {"q_bias": two(a["L0_conv_bias"]), "dw2_b": two(a["L2_conv_dw_b"]), "pw_b": two(a["L2_conv_pw_b"]),
         "dw3_b": two(a["L3_conv_dw_b"]), "ln_g": two(a["L3_conv_ln_g"]), "ln_b": two(a["L3_conv_ln_b"]),
         "out_b": two(a["L3_conv_out_b"]), "t_gamma": a["L1_conv_gn_gamma"].reshape(P, 1),
         "t_beta": a["L1_conv_gn_beta"].reshape(P, 1), "dw2": taps(a["L2_conv_dw_w"]), "dw3": taps(a["L3_conv_dw_w"]),
         "b2": b2}
    for bn in ("bn1", "bn2"):
        for v in "gbmv":
            c[f"{bn}_{v}"] = two(a[f"L2_conv_{bn}_{v}"])
    cols = np.concatenate([c[name] for name in COLS], 1)
    rows = np.tile(np.concatenate([a["L3_conv_in_b"], om_b])[None], (P, 1))
    arrays = {"x_in": a["x"].reshape(B, C, N), "weights_in": weights, "w2x_in": w2x.reshape(P, K * TAPS * P),
              "cols_in": cols, "rows_in": rows, "consts_in": consts()}
    return {k: np.ascontiguousarray(v) for k, v in arrays.items()}


def kernel(**inputs):
    import concourse.bacc as bacc
    from concourse.bass_utils import run_bass_kernel_spmd as run

    arrays = lay_out(inputs)
    nc = bacc.Bacc("TRN2", target_bir_lowering=False, num_devices=1)
    args = {k: nc.dram_tensor(k, v.shape, F32, kind="ExternalInput").ap() for k, v in arrays.items()}
    out = nc.dram_tensor("out", (B, C, N), F32, kind="ExternalOutput").ap()
    build(nc, out=out, **args)
    r = run(nc, [arrays], core_ids=[0])
    return r.results[0]["out"].reshape(B, C, H, W)
```

```python
from contextlib import ExitStack

import concourse.bass as bass
import numpy as np
from concourse import mybir

F32 = mybir.dt.float32
I32 = mybir.dt.int32
ALU = mybir.AluOpType
ACT = mybir.ActivationFunctionType
AX = mybir.AxisListType

P = 128
B, C, H, W = 16, 256, 32, 32
K = C // P
N = H * W
HALF = N // 2
HR = H // 2
TILES = N // P
TR = P // W
GN_EPS, LN_EPS, BN_EPS = 1e-5, 1e-5, 1e-5
DW_THRESH, PW_THRESH = 4.0, 0.001
TAPS = 9
G = 16
CG = C // G
OM = G * 3 * TAPS
R = 4
D = 2 * R + 1
PADW = W + 2 * R
PADH = H + 2 * R
ROWF = PADW * CG
IMGR = TR + 2 * R
PIX = P
CORNERS = 4
TAPS2 = D * D
LEAD = 3
END = 1 << 30

SLOT = {"gn0": -LEAD, "finish": 1}
for _name, _after, _taps in (("L0", "finish", 5), ("L1", "L0", 16), ("dyn", "L1", 9), ("L2", "dyn", 11),
                             ("pw", "L2", 10), ("L3", "pw", 4), ("ln", "L3", 11), ("om", "ln", 5)):
    SLOT[_name] = SLOT[_after] + _taps
SLOT["sparse"] = TAPS2 + 1

COLS = {}
_at = 0
for _name, _n in (("q_bias", K), ("dw2_b", K), ("bn1_g", K), ("bn1_b", K), ("bn1_m", K), ("bn1_v", K),
                  ("pw_b", K), ("bn2_g", K), ("bn2_b", K), ("bn2_m", K), ("bn2_v", K), ("dw3_b", K),
                  ("ln_g", K), ("ln_b", K), ("out_b", K), ("t_gamma", 1), ("t_beta", 1),
                  ("dw2", K * TAPS), ("dw3", K * TAPS), ("b2", K * TAPS)):
    COLS[_name] = (_at, _n)
    _at += _n
NCOLS = _at
WTS = {}
_at = 0
for _name, _n in (("w0", C), ("wv", C), ("w1", P), ("pw", C), ("in_w", C), ("om_w", OM), ("out_w", C)):
    WTS[_name] = (_at, _n)
    _at += _n
NWTS = _at
CST = {}
_at = 0
for _name, _n in (("ident", P), ("group8", P), ("mean256", P), ("code", TILES * G), ("tap_code", TAPS),
                  ("group_of", TILES * G), ("row_of", TILES * G), ("pixel_xy", 2), ("corner", CORNERS), ("minus_d", D),
                  ("grid", OM), ("half", 2), ("eps", 1)):
    CST[_name] = (_at, _n)
    _at += _n
NCST = _at


def build(nc, x_in, weights_in, w2x_in, cols_in, rows_in, consts_in, out, batches=B):
    ctx = ExitStack()
    with ctx:
        def sb(name, shape, dt=F32):
            return ctx.enter_context(nc.sbuf_tensor(name, shape, dt))

        def sem(name):
            return ctx.enter_context(nc.semaphore(name))

        def dram(name, shape):
            return nc.dram_tensor(name, shape, F32, kind="Internal").ap()

        img_dram = dram("img_dram", [G * PADH * PADW, CG])
        om_dram = dram("om_dram", [G, TILES, PIX, 3 * TAPS])
        samp_dram = dram("samp_dram", [G, TILES, PIX, CG])
        spb_dram = dram("spb_dram", [2, P, TILES * C])
        xmid_dram = dram("xmid_dram", [2, P, K * N])

        wts = sb("wts", [P, K, NWTS])
        w2x = sb("w2x", [P, K, TAPS, P])
        cols = sb("cols", [P, NCOLS])
        rows = sb("rows", [P, C + OM])
        cst = sb("cst", [P, NCST])
        x = sb("x", [P, K, N])
        xp = sb("xp", [P, K, H + 2, W + 2])
        qx = sb("qx", [P, K * (H + 2) * (W + 2)])
        work = sb("work", [P, 4 * N])
        big = sb("big", [P, TILES, C])
        keys = sb("keys", [P, TILES * G * TAPS])
        mout = sb("mout", [P, TILES * G * TAPS])
        img = sb("img", [P, IMGR * ROWF])
        tb = sb("tb", [P, PIX, 3 * TAPS])
        hatx = sb("hatx", [P, 3, TAPS, PIX])
        haty = sb("haty", [P, 2, TAPS, PIX])
        wy = sb("wy", [P, TAPS, PIX])
        prod = sb("prod", [P, 3, TAPS, PIX])
        tapped = sb("tapped", [P, 2, PIX * CG])
        samp = sb("samp", [P, PIX * CG])
        pacc = sb("pacc", [P, PIX * CG // 2])
        stats = sb("stats", [P, K, 2, 6])
        small = sb("small", [P, 64])
        rs = sb("rs", [P, 96])
        tg = sb("tg", [P, 2, TILES * G])
        idx4 = sb("idx4", [P, CORNERS], I32)
        fli = sb("fli", [P, 2], I32)
        gat = sb("gat", [P, CORNERS, CG])
        tick = sb("tick", [1, 64])
        pdone = sb("pdone", [1, 1])
        runs = sb("runs", [P, 4])
        runs_i = sb("runs_i", [1, 2], I32)

        q = qx[:, 0:K * N].rearrange("p (k n) -> p k n", k=K)
        xvp = qx[:, :].rearrange("p (k h w) -> p k h w", k=K, h=H + 2)
        flag = qx[:, 0:TILES * G * TAPS]
        onehot = qx[:, TILES * G * TAPS:2 * TILES * G * TAPS]
        acc = work[:, 0:K * N].rearrange("p (k n) -> p k n", k=K)
        tr = work[:, K * N:K * N + N]
        e = tr[:, 0:K * C].rearrange("p (k n) -> p k n", k=K)
        et = tr[:, K * C:2 * K * C].rearrange("p (k n) -> p k n", k=K)
        pwm = tr[:, 0:K * C].rearrange("p (k n) -> p k n", k=K)
        tmp = work[:, 3 * N:4 * N].rearrange("p (b n) -> p b n", b=2)
        om = work[:, 0:TILES * OM].rearrange("p (t m) -> p t m", t=TILES)
        spb = acc
        res = work[:, 2 * N:4 * N].rearrange("p (k n) -> p k n", k=K)
        qT = big
        xflat = x[:, :, :].rearrange("p k n -> p (k n)")
        junk = xflat[:, 0:TILES * G * TAPS]
        bigf = big[:, :, :].rearrange("p t c -> p (t c)")
        UP = PIX * CG // 2

        def cst_(name):
            a, n = CST[name]
            return cst[:, a:a + n]

        def col(name, i=0, n=1):
            return cols[:, COLS[name][0] + i:COLS[name][0] + i + n]

        def wt(name, k, a=0, n=None):
            s, m = WTS[name]
            return wts[:, k, s + a:s + a + (m if n is None else n)]

        ident = cst_("ident")
        ps = ctx.enter_context(nc.psum_tensor("ps", [P, 8, 512], F32))

        s_load = sem("s_weights_loaded")
        s_x = sem("s_x_loaded")
        s_zero = sem("s_border_zeroed")
        s_zeroed_dram = sem("s_dram_border_zeroed")
        s_vset = sem("s_vector_setup")
        s_gset = sem("s_pool_setup")
        s_v = sem("s_vector_chain")
        s_a = sem("s_scalar_chain")
        s_gstat = sem("s_channel_stats")
        s_gsum = sem("s_group_stats")
        s_var = sem("s_group_variance")
        s_rstd = sem("s_group_rstd")
        s_norm = sem("s_normed")
        s_q = sem("s_q_psum")
        s_qs = sem("s_q_sbuf")
        s_qt = sem("s_qT_psum")
        s_qtv = sem("s_qT_sbuf_by_vector")
        s_qta = sem("s_qT_sbuf_by_scalar")
        s_sc = sem("s_scores_psum")
        s_mx = sem("s_score_max")
        s_e = sem("s_exp_scores")
        s_et = sem("s_eT_psum")
        s_ets = sem("s_eT_sbuf")
        s_att = sem("s_attention_psum")
        s_x1 = sem("s_x_after_attention")
        s_t1 = sem("s_t_psum")
        s_tsc = sem("s_t_scale")
        s_tr = sem("s_t_relu")
        s_xv = sem("s_xv_psum")
        s_xvs = sem("s_xv_sbuf")
        s_xvz = sem("s_xv_border_zeroed")
        s_w = sem("s_kernel_psum")
        s_wu = sem("s_kernel_used")
        s_dw = sem("s_depthwise_done")
        s_h = sem("s_h_relu")
        s_pwm = sem("s_pruned_pointwise_weights")
        s_pw = sem("s_pointwise_psum")
        s_h2 = sem("s_h2_relu")
        s_xmid = sem("s_x_before_layer_3")
        s_xmidw = sem("s_x_before_layer_3_in_dram")
        s_flat = sem("s_normed_unbordered")
        s_xpr = sem("s_xproj_psum")
        s_xprs = sem("s_xproj_sbuf")
        s_imgw = sem("s_img_in_dram")
        s_dw3 = sem("s_depthwise3_done")
        s_mean = sem("s_ln_mean_psum")
        s_cent = sem("s_ln_centered")
        s_sq = sem("s_ln_squared")
        s_lvar = sem("s_ln_var_psum")
        s_sd = sem("s_ln_sd")
        s_xhat = sem("s_ln_normed")
        s_gelu = sem("s_gelu")
        s_om = sem("s_om_psum")
        s_oms = sem("s_om_sbuf")
        s_msub = sem("s_mask_minus_max")
        s_mexp = sem("s_mask_exp")
        s_omr = sem("s_om_final")
        s_omw = sem("s_om_in_dram")
        s_tb = sem("s_om_by_group_loaded")
        s_img = sem("s_img_by_group_loaded")
        s_cnt = sem("s_sparse_counts")
        s_cntr = sem("s_sparse_count_max")
        s_runs = sem("s_sparse_runs")
        s_rv = sem("s_sparse_chain")
        s_idx = sem("s_sparse_indices")
        s_gat = sem("s_sparse_gathered")
        s_gatu = sem("s_sparse_gathered_used")
        s_gd = sem("s_sparse_gather_done")
        s_spb = sem("s_sparse_sum_done")
        s_spbw = sem("s_sparse_sum_in_dram")
        s_hx = sem("s_hat_x")
        s_hy = sem("s_hat_y")
        s_wyd = sem("s_wy")
        s_prod = sem("s_hat_products")
        s_wd = sem("s_tap_weight_psum")
        s_tap = sem("s_tapped")
        s_psum = sem("s_tensor_sum")
        s_vacc = sem("s_vector_sum")
        s_pacc = sem("s_pool_sum")
        s_az = sem("s_sums_zeroed")
        s_samp = sem("s_sampled")
        s_sampw = sem("s_sampled_in_dram")
        s_back = sem("s_finish_loaded")
        s_mixed = sem("s_sparse_added")
        s_oT = sem("s_outT_psum")
        s_oTs = sem("s_outT_sbuf")
        s_fin = sem("s_out_psum")
        s_xdone = sem("s_x_final")
        s_stored = sem("s_x_stored")

        N_LOAD = 5
        N_BACK = TILES + 2
        block = ctx.enter_context(nc.Block())

        def bank(b, n=512, at=0):
            return ps[:, b, at:at + n]

        def rows_of(t3, k, half):
            return t3[:, k, 1 + half * HR:1 + (half + 1) * HR, 1:1 + W]

        def shifted(t3, k, i, j, r0=0, nr=H):
            return t3[:, k, r0 + i:r0 + i + nr, j:j + W]

        def wait(eng, semaphore, value):
            if not isinstance(value, int) or value > 0:
                eng.wait_ge(semaphore, value)

        cells = iter(range(64))

        def wait_apart(eng, semaphore, value):
            if isinstance(value, int):
                wait(eng, semaphore, value)
                return
            i = next(cells)
            cell = tick[:, i:i + 1]
            if eng is nc.tensor:
                value = eng.snap(value)
                eng.wait_ge(s_load, 16 * N_LOAD)
            eng.wait_ge(semaphore, value)
            if eng is nc.vector:
                eng.memset(cell, 0.0)
            elif eng is nc.gpsimd:
                eng.tensor_tensor(cell, cst_("half")[0:1, 0:1], cst_("half")[0:1, 0:1], ALU.add)

        def run(eng, side, window):
            def body(n, f, m):
                stream = side(f, m)
                until = next(stream, END)
                for u in range(-LEAD, TAPS2 + 2):
                    window(n, u)
                    while until <= u:
                        until = next(stream, END)
                assert until == END

            def alone(f, m):
                for _ in side(f, m):
                    pass

            alone(0, None)
            body(0, 1, None)
            if batches > 2:
                with eng.Fori(1, batches - 1) as n:
                    body(n, n + 1, n - 1)
            body(batches - 1, None, batches - 2)
            alone(None, batches - 1)

        @block.sync
        def _(sp):
            sp.dma_start(wts[:, :, :], weights_in.rearrange("k p n -> p k n")).then_inc(s_load, 16)
            sp.dma_start(w2x[:, :, :, :].rearrange("p k t n -> p (k t n)"), w2x_in).then_inc(s_load, 16)
            sp.dma_start(cols[:, :], cols_in).then_inc(s_load, 16)
            sp.dma_start(rows[:, :], rows_in).then_inc(s_load, 16)
            sp.dma_start(cst[:, :], consts_in).then_inc(s_load, 16)
            sp.wait_ge(s_zero, 1)
            sp.dma_start(img_dram.rearrange("(p n) c -> p (n c)", p=P), img[:, 0:G * PADH * PADW * CG // P])\
                .then_inc(s_zeroed_dram, 16)
            sp.wait_ge(s_zeroed_dram, 16)

            def load_x(f):
                wait(sp, s_xmidw, f * 16)
                wait(sp, s_spb, f)
                sp.dma_start(x[:, :, :], x_in[bass.ds(f, 1)].rearrange("o (k p) n -> p (o k) n", p=P))\
                    .then_inc(s_x, 16)

            def front(f):
                sp.wait_ge(s_xmid, f + 1)
                sp.dma_start(xmid_dram[bass.ds(f % 2, 1)].rearrange("o p n -> p (o n)"), xflat).then_inc(s_xmidw, 16)
                grouped = img_dram.rearrange("(g y x) c -> y x g c", g=G, y=PADH)
                wait(sp, s_img, f * 16 * G)
                for t in range(TILES):
                    sp.wait_ge(s_xprs, f * TILES + t + 1)
                    for r in range(TR):
                        y = R + t * TR + r
                        sp.dma_start(grouped[y, R:R + W], big[r * W:(r + 1) * W, t, :].rearrange(
                            "p (g c) -> p g c", g=G)).then_inc(s_imgw, 16)
                wait(sp, s_tb, f * 16)
                sp.wait_ge(s_omr, f + 1)
                for t in range(TILES):
                    sp.dma_start(om_dram[:, t].rearrange("g n m -> n g m"),
                                 om[:, t, :].rearrange("p (g m) -> p g m", g=G)).then_inc(s_omw, 16)

            def store_sparse(f):
                sp.wait_ge(s_spb, f + 1)
                sp.dma_start(spb_dram[bass.ds(f % 2, 1)].rearrange("o p n -> p (o n)"), bigf).then_inc(s_spbw, 16)

            def window_loads(n):
                sp.wait_ge(s_imgw, (n + 1) * 16 * TILES * TR)
                sp.wait_ge(s_omw, (n + 1) * 16 * TILES)
                wait(sp, s_samp, n * 2)
                sp.dma_start(tb[:, :, :].rearrange("p n m -> p (n m)"),
                             om_dram.rearrange("g t n m -> (g t) (n m)")).then_inc(s_tb, 16)
                gs = img_dram.rearrange("(g y x) c -> g (y x c)", g=G, y=PADH)
                for g in range(G):
                    src = bass.AP(gs.tensor, g * PADH * ROWF, [[TR * ROWF, TILES], [1, IMGR * ROWF]])
                    sp.dma_start(img[g * TILES:(g + 1) * TILES, :], src).then_inc(s_img, 16)

            def save_window(n):
                sp.wait_ge(s_samp, (n + 1) * 2)
                sp.dma_start(samp_dram.rearrange("g t n c -> (g t) (n c)"), samp[:, :]).then_inc(s_sampw, 16)

            def reload(m, last_front):
                sp.wait_ge(s_spbw, last_front * 16)
                sp.wait_ge(s_omw, last_front * 16 * TILES)
                sp.dma_start(work[:, 0:K * N], spb_dram[bass.ds(m % 2, 1)].rearrange("o p n -> p (o n)"))\
                    .then_inc(s_back, 16)
                sp.dma_start(work[:, 2 * N:4 * N], xmid_dram[bass.ds(m % 2, 1)].rearrange("o p n -> p (o n)"))\
                    .then_inc(s_back, 16)
                sp.wait_ge(s_sampw, (m + 1) * 16)
                for t in range(TILES):
                    sp.dma_start(big[:, t, :].rearrange("p (g c) -> p g c", g=G),
                                 samp_dram[:, t].rearrange("g n c -> n g c")).then_inc(s_back, 16)

            def store(m):
                sp.wait_ge(s_xdone, m + 1)
                sp.dma_start(out[bass.ds(m, 1)].rearrange("o (k p) n -> p (o k) n", p=P), res).then_inc(s_stored, 16)

            def body(n, f, m):
                if m is not None:
                    save_window(m)
                window_loads(n)
                if f is not None:
                    load_x(f)
                if m is not None:
                    reload(m, n + 1)
                    store(m)
                if f is not None:
                    front(f)
                    store_sparse(f)

            load_x(0)
            front(0)
            store_sparse(0)
            body(0, 1, None)
            if batches > 2:
                with sp.Fori(1, batches - 1) as n:
                    body(n, n + 1, n - 1)
            body(batches - 1, None, batches - 2)
            save_window(batches - 1)
            reload(batches - 1, batches)
            store(batches - 1)
            sp.wait_ge(s_stored, batches * 16)

        @block.tensor
        def _(pe):
            pe.wait_ge(s_load, 16 * N_LOAD)

            def group_stats(stat, c):
                pe.wait_ge(s_gstat, stat)
                pe.matmul(bank(7, c), cst_("group8"), small[:, 0:c], start=True, stop=True).then_inc(s_gsum, 1)

            def product(b, w, t, signal):
                for k in range(K):
                    mm = pe.matmul(bank(b), w(k), t(k), start=(k == 0), stop=(k == K - 1))
                mm.then_inc(signal, 1)

            def half_of(t3, h):
                return lambda k: t3[:, k, h * HALF:(h + 1) * HALF]

            def side(f, m):
                if f is not None:
                    yield SLOT["gn0"]
                    group_stats(f * 5 + 1, 4)
                if m is not None:
                    yield SLOT["finish"] + 1
                    if f is not None:
                        pe.wait_ge(s_norm, f * 4 + 1)
                    pe.wait_ge(s_mixed, m + 1)
                    for k in range(K):
                        for t in range(TILES):
                            mm = pe.transpose(bank(4 + 2 * k + t // 4, P, t % 4 * P), big[:, t, k * P:(k + 1) * P], ident)
                        mm.then_inc(s_oT, 1)
                    yield SLOT["finish"] + 3
                    pe.wait_ge(s_oTs, m * 4 + 4)
                    for j in range(4):
                        product(4 + j, lambda k: wt("out_w", k, j // 2 * P, P), half_of(q, j % 2), s_fin)
                        if j == 1:
                            yield SLOT["finish"] + 4
                if f is None:
                    return
                yield SLOT["L0"]
                pe.wait_ge(s_norm, f * 4 + 1)
                if m is not None:
                    pe.wait_ge(s_xdone, m + 1)
                for j in range(4):
                    product(4 + j, lambda k: wt("w0", k, j // 2 * P, P), lambda k: rows_of(xp, k, j % 2), s_q)
                    yield SLOT["L0"] + 1 + j
                pe.wait_ge(s_qs, f * 4 + 4)
                for j in range(4):
                    for t in (2 * j, 2 * j + 1):
                        for k in range(K):
                            mm = pe.transpose(bank(4 + j, P, (t % 2) * C + k * P), q[:, k, t * P:(t + 1) * P], ident)
                    mm.then_inc(s_qt, 1)
                yield SLOT["L0"] + 6
                pe.wait_ge(s_qtv, f * 2 + 2)
                pe.wait_ge(s_qta, f * 2 + 2)
                for k in range(K):
                    for t in range(TILES):
                        mm = pe.matmul(bank(4, C, k * C), qT[:, t, k * P:(k + 1) * P], qT[:, t, :],
                                       start=(t == 0), stop=(t == TILES - 1))
                        if t % 4 == 3 and (k, t) != (K - 1, TILES - 1):
                            yield SLOT["L0"] + 7 + 2 * k + t // 4
                mm.then_inc(s_sc, 1)
                yield SLOT["L0"] + 11
                pe.wait_ge(s_e, f * 2 + 2)
                for d in range(K):
                    for k in range(K):
                        mm = pe.transpose(bank(5, P, d * C + k * P), e[:, k, d * P:(d + 1) * P], ident)
                mm.then_inc(s_et, 1)
                yield SLOT["L0"] + 13
                pe.wait_ge(s_ets, f + 1)
                for j in range(4):
                    product(4 + j, lambda d: et[:, d, j // 2 * P:(j // 2 + 1) * P], half_of(q, j % 2), s_att)
                    yield SLOT["L0"] + 14 + j // 2

                yield SLOT["L1"] + 1
                group_stats(f * 5 + 2, 4)
                yield SLOT["L1"] + 4
                pe.wait_ge(s_norm, f * 4 + 2)
                for h in range(2):
                    product(4 + h, lambda k: wt("w1", k), lambda k: rows_of(xp, k, h), s_t1)
                for h in range(2):
                    yield SLOT["L1"] + 5
                    product(6 + h, lambda k: wt("wv", k, 0, P), lambda k: rows_of(xp, k, h), s_xv)
                yield SLOT["L1"] + 6
                pe.wait_ge(s_xvs, f * 4 + 2)
                group_stats(f * 5 + 3, 2)
                product(6, lambda k: wt("wv", k, P, P), lambda k: rows_of(xp, k, 0), s_xv)
                yield SLOT["L1"] + 8
                pe.wait_ge(s_tr, f + 1)
                product(4, lambda k: wt("wv", k, P, P), lambda k: rows_of(xp, k, 1), s_xv)
                yield SLOT["dyn"]
                pe.wait_ge(s_xvs, f * 4 + 4)
                for i in range(K * TAPS * 2):
                    half, tap, h = i // (2 * TAPS), i // 2 % TAPS, i % 2
                    if i >= 4:
                        pe.wait_ge(s_wu, f * 2 * K * TAPS + i - 3)
                    pe.matmul(bank(4 + i % 4), w2x[:, half, tap, :], tr[:, h * HALF:(h + 1) * HALF],
                              start=True, stop=True).then_inc(s_w, 1)
                    if i % 4 == 3:
                        yield SLOT["dyn"] + i // 4 + 1
                yield SLOT["L2"] + 1
                group_stats(f * 5 + 4, 4)
                yield SLOT["pw"]
                pe.wait_ge(s_h, f * 2 + 2)
                pe.wait_ge(s_pwm, f * 2 + 2)
                for j in range(4):
                    product(4 + j, lambda k: pwm[:, k, j // 2 * P:(j // 2 + 1) * P], half_of(q, j % 2), s_pw)
                    yield SLOT["pw"] + j // 2 + 1
                yield SLOT["L3"] + 1
                group_stats(f * 5 + 5, 4)
                yield SLOT["L3"] + 5
                pe.wait_ge(s_flat, f * 2 + 2)
                for t in range(TILES):
                    for k in range(K):
                        mm = pe.matmul(bank(4 + t // 2, C, t % 2 * C), acc[:, k, t * P:(t + 1) * P],
                                       wt("in_w", k), start=(k == 0), stop=(k == K - 1))
                    if t % 2:
                        mm.then_inc(s_xpr, 1)
                        yield SLOT["L3"] + 6 + t // 2
                yield SLOT["ln"]
                pe.wait_ge(s_xprs, f * TILES + TILES)
                pe.wait_ge(s_dw3, f * 2 + 2)
                for h in range(2):
                    product(4 + h, lambda k: cst_("mean256"), half_of(q, h), s_mean)
                yield SLOT["ln"] + 2
                pe.wait_ge(s_sq, f * 2 + 2)
                for h in range(2):
                    product(4 + h, lambda k: cst_("mean256"), half_of(acc, h), s_lvar)
                yield SLOT["om"]
                pe.wait_ge(s_gelu, f * 2 + 2)
                for t in range(TILES):
                    if t >= 4:
                        pe.wait_ge(s_oms, f * TILES + t - 3)
                    for k in range(K):
                        mm = pe.matmul(bank(4 + t % 4, OM), q[:, k, t * P:(t + 1) * P], wt("om_w", k),
                                       start=(k == 0), stop=(k == K - 1))
                    mm.then_inc(s_om, 1)
                    yield SLOT["om"] + (t + 1) // 2

            def window(n, u):
                v, w = u + 1, u - 1
                if 0 <= v < TAPS2:
                    at = n * TAPS2 + v
                    if v == 0:
                        wait_apart(pe, s_tap, n * TAPS2)
                    elif v >= 2:
                        pe.wait_ge(s_tap, at - 1)
                    pe.wait_ge(s_prod, at + 1)
                    for p in range(TAPS):
                        mm = pe.matmul(bank(v % 2, PIX), ident, prod[:, v % 3, p, :],
                                       start=(p == 0), stop=(p == TAPS - 1))
                    mm.then_inc(s_wd, 1)
                if 0 <= w < TAPS2:
                    if w == 0:
                        wait_apart(pe, s_samp, n * 2)
                    pe.wait_ge(s_tap, n * TAPS2 + w + 1)
                    for b in range(2):
                        mm = pe.matmul(bank(2 + b), ident, tapped[:, w % 2, b * 512:(b + 1) * 512],
                                       start=(w == 0), stop=(w == TAPS2 - 1), skip_group_check=True)
                    mm.then_inc(s_psum, 1)

            run(pe, side, window)

        @block.vector
        def _(ve):
            vec = nc.vector
            vec.memset(img[:, :], 0.0).then_inc(s_zero, 1)
            vec.memset(xp[:, :, :, :], 0.0).then_inc(s_zero, 1)
            ve.wait_ge(s_load, 16 * N_LOAD)
            for i, bn in enumerate(("bn1", "bn2")):
                vec.tensor_scalar(col(bn + "_v", 0, K), col(bn + "_v", 0, K), BN_EPS, None, ALU.add)\
                    .then_inc(s_vset, 1)
            vec.tensor_tensor(rows[:, C:C + OM], rows[:, C:C + OM], cst_("grid"), ALU.add).then_inc(s_vset, 1)
            vec.memset(runs[:, :], 0.0).then_inc(s_vset, 1)
            ve.wait_ge(s_gset, 2)
            for i, (bn, bias) in enumerate((("bn1", "dw2_b"), ("bn2", "pw_b"))):
                at = 4 + 4 * i
                vec.tensor_tensor(col(bn + "_g", 0, K), col(bn + "_g", 0, K), col(bn + "_v", 0, K), ALU.mult)\
                    .then_inc(s_vset, 1)
                vec.tensor_tensor(col(bias, 0, K), col(bias, 0, K), col(bn + "_m", 0, K), ALU.subtract)\
                    .then_inc(s_vset, 1)
                ve.wait_ge(s_vset, at + 2)
                vec.tensor_tensor(col(bias, 0, K), col(bias, 0, K), col(bn + "_g", 0, K), ALU.mult)\
                    .then_inc(s_vset, 1)
                ve.wait_ge(s_vset, at + 3)
                vec.tensor_tensor(col(bias, 0, K), col(bias, 0, K), col(bn + "_b", 0, K), ALU.add)\
                    .then_inc(s_vset, 1)
            ve.wait_ge(s_vset, 12)
            ve.wait_ge(s_zero, 2)

            def side(f, m):
                chain = {"k": 0}

                def link(ins, alone=False):
                    chain["k"] += 1
                    ins.then_inc(s_v, 1)
                    if alone:
                        wait_apart(ve, s_v, f * VLINKS + chain["k"])
                    else:
                        ve.wait_ge(s_v, f * VLINKS + chain["k"])

                def moments(src, c, stat, start):
                    for k in range(c):
                        for h in range(2):
                            last = vec.bn_stats(stats[:, k, h, :], src(k, h))
                    link(last, alone=True)
                    for k in range(c):
                        last = vec.bn_aggr(small[:, 2 * k:2 * k + 2], stats[:, k, :, :].rearrange("p a b -> p (a b)"))
                    link(last)
                    mean, var = small[:, 0:2 * c:2], small[:, 1:2 * c:2]
                    link(vec.tensor_tensor(small[:, 8:8 + c], mean, mean, ALU.mult))
                    vec.tensor_tensor(var, var, small[:, 8:8 + c], ALU.add).then_inc(s_gstat, 1)
                    yield start + 2
                    ve.wait_ge(s_gsum, stat)
                    link(vec.tensor_copy(small[:, 12:12 + 2 * c], bank(7, 2 * c)))
                    mean, msq = small[:, 12:12 + 2 * c:2], small[:, 13:12 + 2 * c:2]
                    link(vec.tensor_tensor(small[:, 20:20 + c], mean, mean, ALU.mult))
                    link(vec.tensor_tensor(small[:, 24:24 + c], msq, small[:, 20:20 + c], ALU.subtract))
                    vec.tensor_scalar(small[:, 24:24 + c], small[:, 24:24 + c], GN_EPS, None, ALU.add)\
                        .then_inc(s_var, 1)
                    yield start + 3
                    ve.wait_ge(s_rstd, stat)

                mean2 = small[:, 12:16:2]

                def group_norm(stat, start):
                    yield from moments(lambda k, h: x[:, k, h * HALF:(h + 1) * HALF], K, stat, start)
                    for k in range(K):
                        last = vec.tensor_scalar(xp[:, k, 1:1 + H, 1:1 + W], x[:, k, :].rearrange("p (h w) -> p h w", h=H),
                                                 mean2[:, k:k + 1], small[:, 28 + k:29 + k], ALU.subtract, ALU.mult)
                    last.then_inc(s_norm, 1)

                def depthwise(dst, w, bias, start):
                    for tap in range(TAPS):
                        for k in range(K):
                            o = dst[:, k, :].rearrange("p (h w) -> p h w", h=H)
                            wcol = col(w, k * TAPS + tap)
                            src = shifted(xp, k, tap // 3, tap % 3)
                            if tap > 0:
                                last = vec.scalar_tensor_tensor(out=o, in0=src, scalar=wcol, in1=o,
                                                                op0=ALU.mult, op1=ALU.add)
                            elif bias is None:
                                last = vec.tensor_scalar(o, src, wcol, None, ALU.mult)
                            else:
                                last = vec.tensor_scalar(o, src, wcol, col(bias, k), ALU.mult, ALU.add)
                            if tap == TAPS - 1:
                                last.then_inc(s_dw if w == "dw2" else s_dw3, 1)
                            else:
                                link(last)
                        if tap % 2:
                            yield start + tap // 2 + 1

                if f is not None:
                    yield SLOT["gn0"]
                    ve.wait_ge(s_x, f * 16 + 16)
                    yield from group_norm(f * 5 + 1, SLOT["gn0"] - 3)
                if m is not None:
                    yield SLOT["finish"]
                    ve.wait_ge(s_back, (m + 1) * 16 * N_BACK)
                    vec.tensor_tensor(bigf, bigf, work[:, 0:K * N], ALU.add).then_inc(s_mixed, 1)
                    for j in range(4):
                        yield SLOT["finish"] + 4 + j // 2
                        ve.wait_ge(s_fin, m * 4 + j + 1)
                        o = res[:, j // 2, j % 2 * HALF:(j % 2 + 1) * HALF]
                        last = vec.scalar_tensor_tensor(out=o, in0=bank(4 + j), scalar=col("out_b", j // 2),
                                                        in1=o, op0=ALU.add, op1=ALU.add)
                    last.then_inc(s_xdone, 1)
                if f is None:
                    return
                yield SLOT["L0"] + 5
                for j in (0, 2):
                    ve.wait_ge(s_qt, f * 4 + j + 1)
                    vec.tensor_copy(qT[:, 2 * j:2 * j + 2, :].rearrange("p t c -> p (t c)"), bank(4 + j)).then_inc(s_qtv, 1)
                yield SLOT["L0"] + 10
                ve.wait_ge(s_sc, f + 1)
                vec.tensor_reduce(small[:, 32:34], bank(4).rearrange("p (m d) -> p m d", m=K), AX.X, ALU.max,
                                  negate=True).then_inc(s_mx, 1)
                yield SLOT["L0"] + 12
                ve.wait_ge(s_et, f + 1)
                vec.tensor_copy(et[:, :, :].rearrange("p k n -> p (k n)"), bank(5)).then_inc(s_ets, 1)
                link(vec.reciprocal(small[:, 36:38], small[:, 34:36]))
                for j in range(4):
                    yield SLOT["L0"] + 14 + j // 2
                    ve.wait_ge(s_att, f * 4 + j + 1)
                    o = x[:, j // 2, j % 2 * HALF:(j % 2 + 1) * HALF]
                    last = vec.scalar_tensor_tensor(out=o, in0=bank(4 + j), scalar=small[:, 36 + j // 2:37 + j // 2],
                                                    in1=o, op0=ALU.mult, op1=ALU.add)
                last.then_inc(s_x1, 1)
                ve.wait_ge(s_x1, f + 1)
                yield SLOT["L1"]
                yield from group_norm(f * 5 + 2, SLOT["L1"])
                yield SLOT["L1"] + 5
                ve.wait_ge(s_t1, f * 2 + 2)
                yield from moments(lambda k, h: bank(4 + h), 1, f * 5 + 3, SLOT["L1"] + 5)
                link(vec.tensor_tensor(small[:, 40:41], col("t_gamma"), small[:, 28:29], ALU.mult))
                link(vec.tensor_tensor(small[:, 42:43], small[:, 12:13], small[:, 40:41], ALU.mult))
                vec.tensor_tensor(small[:, 41:42], col("t_beta"), small[:, 42:43], ALU.subtract).then_inc(s_tsc, 1)
                yield SLOT["dyn"]
                ve.wait_ge(s_xvz, f + 1)
                ve.wait_ge(s_xvs, f * 4 + 4)
                for i in range(K * TAPS * 2):
                    half, tap, h = i // (2 * TAPS), i // 2 % TAPS, i % 2
                    if i % 4 == 0:
                        yield SLOT["dyn"] + i // 4 + 1
                    if i >= 2:
                        ve.wait_ge(s_v, f * VLINKS + chain["k"])
                    ve.wait_ge(s_w, f * 2 * K * TAPS + i + 1)
                    o = acc[:, half, h * HALF:(h + 1) * HALF]
                    t = o if tap == 0 else tmp[:, h, :]
                    vec.scalar_tensor_tensor(
                        out=t.rearrange("p (h w) -> p h w", w=W), in0=bank(4 + i % 4).rearrange("p (h w) -> p h w", w=W),
                        scalar=col("b2", half * TAPS + tap), in1=shifted(xvp, half, tap // 3, tap % 3, h * HR, HR),
                        op0=ALU.add, op1=ALU.mult).then_inc(s_wu, 1)
                    if h == 1 and tap > 0:
                        ve.wait_ge(s_wu, f * 2 * K * TAPS + i + 1)
                        o = acc[:, half, :]
                        chain["k"] += 1
                        vec.tensor_tensor(o, o, work[:, 3 * N:4 * N], ALU.add).then_inc(s_v, 1)
                yield SLOT["dyn"] + 10
                ve.wait_ge(s_v, f * VLINKS + chain["k"])
                link(vec.tensor_tensor(xflat, xflat, work[:, 0:K * N], ALU.add))
                yield SLOT["L2"]
                yield from group_norm(f * 5 + 4, SLOT["L2"])
                yield SLOT["L2"] + 4
                ve.wait_ge(s_norm, f * 4 + 3)
                yield from depthwise(acc, "dw2", None, SLOT["L2"] + 4)
                yield SLOT["pw"] - 1
                ve.wait_ge(s_h, f * 2 + 2)
                for k in range(K):
                    last = vec.tensor_reduce(small[:, 44 + k:45 + k], q[:, k, :], AX.X, ALU.max)
                link(last)
                link(vec.tensor_scalar(small[:, 46:48], small[:, 44:46], DW_THRESH, None, ALU.is_ge))
                for k in range(K):
                    vec.tensor_scalar(pwm[:, k, :], wt("pw", k), small[:, 46 + k:47 + k], None, ALU.mult)\
                        .then_inc(s_pwm, 1)
                yield SLOT["pw"] + 3
                ve.wait_ge(s_h2, f * 4 + 4)
                for k in range(K):
                    last = vec.tensor_reduce(small[:, 48 + k:49 + k], acc[:, k, :], AX.X, ALU.max)
                link(last)
                link(vec.tensor_scalar(small[:, 50:52], small[:, 48:50], PW_THRESH, None, ALU.is_ge))
                for k in range(K):
                    last = vec.scalar_tensor_tensor(out=x[:, k, :], in0=acc[:, k, :], scalar=small[:, 50 + k:51 + k],
                                                    in1=x[:, k, :], op0=ALU.mult, op1=ALU.add)
                last.then_inc(s_xmid, 1)
                ve.wait_ge(s_xmid, f + 1)
                yield SLOT["L3"]
                yield from group_norm(f * 5 + 5, SLOT["L3"])
                yield SLOT["L3"] + 4
                ve.wait_ge(s_norm, f * 4 + 4)
                yield from depthwise(q, "dw3", "dw3_b", SLOT["L3"] + 4)
                for t in range(TILES):
                    if t % 4 == 0:
                        yield SLOT["L3"] + 9 + t // 4
                    if t % 2 == 0:
                        ve.wait_ge(s_xpr, f * 4 + t // 2 + 1)
                    vec.tensor_tensor(big[:, t, :], bank(4 + t // 2, C, t % 2 * C), rows[:, 0:C], ALU.add)\
                        .then_inc(s_xprs, 1)
                yield SLOT["ln"] + 1
                ve.wait_ge(s_mean, f * 2 + 2)
                for k in range(K):
                    for h in range(2):
                        o = q[:, k, h * HALF:(h + 1) * HALF]
                        last = vec.tensor_tensor(o, o, bank(4 + h), ALU.subtract)
                    last.then_inc(s_cent, 1)
                yield SLOT["ln"] + 4
                ve.wait_ge(s_sd, f * 2 + 2)
                link(vec.reciprocal(tr, tr))
                for k in range(K):
                    vec.tensor_tensor(q[:, k, :], q[:, k, :], tr, ALU.mult).then_inc(s_xhat, 1)
                for t in range(TILES):
                    yield SLOT["om"] + (t + 1) // 2
                    ve.wait_ge(s_om, f * TILES + t + 1)
                    vec.tensor_tensor(om[:, t, :], bank(4 + t % 4, OM), rows[:, C:C + OM], ALU.add).then_inc(s_oms, 1)
                yield SLOT["om"] + 5
                ve.wait_ge(s_oms, f * TILES + TILES)
                planes = om.rearrange("p t (g c m) -> p (t g) c m", g=G, c=3)
                tx, ty, mask = planes[:, :, 0, :], planes[:, :, 1, :], planes[:, :, 2, :]
                red = tg[:, 0, :]
                wide = red.rearrange("p (a o) -> p a o", o=1).broadcast_to([P, TILES * G, TAPS])
                link(vec.tensor_reduce(red, mask, AX.X, ALU.max))
                vec.tensor_tensor(mask, mask, wide, ALU.subtract).then_inc(s_msub, 1)
                yield SLOT["om"] + 6
                by_tg = lambda ap: ap.rearrange("p (a m) -> p a m", m=TAPS)
                f3, m3, k3 = by_tg(flag), by_tg(mout[:, :]), by_tg(keys[:, :])
                for o, t in ((f3, tx), (m3, ty)):
                    last = vec.scalar_tensor_tensor(out=o, in0=t, scalar=-1.0, in1=t, op0=ALU.mult, op1=ALU.max)
                link(last)
                link(vec.tensor_tensor(f3, f3, m3, ALU.max))
                link(vec.tensor_scalar(f3, f3, float(R), None, ALU.is_gt))
                yield SLOT["om"] + 7
                ve.wait_ge(s_mexp, f + 1)
                link(vec.tensor_reduce(red, mask, AX.X, ALU.add))
                link(vec.reciprocal(red, red))
                link(vec.tensor_tensor(mask, mask, wide, ALU.mult))
                link(vec.tensor_tensor(m3, mask, f3, ALU.mult))
                vec.tensor_tensor(mask, mask, m3, ALU.subtract).then_inc(s_omr, 1)
                yield SLOT["sparse"]
                vec.tensor_reduce(runs[:, 0:1], flag, AX.X, ALU.add).then_inc(s_cnt, 1)
                link(vec.tensor_tensor(k3, f3, cst_("code").rearrange("p (a o) -> p a o", o=1)
                                       .broadcast_to([P, TILES * G, TAPS]), ALU.mult))
                link(vec.tensor_tensor(k3, k3, cst_("tap_code").rearrange("p (o m) -> p o m", o=1)
                                       .broadcast_to([P, TILES * G, TAPS]), ALU.add))
                link(vec.tensor_tensor(k3, k3, f3, ALU.mult))
                ve.wait_ge(s_imgw, (f + 1) * 16 * TILES * TR)
                link(vec.memset(bigf, 0.0))
                ve.wait_ge(s_xmidw, (f + 1) * 16)
                ve.wait_ge(s_cntr, f + 1)
                link(vec.tensor_scalar(runs[:, 1:2], runs[:, 1:2], 1.0, None, ALU.max))
                link(vec.tensor_tensor(runs[:, 1:2], runs[:, 2:3], runs[:, 1:2], ALU.add))
                vec.tensor_copy(runs_i[0:1, 0:1], runs[0:1, 2:3]).then_inc(s_runs, 1)
                vec.tensor_copy(runs_i[0:1, 1:2], runs[0:1, 1:2]).then_inc(s_runs, 1)
                ve.wait_ge(s_runs, f * 2 + 2)
                link(vec.tensor_copy(runs[:, 2:3], runs[:, 1:2]), alone=True)
                first = ve.value_load(runs_i[0:1, 0:1], min_val=0, max_val=1 << 20)
                end = ve.value_load(runs_i[0:1, 1:2], min_val=0, max_val=1 << 20)
                with ve.Fori(first, end) as it:
                    rk = {"k": 0}

                    def rlink(ins):
                        rk["k"] += 1
                        ins.then_inc(s_rv, 1)
                        ve.wait_ge(s_rv, it * RLINKS + rk["k"])

                    top, sel, pos, flr, frac = rs[:, 0:1], rs[:, 8:13], rs[:, 13:15], rs[:, 15:17], rs[:, 17:19]
                    wxa, wya, w4 = rs[:, 19:21], rs[:, 21:23], rs[:, 23:27]
                    lin, val, up = rs[:, 27:29], rs[:, 32:48], rs[:, 48:50]
                    kmax, tgsel = tg[:, 0, :], tg[:, 1, :]
                    rlink(vec.tensor_reduce(kmax, k3, AX.X, ALU.max))
                    rlink(vec.tensor_reduce(top, kmax, AX.X, ALU.max))
                    rlink(vec.tensor_scalar(top, top, 0.5, None, ALU.max))
                    vec.tensor_scalar(tgsel, kmax, top, None, ALU.is_equal)
                    rlink(vec.tensor_scalar(onehot, keys[:, :], top, None, ALU.is_equal))
                    for c, table in enumerate((tx, ty, m3)):
                        rlink(vec.scalar_tensor_tensor(out=by_tg(junk), in0=by_tg(onehot), scalar=1.0, in1=table,
                                                       op0=ALU.mult, op1=ALU.mult, accum_out=sel[:, c:c + 1]))
                    for c, table in enumerate(("group_of", "row_of")):
                        rlink(vec.scalar_tensor_tensor(out=junk[:, 0:TILES * G], in0=tgsel, scalar=1.0, in1=cst_(table),
                                                       op0=ALU.mult, op1=ALU.mult, accum_out=sel[:, 3 + c:4 + c]))
                    rlink(vec.tensor_tensor(pos[:, 1:2], sel[:, 1:2], sel[:, 4:5], ALU.add))
                    rlink(vec.tensor_copy(pos[:, 0:1], sel[:, 0:1]))
                    rlink(vec.tensor_tensor(pos, pos, cst_("pixel_xy"), ALU.add))
                    rlink(vec.tensor_scalar(pos, pos, -2.0, float(H), ALU.max, ALU.min))
                    rlink(vec.tensor_copy(fli[:, :], pos))
                    rlink(vec.tensor_copy(flr, fli[:, :]))
                    rlink(vec.tensor_tensor(up, flr, pos, ALU.is_gt))
                    rlink(vec.tensor_tensor(flr, flr, up, ALU.subtract))
                    rlink(vec.tensor_scalar(lin[:, 0:1], sel[:, 3:4], float(PADH * PADW), flr[:, 0:1], ALU.mult, ALU.add))
                    rlink(vec.scalar_tensor_tensor(out=lin[:, 1:2], in0=flr[:, 1:2], scalar=float(PADW), in1=lin[:, 0:1],
                                                   op0=ALU.mult, op1=ALU.add))
                    vec.tensor_scalar(idx4[:, :], cst_("corner"), lin[:, 1:2], None, ALU.add).then_inc(s_idx, 1)
                    vec.scalar_tensor_tensor(out=keys[:, :], in0=keys[:, :], scalar=top, in1=keys[:, :],
                                             op0=ALU.not_equal, op1=ALU.mult)
                    rlink(vec.tensor_tensor(frac, pos, flr, ALU.subtract))
                    vec.tensor_copy(wxa[:, 1:2], frac[:, 0:1])
                    vec.tensor_scalar(wxa[:, 0:1], frac[:, 0:1], -1.0, 1.0, ALU.mult, ALU.add)
                    vec.tensor_scalar(wya[:, 1:2], frac[:, 1:2], sel[:, 2:3], None, ALU.mult)
                    rlink(vec.tensor_scalar(up[:, 0:1], frac[:, 1:2], -1.0, 1.0, ALU.mult, ALU.add))
                    rlink(vec.tensor_scalar(wya[:, 0:1], up[:, 0:1], sel[:, 2:3], None, ALU.mult))
                    for c in range(2):
                        last = vec.tensor_scalar(w4[:, 2 * c:2 * c + 2], wxa, wya[:, c:c + 1], None, ALU.mult)
                    rlink(last)
                    ve.wait_ge(s_gd, it + 1)
                    vec.tensor_tensor(gat[:, :, :], gat[:, :, :], w4.rearrange("p (k o) -> p k o", o=1)
                                      .broadcast_to([P, CORNERS, CG]), ALU.mult).then_inc(s_gatu, 1)
                    ve.wait_ge(s_gatu, it + 1)
                    rlink(vec.tensor_reduce(val, gat[:, :, :].rearrange("p k c -> p c k"), AX.X, ALU.add))
                    for c in range(CG):
                        o = bigf.rearrange("p (a c) -> p a c", c=CG)[:, :, c]
                        last = vec.scalar_tensor_tensor(out=o, in0=tgsel, scalar=val[:, c:c + 1], in1=o,
                                                        op0=ALU.mult, op1=ALU.add)
                    rlink(last)
                    assert rk["k"] == RLINKS, rk
                vec.memset(small[0:1, 62:63], 0.0).then_inc(s_spb, 1)
                assert chain["k"] == VLINKS, chain

            def window(n, u):
                at, w = n * TAPS2 + u, u - 1
                if u == -1:
                    wait(ve, s_sampw, n * 16)
                    vec.memset(samp[:, UP:], 0.0)
                    vec.memset(pacc[:, :], 0.0).then_inc(s_az, 1)
                    ve.wait_ge(s_az, n + 1)
                    ve.wait_ge(s_img, (n + 1) * 16 * G)
                    vec.memset(small[0:1, 61:62], 0.0)
                if 0 <= u < TAPS2:
                    dy, d = u // D, u % D
                    if u >= 2:
                        ve.wait_ge(s_psum, at - 1)
                        if VSUM(u - 2):
                            ve.wait_ge(s_vacc, n * NV + vcount(u - 2))
                        else:
                            ve.wait_ge(s_pacc, n * (TAPS2 - NV) + (u - 1) - vcount(u - 2))
                    ve.wait_ge(s_wd, at + 1)
                    wtap = bank(u % 2, PIX).rearrange("p (r x o) -> p r x o", r=TR, o=1).broadcast_to([P, TR, W, CG])
                    src = img[:, :].rearrange("p (y x) -> p y x", y=IMGR)[:, dy:dy + TR, d * CG:(d + W) * CG]\
                        .rearrange("p r (x c) -> p r x c", c=CG)
                    dst = tapped[:, u % 2, :].rearrange("p (r x c) -> p r x c", r=TR, c=CG)
                    vec.tensor_tensor(dst, wtap, src, ALU.mult).then_inc(s_tap, 1)
                if 0 <= w < TAPS2 and VSUM(w):
                    ve.wait_ge(s_tap, n * TAPS2 + w + 1)
                    if vcount(w) > 1:
                        ve.wait_ge(s_vacc, n * NV + vcount(w) - 1)
                    vec.tensor_tensor(samp[:, UP:], samp[:, UP:], tapped[:, w % 2, UP:], ALU.add).then_inc(s_vacc, 1)
                if u == TAPS2 + 1:
                    ve.wait_ge(s_psum, (n + 1) * TAPS2)
                    vec.tensor_copy(samp[:, 0:UP], ps[:, 2:4, :].rearrange("p b n -> p (b n)")).then_inc(s_samp, 1)
                    ve.wait_ge(s_pacc, (n + 1) * (TAPS2 - NV))
                    ve.wait_ge(s_vacc, (n + 1) * NV)
                    vec.tensor_tensor(samp[:, UP:], samp[:, UP:], pacc[:, :], ALU.add).then_inc(s_samp, 1)

            run(ve, side, window)

        @block.scalar
        def _(ac):
            act = nc.scalar
            ac.wait_ge(s_load, 16 * N_LOAD)
            ac.wait_ge(s_vset, 12)

            def side(f, m):
                if m is not None:
                    yield SLOT["finish"] + 2
                    for j in range(4):
                        ac.wait_ge(s_oT, m * 2 + j // 2 + 1)
                        act.activation(q[:, j // 2, j % 2 * HALF:(j % 2 + 1) * HALF], bank(4 + j), ACT.Copy)\
                            .then_inc(s_oTs, 1)
                if f is None:
                    return
                for j in range(4):
                    yield SLOT["L0"] + 1 + j
                    ac.wait_ge(s_q, f * 4 + j + 1)
                    act.activation(q[:, j // 2, j % 2 * HALF:(j % 2 + 1) * HALF], bank(4 + j), ACT.Identity,
                                   bias=col("q_bias", j // 2)).then_inc(s_qs, 1)
                yield SLOT["L0"] + 5
                for j in (1, 3):
                    ac.wait_ge(s_qt, f * 4 + j + 1)
                    act.activation(qT[:, 2 * j:2 * j + 2, :].rearrange("p t c -> p (t c)"), bank(4 + j), ACT.Copy)\
                        .then_inc(s_qta, 1)
                yield SLOT["L0"] + 10
                if m is not None:
                    ac.wait_ge(s_stored, (m + 1) * 16)
                ac.wait_ge(s_mx, f + 1)
                for k in range(K):
                    act.activation(e[:, k, :], bank(4, C, k * C), ACT.Exp, bias=small[:, 32 + k:33 + k],
                                   accum_out=small[:, 34 + k:35 + k]).then_inc(s_e, 1)
                yield SLOT["L1"] + 6
                ac.wait_ge(s_xvz, f + 1)

                def keep_xv(j, b):
                    ac.wait_ge(s_xv, f * 4 + j + 1)
                    act.activation(rows_of(xvp, j // 2, j % 2), bank(b).rearrange("p (h w) -> p h w", w=W),
                                   ACT.Copy).then_inc(s_xvs, 1)

                keep_xv(0, 6)
                keep_xv(1, 7)
                yield SLOT["L1"] + 7
                keep_xv(2, 6)
                yield SLOT["L1"] + 8
                ac.wait_ge(s_tsc, f + 1)
                act.activation(tr, ps[:, 4:6, :].rearrange("p b n -> p (b n)"), ACT.Relu, bias=small[:, 41:42],
                               scale=small[:, 40:41]).then_inc(s_tr, 1)
                yield SLOT["dyn"]
                keep_xv(3, 4)
                yield SLOT["pw"] - 2
                for k in range(K):
                    ac.wait_ge(s_dw, f * 2 + k + 1)
                    act.activation(q[:, k, :], acc[:, k, :], ACT.Relu, bias=col("dw2_b", k), scale=col("bn1_g", k))\
                        .then_inc(s_h, 1)
                for j in range(4):
                    yield SLOT["pw"] + 1 + j // 2
                    ac.wait_ge(s_pw, f * 4 + j + 1)
                    act.activation(acc[:, j // 2, j % 2 * HALF:(j % 2 + 1) * HALF], bank(4 + j), ACT.Relu,
                                   bias=col("pw_b", j // 2), scale=col("bn2_g", j // 2)).then_inc(s_h2, 1)
                yield SLOT["L3"] + 4
                ac.wait_ge(s_norm, f * 4 + 4)
                for k in range(K):
                    act.activation(acc[:, k, :].rearrange("p (h w) -> p h w", h=H), xp[:, k, 1:1 + H, 1:1 + W], ACT.Copy)\
                        .then_inc(s_flat, 1)
                yield SLOT["ln"] + 1
                ac.wait_ge(s_xpr, f * 4 + 4)
                for k in range(K):
                    ac.wait_ge(s_cent, f * 2 + k + 1)
                    act.activation(acc[:, k, :], q[:, k, :], ACT.Square).then_inc(s_sq, 1)
                yield SLOT["ln"] + 3
                for h in range(2):
                    ac.wait_ge(s_lvar, f * 2 + h + 1)
                    act.activation(tr[:, h * HALF:(h + 1) * HALF], bank(4 + h), ACT.Sqrt, bias=cst_("eps"))\
                        .then_inc(s_sd, 1)
                yield SLOT["ln"] + 4
                for k in range(K):
                    ac.wait_ge(s_xhat, f * 2 + k + 1)
                    act.activation(q[:, k, :], q[:, k, :], ACT.Gelu, bias=col("ln_b", k), scale=col("ln_g", k))\
                        .then_inc(s_gelu, 1)
                yield SLOT["om"] + 6
                ac.wait_ge(s_msub, f + 1)
                mask = om.rearrange("p t (g c m) -> p (t g) c m", g=G, c=3)[:, :, 2, :]
                act.activation(mask, mask, ACT.Exp).then_inc(s_mexp, 1)

            def window(n, u):
                v = u + 3
                if v >= TAPS2:
                    return
                dy, d = v // D, v % D
                hats = TAPS2 + D
                tv = tb[:, :, :].rearrange("p n (c m) -> p c m n", c=3)
                k = n * hats + dy * (D + 1) + d
                if d == 0:
                    if v == 0:
                        ac.wait_ge(s_tb, (n + 1) * 16)
                    elif dy >= 2:
                        ac.wait_ge(s_wyd, n * D + dy - 1)
                    act.activation(haty[:, dy % 2], tv[:, 1], ACT.Abs, bias=cst_("minus_d")[:, dy:dy + 1]).then_inc(s_a, 1)
                    ac.wait_ge(s_a, k + 1)
                    act.activation(haty[:, dy % 2], haty[:, dy % 2], ACT.Relu, bias=1.0, scale=-1.0).then_inc(s_hy, 1)
                if v >= 3:
                    ac.wait_ge(s_prod, n * TAPS2 + v - 2)
                act.activation(hatx[:, v % 3], tv[:, 0], ACT.Abs, bias=cst_("minus_d")[:, d:d + 1]).then_inc(s_a, 1)
                ac.wait_ge(s_a, k + 2)
                act.activation(hatx[:, v % 3], hatx[:, v % 3], ACT.Relu, bias=1.0, scale=-1.0).then_inc(s_hx, 1)

            run(ac, side, window)

        @block.gpsimd
        def _(po):
            pool = nc.gpsimd
            po.wait_ge(s_vset, 2)
            po.wait_ge(s_load, 16 * N_LOAD)
            for bn in ("bn1", "bn2"):
                pool.tensor_tensor(col(bn + "_v", 0, K), col(bn + "_v", 0, K), cst_("half")[:, 0:K], ALU.pow)\
                    .then_inc(s_gset, 1)
            po.wait_ge(s_vset, 12)

            def side(f, m):
                if f is None:
                    return

                def rstd(stat, c):
                    po.wait_ge(s_var, stat)
                    pool.tensor_tensor(small[:, 28:28 + c], small[:, 24:24 + c], cst_("half")[:, 0:c], ALU.pow)\
                        .then_inc(s_rstd, 1)

                yield SLOT["gn0"]
                rstd(f * 5 + 1, K)
                yield SLOT["L1"]
                wait_apart(po, s_x1, f + 1)
                pool.memset(qx[:, :], 0.0).then_inc(s_xvz, 1)
                yield SLOT["L1"] + 2
                rstd(f * 5 + 2, K)
                yield SLOT["L1"] + 7
                rstd(f * 5 + 3, 1)
                yield SLOT["L2"] + 2
                rstd(f * 5 + 4, K)
                yield SLOT["L3"] + 2
                rstd(f * 5 + 5, K)
                yield SLOT["sparse"]
                wait_apart(po, s_cnt, f + 1)
                pool.partition_all_reduce(runs[:, 1:2], runs[:, 0:1], P, bass.bass_isa.ReduceOp.max).then_inc(s_cntr, 1)
                wait_apart(po, s_imgw, (f + 1) * 16 * TILES * TR)
                wait_apart(po, s_runs, f * 2 + 2)
                first = po.value_load(runs_i[0:1, 0:1], min_val=0, max_val=1 << 20)
                end = po.value_load(runs_i[0:1, 1:2], min_val=0, max_val=1 << 20)
                with po.Fori(first, end) as it:
                    wait_apart(po, s_idx, it + 1)
                    for c in range(CORNERS):
                        pool.indirect_dma_start(
                            out=gat[:, c, :], out_offset=None, in_=img_dram,
                            in_offset=bass.IndirectOffsetOnAxis(ap=idx4[:, c:c + 1], axis=0)).then_inc(s_gat, 16)
                    po.wait_ge(s_gat, 16 * CORNERS)
                    pool.memset(pdone[:, :], 0.0).then_inc(s_gd, 1)
                    po.inc_swdge_sem([s_gat], [16 * CORNERS], mode="sub")
                    po.wait_ge(s_gd, it + 1)

            def window(n, u):
                v, w = u + 2, u - 1
                if 0 <= v < TAPS2:
                    dy, d = v // D, v % D
                    at = n * TAPS2 + v
                    if d == 0:
                        po.wait_ge(s_hy, n * D + dy + 1)
                        if v > 0:
                            po.wait_ge(s_prod, at)
                        mk = tb[:, :, :].rearrange("p n (c m) -> p c m n", c=3)[:, 2]
                        pool.tensor_tensor(wy[:, :, :], haty[:, dy % 2], mk, ALU.mult).then_inc(s_wyd, 1)
                        po.wait_ge(s_wyd, n * D + dy + 1)
                    po.wait_ge(s_hx, at + 1)
                    if v >= 3:
                        po.wait_ge(s_wd, at - 2)
                    pool.tensor_tensor(prod[:, v % 3], wy[:, :, :], hatx[:, v % 3], ALU.mult).then_inc(s_prod, 1)
                if 0 <= w < TAPS2 and not VSUM(w):
                    k = n * (TAPS2 - NV) + w + 1 - vcount(w)
                    po.wait_ge(s_tap, n * TAPS2 + w + 1)
                    if w + 1 - vcount(w) == 1:
                        po.wait_ge(s_az, n + 1)
                    else:
                        po.wait_ge(s_pacc, k - 1)
                    pool.tensor_tensor(pacc[:, :], pacc[:, :], tapped[:, w % 2, UP:], ALU.add).then_inc(s_pacc, 1)

            run(po, side, window)


VLINKS = 102
RLINKS = 25


def VSUM(u):
    return u % 2 == 0


def vcount(u):
    return sum(VSUM(i) for i in range(u + 1))


NV = vcount(TAPS2 - 1)


def consts():
    out = np.zeros((P, NCST), np.float32)

    def put(name, value):
        a, n = CST[name]
        out[:, a:a + n] = value

    put("ident", np.eye(P))
    put("group8", np.kron(np.eye(P // 8), np.full((8, 8), 1 / 8)))
    put("mean256", 1 / C)
    tile_group = np.arange(TILES * G)
    put("code", (TILES * G - tile_group) * TAPS)
    put("tap_code", -np.arange(TAPS))
    put("group_of", tile_group % G)
    put("row_of", tile_group // G * TR)
    pix = np.arange(P)
    put("pixel_xy", np.stack([pix % W, pix // W], 1))
    put("corner", R * PADW + R + np.array([0, 1, PADW, PADW + 1]))
    put("minus_d", R - np.arange(D))
    grid = np.zeros((G, 3, TAPS))
    grid[:, 0], grid[:, 1] = np.arange(TAPS) // 3 - 1, np.arange(TAPS) % 3 - 1
    put("grid", grid.reshape(-1))
    put("half", -0.5)
    put("eps", LN_EPS)
    return out


PERMS = ((0, 1, 2, 3, 4, 5, 6, 7), (3, 0, 1, 2, 5, 6, 7, 4), (2, 3, 0, 1, 6, 7, 4, 5), (1, 2, 3, 0, 7, 4, 5, 6),
         (4, 5, 6, 7, 0, 1, 2, 3), (5, 6, 7, 4, 3, 0, 1, 2), (6, 7, 4, 5, 2, 3, 0, 1), (7, 4, 5, 6, 1, 2, 3, 0))


def tap_perms():
    a = np.arange(TAPS).reshape(3, 3)
    turned = [a, np.rot90(a, 1), np.rot90(a, 2), np.rot90(a, 3),
              np.rot90(a.T, 3), np.rot90(a.T, 2), np.rot90(a.T, 1), a.T]
    return np.stack([t.reshape(-1) for t in turned])


def lay_out(inp):
    a = {k: np.asarray(v) for k, v in inp.items()}

    def chunks(w):
        return w.reshape(K, P, -1)

    def d4(w):
        perms = np.array(PERMS)
        full = w[:, :, perms]
        return full.transpose(1, 3, 0, 2).reshape(w.shape[1] * 8, w.shape[0] * 8)

    off = a["L3_conv_off_w"].reshape(C, G, TAPS, 2)
    offb = a["L3_conv_off_b"].reshape(G, TAPS, 2)
    om_w = np.stack([off[..., 0], off[..., 1], a["L3_conv_mask_w"].reshape(C, G, TAPS)], 2).reshape(C, OM)
    om_b = np.stack([offb[..., 0], offb[..., 1], a["L3_conv_mask_b"].reshape(G, TAPS)], 1).reshape(OM)
    parts = {"w0": a["L0_conv_w"].T, "wv": d4(a["L1_conv_w_v"]), "w1": d4(a["L1_conv_w1"]),
             "pw": a["L2_conv_pw_w"].reshape(C, C).T, "in_w": a["L3_conv_in_w"], "om_w": om_w, "out_w": a["L3_conv_out_w"]}
    weights = np.concatenate([chunks(parts[name]) for name in WTS], 2)

    perm = tap_perms()
    w2 = a["L1_conv_w2"].reshape(K, TAPS, P // 8)
    w2x = np.zeros((P // 8, 8, K, TAPS, P // 8, 8), np.float32)
    for g in range(8):
        for c in range(P // 8):
            w2x[:, g, :, :, c, g] = w2[:, perm[g], :].transpose(2, 0, 1)
    b2 = a["L1_conv_b2"].reshape(K, TAPS)[:, perm]
    b2 = np.tile(b2.transpose(1, 0, 2).reshape(8, K * TAPS), (P // 8, 1))

    def two(v):
        return v.reshape(K, P).T

    def taps(w):
        return w.reshape(K, P, TAPS).transpose(1, 0, 2).reshape(P, K * TAPS)

    c = {"q_bias": two(a["L0_conv_bias"]), "dw2_b": two(a["L2_conv_dw_b"]), "pw_b": two(a["L2_conv_pw_b"]),
         "dw3_b": two(a["L3_conv_dw_b"]), "ln_g": two(a["L3_conv_ln_g"]), "ln_b": two(a["L3_conv_ln_b"]),
         "out_b": two(a["L3_conv_out_b"]), "t_gamma": a["L1_conv_gn_gamma"].reshape(P, 1),
         "t_beta": a["L1_conv_gn_beta"].reshape(P, 1), "dw2": taps(a["L2_conv_dw_w"]), "dw3": taps(a["L3_conv_dw_w"]),
         "b2": b2}
    for bn in ("bn1", "bn2"):
        for v in "gbmv":
            c[f"{bn}_{v}"] = two(a[f"L2_conv_{bn}_{v}"])
    cols = np.concatenate([c[name] for name in COLS], 1)
    rows = np.tile(np.concatenate([a["L3_conv_in_b"], om_b])[None], (P, 1))
    arrays = {"x_in": a["x"].reshape(B, C, N), "weights_in": weights, "w2x_in": w2x.reshape(P, K * TAPS * P),
              "cols_in": cols, "rows_in": rows, "consts_in": consts()}
    return {k: np.ascontiguousarray(v) for k, v in arrays.items()}


def kernel(**inputs):
    import concourse.bacc as bacc
    from concourse.bass_utils import run_bass_kernel_spmd as run

    arrays = lay_out(inputs)
    nc = bacc.Bacc("TRN2", target_bir_lowering=False, num_devices=1)
    args = {k: nc.dram_tensor(k, v.shape, F32, kind="ExternalInput").ap() for k, v in arrays.items()}
    out = nc.dram_tensor("out", (B, C, N), F32, kind="ExternalOutput").ap()
    build(nc, out=out, **args)
    r = run(nc, [arrays], core_ids=[0])
    return r.results[0]["out"].reshape(B, C, H, W)
```

```python
from contextlib import ExitStack

import concourse.bass as bass
import numpy as np
from concourse import mybir

F32 = mybir.dt.float32
I32 = mybir.dt.int32
ALU = mybir.AluOpType
ACT = mybir.ActivationFunctionType
AX = mybir.AxisListType

P = 128
B, C, H, W = 16, 256, 32, 32
K = C // P
N = H * W
HALF = N // 2
HR = H // 2
TILES = N // P
TR = P // W
GN_EPS, LN_EPS, BN_EPS = 1e-5, 1e-5, 1e-5
DW_THRESH, PW_THRESH = 4.0, 0.001
TAPS = 9
G = 16
CG = C // G
OM = G * 3 * TAPS
R = 4
D = 2 * R + 1
PADW = W + 2 * R
PADH = H + 2 * R
ROWF = PADW * CG
IMGR = TR + 2 * R
PIX = P
REACH = R
TAP = [(i, j) for i in range(D) for j in range(D) if abs(i - R) + abs(j - R) < 2 * R]
TAPS2 = len(TAP)
CH = 4
LEAD = 3
END = 1 << 30

STEP = {"gn0": -LEAD, "finish": 5}
for _name, _after, _steps in (("L0", "finish", 5), ("L1", "L0", 16), ("dyn", "L1", 9), ("L2", "dyn", 11),
                              ("pw", "L2", 9), ("L3", "pw", 4), ("ln", "L3", 11), ("om", "ln", 5), ("sparse", "om", 8)):
    STEP[_name] = STEP[_after] + _steps


def tap_of(step):
    if step <= 0:
        return step
    if step >= STEP["sparse"]:
        return TAPS2 + 1 + step - STEP["sparse"]
    return step * TAPS2 // STEP["sparse"]


COLS = {}
_at = 0
for _name, _n in (("q_bias", K), ("dw2_b", K), ("bn1_g", K), ("bn1_b", K), ("bn1_m", K), ("bn1_v", K),
                  ("pw_b", K), ("bn2_g", K), ("bn2_b", K), ("bn2_m", K), ("bn2_v", K), ("dw3_b", K),
                  ("ln_g", K), ("ln_b", K), ("out_b", K), ("t_gamma", 1), ("t_beta", 1),
                  ("dw2", K * TAPS), ("dw3", K * TAPS), ("b2", K * TAPS)):
    COLS[_name] = (_at, _n)
    _at += _n
NCOLS = _at
WTS = {}
_at = 0
for _name, _n in (("w0", C), ("wv", C), ("w1", P), ("pw", C), ("in_w", C), ("om_w", OM), ("out_w", C)):
    WTS[_name] = (_at, _n)
    _at += _n
NWTS = _at
CST = {}
_at = 0
for _name, _n in (("ident", P), ("group8", P), ("mean256", P), ("code", TILES * G), ("tap_code", TAPS),
                  ("group_of", TILES * G), ("row_of", TILES * G), ("tg_code", TILES * G), ("pixel_xy", 2),
                  ("middle", 2 * TAPS), ("reach", 2 * TAPS), ("minus_d", D),
                  ("grid", OM), ("half", 2), ("eps", 1)):
    CST[_name] = (_at, _n)
    _at += _n
NCST = _at


def build(nc, x_in, weights_in, w2x_in, cols_in, rows_in, consts_in, out, batches=B):
    ctx = ExitStack()
    with ctx:
        def sb(name, shape, dt=F32):
            return ctx.enter_context(nc.sbuf_tensor(name, shape, dt))

        def sem(name):
            return ctx.enter_context(nc.semaphore(name))

        def dram(name, shape):
            return nc.dram_tensor(name, shape, F32, kind="Internal").ap()

        img_dram = dram("img_dram", [G * PADH * PADW, CG])
        om_dram = dram("om_dram", [G, TILES, PIX, 3 * TAPS])
        samp_dram = dram("samp_dram", [G, TILES, PIX, CG])
        spb_dram = dram("spb_dram", [2, P, TILES * C])
        xmid_dram = dram("xmid_dram", [2, P, K * N])

        wts = sb("wts", [P, K, NWTS])
        w2x = sb("w2x", [P, K, TAPS, P])
        cols = sb("cols", [P, NCOLS])
        rows = sb("rows", [P, C + OM])
        cst = sb("cst", [P, NCST])
        x = sb("x", [P, K, N])
        xp = sb("xp", [P, K, H + 2, W + 2])
        qx = sb("qx", [P, K * (H + 2) * (W + 2)])
        work = sb("work", [P, 4 * N])
        big = sb("big", [P, TILES, C])
        keys = sb("keys", [P, TILES * G * TAPS])
        mout = sb("mout", [P, TILES * G * TAPS])
        img = sb("img", [P, IMGR * ROWF])
        tb = sb("tb", [P, PIX, 3 * TAPS])
        hatx = sb("hatx", [P, 3, TAPS, PIX])
        haty = sb("haty", [P, 2, TAPS, PIX])
        wy = sb("wy", [P, TAPS, PIX])
        prod = sb("prod", [P, 3, TAPS, PIX])
        tapped = sb("tapped", [P, 2, PIX * CG])
        samp = sb("samp", [P, PIX * CG])
        pacc = sb("pacc", [P, PIX * CG // 2])
        stats = sb("stats", [P, K, 2, 6])
        small = sb("small", [P, 64])
        rs = sb("rs", [P, 160])
        red = sb("red", [P, TILES * G])
        idx = sb("idx", [P, 2, CH], I32)
        fli = sb("fli", [P, 2 * CH], I32)
        gat = sb("gat", [P, CH, 2, 2 * CG])
        zeros = sb("zeros", [P, P])
        tick = sb("tick", [1, 64])
        pdone = sb("pdone", [1, 1])
        runs = sb("runs", [P, 6])
        runs_i = sb("runs_i", [1, 2], I32)

        q = qx[:, 0:K * N].rearrange("p (k n) -> p k n", k=K)
        xvp = qx[:, :].rearrange("p (k h w) -> p k h w", k=K, h=H + 2)
        flag = qx[:, 0:TILES * G * TAPS]
        junk = qx[:, TILES * G * TAPS:2 * TILES * G * TAPS]
        beyond = qx[:, 0:2 * TILES * G * TAPS].rearrange("p (a c m) -> p a c m", c=2, m=TAPS)
        acc = work[:, 0:K * N].rearrange("p (k n) -> p k n", k=K)
        tr = work[:, K * N:K * N + N]
        e = tr[:, 0:K * C].rearrange("p (k n) -> p k n", k=K)
        et = tr[:, K * C:2 * K * C].rearrange("p (k n) -> p k n", k=K)
        pwm = tr[:, 0:K * C].rearrange("p (k n) -> p k n", k=K)
        tmp = work[:, 3 * N:4 * N].rearrange("p (b n) -> p b n", b=2)
        om = work[:, 0:TILES * OM].rearrange("p (t m) -> p t m", t=TILES)
        spb = acc
        res = work[:, 2 * N:4 * N].rearrange("p (k n) -> p k n", k=K)
        qT = big
        tg = flag[:, 0:CH * TILES * G].rearrange("p (j a) -> p j a", j=CH)
        xflat = x[:, :, :].rearrange("p k n -> p (k n)")
        bigf = big[:, :, :].rearrange("p t c -> p (t c)")
        placed_at = [tapped[:, 0, :], tapped[:, 1, :], bigf, tapped[:, 0, :]]
        assert len(placed_at) == CH
        UP = PIX * CG // 2

        def cst_(name):
            a, n = CST[name]
            return cst[:, a:a + n]

        def col(name, i=0, n=1):
            return cols[:, COLS[name][0] + i:COLS[name][0] + i + n]

        def wt(name, k, a=0, n=None):
            s, m = WTS[name]
            return wts[:, k, s + a:s + a + (m if n is None else n)]

        ident = cst_("ident")
        ps = ctx.enter_context(nc.psum_tensor("ps", [P, 8, 512], F32))

        s_load = sem("s_weights_loaded")
        s_x = sem("s_x_loaded")
        s_zero = sem("s_border_zeroed")
        s_zeroed_dram = sem("s_dram_border_zeroed")
        s_vset = sem("s_vector_setup")
        s_gset = sem("s_pool_setup")
        s_v = sem("s_vector_chain")
        s_a = sem("s_scalar_chain")
        s_gstat = sem("s_channel_stats")
        s_gsum = sem("s_group_stats")
        s_var = sem("s_group_variance")
        s_rstd = sem("s_group_rstd")
        s_norm = sem("s_normed")
        s_q = sem("s_q_psum")
        s_qs = sem("s_q_sbuf")
        s_qt = sem("s_qT_psum")
        s_qta = sem("s_qT_sbuf")
        s_sc = sem("s_scores_psum")
        s_mx = sem("s_score_max")
        s_e = sem("s_exp_scores")
        s_et = sem("s_eT_psum")
        s_ets = sem("s_eT_sbuf")
        s_att = sem("s_attention_psum")
        s_x1 = sem("s_x_after_attention")
        s_t1 = sem("s_t_psum")
        s_tsc = sem("s_t_scale")
        s_tr = sem("s_t_relu")
        s_xv = sem("s_xv_psum")
        s_xvs = sem("s_xv_sbuf")
        s_xvz = sem("s_xv_border_zeroed")
        s_dw0 = sem("s_depthwise_first_tap")
        s_w = sem("s_kernel_psum")
        s_wu = sem("s_kernel_used")
        s_dw = sem("s_depthwise_done")
        s_h = sem("s_h_relu")
        s_pwm = sem("s_pruned_pointwise_weights")
        s_pw = sem("s_pointwise_psum")
        s_h2 = sem("s_h2_relu")
        s_xmid = sem("s_x_before_layer_3")
        s_xmidw = sem("s_x_before_layer_3_in_dram")
        s_flat = sem("s_normed_unbordered")
        s_xpr = sem("s_xproj_psum")
        s_xprs = sem("s_xproj_sbuf")
        s_imgw = sem("s_img_in_dram")
        s_dw3 = sem("s_depthwise3_done")
        s_mean = sem("s_ln_mean_psum")
        s_cent = sem("s_ln_centered")
        s_sq = sem("s_ln_squared")
        s_lvar = sem("s_ln_var_psum")
        s_sd = sem("s_ln_sd")
        s_xhat = sem("s_ln_normed")
        s_gelu = sem("s_gelu")
        s_om = sem("s_om_psum")
        s_oms = sem("s_om_sbuf")
        s_ctr = sem("s_offsets_centred")
        s_far = sem("s_offsets_beyond_reach")
        s_abs = sem("s_offsets_absolute")
        s_msub = sem("s_mask_minus_max")
        s_mexp = sem("s_mask_exp")
        s_omr = sem("s_om_final")
        s_omw = sem("s_om_in_dram")
        s_tb = sem("s_om_by_group_loaded")
        s_img = sem("s_img_by_group_loaded")
        s_flag = sem("s_sparse_flags")
        s_cnt = sem("s_sparse_counts")
        s_cntr = sem("s_sparse_count_max")
        s_runs = sem("s_sparse_runs")
        s_rv = sem("s_sparse_chain")
        s_wg = sem("s_sparse_weighed")
        s_idx = sem("s_sparse_indices")
        s_gat = sem("s_sparse_gathered")
        s_gd = sem("s_sparse_gather_done")
        s_sval = sem("s_sparse_sample")
        s_spsum = sem("s_sparse_sample_summed")
        s_spend = sem("s_sparse_sum_psum")
        s_spb = sem("s_sparse_sum_done")
        s_spbw = sem("s_sparse_sum_in_dram")
        s_hx = sem("s_hat_x")
        s_hy = sem("s_hat_y")
        s_wyd = sem("s_wy")
        s_prod = sem("s_hat_products")
        s_wd = sem("s_tap_weight_psum")
        s_tap = sem("s_tapped")
        s_psum = sem("s_tensor_sum")
        s_vacc = sem("s_vector_sum")
        s_pacc = sem("s_pool_sum")
        s_az = sem("s_sums_zeroed")
        s_samp = sem("s_sampled")
        s_sampw = sem("s_sampled_in_dram")
        s_back = sem("s_finish_loaded")
        s_mixed = sem("s_sparse_added")
        s_oT = sem("s_outT_psum")
        s_oTs = sem("s_outT_sbuf")
        s_fin = sem("s_out_psum")
        s_xdone = sem("s_x_final")
        s_stored = sem("s_x_stored")

        N_LOAD = 5
        N_BACK = TILES + 2
        block = ctx.enter_context(nc.Block())

        def bank(b, n=512, at=0):
            return ps[:, b, at:at + n]

        def rows_of(t3, k, half):
            return t3[:, k, 1 + half * HR:1 + (half + 1) * HR, 1:1 + W]

        def shifted(t3, k, i, j, r0=0, nr=H):
            return t3[:, k, r0 + i:r0 + i + nr, j:j + W]

        def wait(eng, semaphore, value):
            if not isinstance(value, int) or value > 0:
                eng.wait_ge(semaphore, value)

        cells = iter(range(64))

        def wait_apart(eng, semaphore, value):
            if isinstance(value, int):
                wait(eng, semaphore, value)
                return
            i = next(cells)
            cell = tick[:, i:i + 1]
            if eng is nc.tensor:
                value = eng.snap(value)
                eng.wait_ge(s_load, 16 * N_LOAD)
            eng.wait_ge(semaphore, value)
            if eng is nc.vector:
                eng.memset(cell, 0.0)
            elif eng is nc.gpsimd:
                eng.tensor_tensor(cell, cst_("half")[0:1, 0:1], cst_("half")[0:1, 0:1], ALU.add)

        def run(eng, side, window):
            def body(n, f, m):
                stream = side(f, m)
                until = next(stream, END)
                for u in range(-LEAD, TAPS2 + 2):
                    window(n, u)
                    while tap_of(until) <= u:
                        until = next(stream, END)
                assert until == END

            def alone(f, m):
                for _ in side(f, m):
                    pass

            alone(0, None)
            body(0, 1, None)
            if batches > 2:
                with eng.Fori(1, batches - 1) as n:
                    body(n, n + 1, n - 1)
            body(batches - 1, None, batches - 2)
            alone(None, batches - 1)

        @block.sync
        def _(sp):
            sp.dma_start(wts[:, :, :], weights_in.rearrange("k p n -> p k n")).then_inc(s_load, 16)
            sp.dma_start(w2x[:, :, :, :].rearrange("p k t n -> p (k t n)"), w2x_in).then_inc(s_load, 16)
            sp.dma_start(cols[:, :], cols_in).then_inc(s_load, 16)
            sp.dma_start(rows[:, :], rows_in).then_inc(s_load, 16)
            sp.dma_start(cst[:, :], consts_in).then_inc(s_load, 16)
            sp.wait_ge(s_zero, 1)
            sp.dma_start(img_dram.rearrange("(p n) c -> p (n c)", p=P), img[:, 0:G * PADH * PADW * CG // P])\
                .then_inc(s_zeroed_dram, 16)
            sp.wait_ge(s_zeroed_dram, 16)

            def load_x(f):
                wait(sp, s_xmidw, f * 16)
                sp.dma_start(x[:, :, :], x_in[bass.ds(f, 1)].rearrange("o (k p) n -> p (o k) n", p=P))\
                    .then_inc(s_x, 16)

            def front(f, more=True):
                sp.wait_ge(s_xmid, f + 1)
                sp.dma_start(xmid_dram[bass.ds(f % 2, 1)].rearrange("o p n -> p (o n)"), xflat).then_inc(s_xmidw, 16)
                grouped = img_dram.rearrange("(g y x) c -> y x g c", g=G, y=PADH)
                wait(sp, s_img, f * 16 * G)
                for t in range(TILES):
                    sp.wait_ge(s_xprs, f * TILES + t + 1)
                    for r in range(TR):
                        y = R + t * TR + r
                        sp.dma_start(grouped[y, R:R + W], big[r * W:(r + 1) * W, t, :].rearrange(
                            "p (g c) -> p g c", g=G)).then_inc(s_imgw, 16)
                if more:
                    load_x(f + 1)
                wait(sp, s_tb, f * 16)
                sp.wait_ge(s_omr, f + 1)
                for t in range(TILES):
                    sp.dma_start(om_dram[:, t].rearrange("g n m -> n g m"),
                                 om[:, t, :].rearrange("p (g m) -> p g m", g=G)).then_inc(s_omw, 16)

            def store_sparse(f):
                sp.wait_ge(s_spb, f + 1)
                sp.dma_start(spb_dram[bass.ds(f % 2, 1)].rearrange("o p n -> p (o n)"), bigf).then_inc(s_spbw, 16)

            def window_loads(n):
                sp.wait_ge(s_imgw, (n + 1) * 16 * TILES * TR)
                sp.wait_ge(s_omw, (n + 1) * 16 * TILES)
                wait(sp, s_samp, n * 2)
                sp.dma_start(tb[:, :, :].rearrange("p n m -> p (n m)"),
                             om_dram.rearrange("g t n m -> (g t) (n m)")).then_inc(s_tb, 16)
                gs = img_dram.rearrange("(g y x) c -> g (y x c)", g=G, y=PADH)
                for g in range(G):
                    src = bass.AP(gs.tensor, g * PADH * ROWF, [[TR * ROWF, TILES], [1, IMGR * ROWF]])
                    sp.dma_start(img[g * TILES:(g + 1) * TILES, :], src).then_inc(s_img, 16)

            def save_window(n):
                sp.wait_ge(s_samp, (n + 1) * 2)
                sp.dma_start(samp_dram.rearrange("g t n c -> (g t) (n c)"), samp[:, :]).then_inc(s_sampw, 16)

            def reload(m, last_front):
                sp.wait_ge(s_spbw, last_front * 16)
                sp.dma_start(work[:, 0:K * N], spb_dram[bass.ds(m % 2, 1)].rearrange("o p n -> p (o n)"))\
                    .then_inc(s_back, 16)
                sp.dma_start(work[:, 2 * N:4 * N], xmid_dram[bass.ds(m % 2, 1)].rearrange("o p n -> p (o n)"))\
                    .then_inc(s_back, 16)
                sp.wait_ge(s_sampw, (m + 1) * 16)
                for t in range(TILES):
                    sp.dma_start(big[:, t, :].rearrange("p (g c) -> p g c", g=G),
                                 samp_dram[:, t].rearrange("g n c -> n g c")).then_inc(s_back, 16)

            def store(m):
                sp.wait_ge(s_xdone, m + 1)
                sp.dma_start(out[bass.ds(m, 1)].rearrange("o (k p) n -> p (o k) n", p=P), res).then_inc(s_stored, 16)

            def body(n, f, m, more=True):
                if m is not None:
                    reload(m, n + 1)
                    store(m)
                if f is not None:
                    front(f, more)
                save_window(n)
                if f is not None:
                    window_loads(f)
                    store_sparse(f)

            load_x(0)
            front(0)
            window_loads(0)
            store_sparse(0)
            body(0, 1, None, more=batches > 2)
            if batches > 3:
                with sp.Fori(1, batches - 2) as n:
                    body(n, n + 1, n - 1)
            if batches > 2:
                body(batches - 2, batches - 1, batches - 3, more=False)
            body(batches - 1, None, batches - 2)
            reload(batches - 1, batches)
            store(batches - 1)
            sp.wait_ge(s_stored, batches * 16)

        @block.tensor
        def _(pe):
            pe.wait_ge(s_load, 16 * N_LOAD)
            pe.wait_ge(s_zero, 6)
            pe.matmul(bank(4), zeros[:, :], cst[:, 0:512], start=True, stop=True).then_inc(s_spsum, CH)

            def group_stats(stat, c):
                pe.wait_ge(s_gstat, stat)
                pe.matmul(bank(7, c), cst_("group8"), small[:, 0:c], start=True, stop=True).then_inc(s_gsum, 1)

            def product(b, w, t, signal):
                for k in range(K):
                    mm = pe.matmul(bank(b), w(k), t(k), start=(k == 0), stop=(k == K - 1))
                mm.then_inc(signal, 1)

            def half_of(t3, h):
                return lambda k: t3[:, k, h * HALF:(h + 1) * HALF]

            def side(f, m):
                if f is not None:
                    yield STEP["gn0"] + 2
                    wait(pe, s_spb, f)
                    group_stats(f * 5 + 1, 4)
                if m is not None:
                    yield STEP["finish"] + 1
                    if f is not None:
                        pe.wait_ge(s_norm, f * 4 + 1)
                    pe.wait_ge(s_mixed, m + 1)
                    for k in range(K):
                        for t in range(TILES):
                            mm = pe.transpose(bank(4 + 2 * k + t // 4, P, t % 4 * P), big[:, t, k * P:(k + 1) * P], ident)
                        mm.then_inc(s_oT, 1)
                    yield STEP["finish"] + 3
                    pe.wait_ge(s_oTs, m * 4 + 4)
                    for j in range(4):
                        product(4 + j, lambda k: wt("out_w", k, j // 2 * P, P), half_of(q, j % 2), s_fin)
                        if j == 1:
                            yield STEP["finish"] + 4
                if f is None:
                    return
                yield STEP["L0"]
                pe.wait_ge(s_norm, f * 4 + 1)
                if m is not None:
                    pe.wait_ge(s_xdone, m + 1)
                for j in range(4):
                    product(4 + j, lambda k: wt("w0", k, j // 2 * P, P), lambda k: rows_of(xp, k, j % 2), s_q)
                    yield STEP["L0"] + 1 + j
                pe.wait_ge(s_qs, f * 4 + 4)
                for j in range(4):
                    for t in (2 * j, 2 * j + 1):
                        for k in range(K):
                            mm = pe.transpose(bank(4 + j, P, (t % 2) * C + k * P), q[:, k, t * P:(t + 1) * P], ident)
                    mm.then_inc(s_qt, 1)
                yield STEP["L0"] + 6
                pe.wait_ge(s_qta, f * 4 + 4)
                for k in range(K):
                    for t in range(TILES):
                        mm = pe.matmul(bank(4, C, k * C), qT[:, t, k * P:(k + 1) * P], qT[:, t, :],
                                       start=(t == 0), stop=(t == TILES - 1))
                        if t % 4 == 3 and (k, t) != (K - 1, TILES - 1):
                            yield STEP["L0"] + 7 + 2 * k + t // 4
                mm.then_inc(s_sc, 1)
                yield STEP["L0"] + 11
                pe.wait_ge(s_e, f * 2 + 2)
                for d in range(K):
                    for k in range(K):
                        mm = pe.transpose(bank(5, P, d * C + k * P), e[:, k, d * P:(d + 1) * P], ident)
                mm.then_inc(s_et, 1)
                yield STEP["L0"] + 13
                pe.wait_ge(s_ets, f + 1)
                for j in range(4):
                    product(4 + j, lambda d: et[:, d, j // 2 * P:(j // 2 + 1) * P], half_of(q, j % 2), s_att)
                    yield STEP["L0"] + 14 + j // 2

                yield STEP["L1"] + 1
                group_stats(f * 5 + 2, 4)
                yield STEP["L1"] + 4
                pe.wait_ge(s_norm, f * 4 + 2)
                for h in range(2):
                    product(4 + h, lambda k: wt("w1", k), lambda k: rows_of(xp, k, h), s_t1)
                for h in range(2):
                    yield STEP["L1"] + 5
                    product(6 + h, lambda k: wt("wv", k, 0, P), lambda k: rows_of(xp, k, h), s_xv)
                yield STEP["L1"] + 6
                pe.wait_ge(s_xvs, f * 4 + 2)
                group_stats(f * 5 + 3, 2)
                product(6, lambda k: wt("wv", k, P, P), lambda k: rows_of(xp, k, 0), s_xv)
                yield STEP["L1"] + 8
                pe.wait_ge(s_tr, f + 1)
                product(4, lambda k: wt("wv", k, P, P), lambda k: rows_of(xp, k, 1), s_xv)
                yield STEP["dyn"]
                pe.wait_ge(s_xvs, f * 4 + 4)
                for i in range(K * TAPS * 2):
                    half, tap, h = i // (2 * TAPS), i // 2 % TAPS, i % 2
                    if i >= 4:
                        pe.wait_ge(s_wu, f * 2 * K * TAPS + i - 3)
                    pe.matmul(bank(4 + i % 4), w2x[:, half, tap, :], tr[:, h * HALF:(h + 1) * HALF],
                              start=True, stop=True).then_inc(s_w, 1)
                    if i % 4 == 3:
                        yield STEP["dyn"] + i // 4 + 1
                yield STEP["L2"] + 1
                group_stats(f * 5 + 4, 4)
                yield STEP["pw"]
                pe.wait_ge(s_h, f * 2 + 2)
                pe.wait_ge(s_pwm, f * 2 + 2)
                for j in range(4):
                    product(4 + j, lambda k: pwm[:, k, j // 2 * P:(j // 2 + 1) * P], half_of(q, j % 2), s_pw)
                    yield STEP["pw"] + j // 2 + 1
                yield STEP["L3"] + 1
                group_stats(f * 5 + 5, 4)
                yield STEP["L3"] + 5
                pe.wait_ge(s_flat, f * 2 + 2)
                for t in range(TILES):
                    for k in range(K):
                        mm = pe.matmul(bank(4 + t // 2, C, t % 2 * C), acc[:, k, t * P:(t + 1) * P],
                                       wt("in_w", k), start=(k == 0), stop=(k == K - 1))
                    if t % 2:
                        mm.then_inc(s_xpr, 1)
                        yield STEP["L3"] + 6 + t // 2
                yield STEP["ln"]
                pe.wait_ge(s_xprs, f * TILES + TILES)
                pe.wait_ge(s_dw3, f * 2 + 2)
                for h in range(2):
                    product(4 + h, lambda k: cst_("mean256"), half_of(q, h), s_mean)
                yield STEP["ln"] + 2
                pe.wait_ge(s_sq, f * 2 + 2)
                for h in range(2):
                    product(4 + h, lambda k: cst_("mean256"), half_of(acc, h), s_lvar)
                yield STEP["om"]
                pe.wait_ge(s_gelu, f * 2 + 2)
                for t in range(TILES):
                    if t >= 4:
                        pe.wait_ge(s_oms, f * TILES + t - 3)
                    for k in range(K):
                        mm = pe.matmul(bank(4 + t % 4, OM), q[:, k, t * P:(t + 1) * P], wt("om_w", k),
                                       start=(k == 0), stop=(k == K - 1))
                    mm.then_inc(s_om, 1)
                    yield STEP["om"] + (t + 1) // 2
                yield STEP["sparse"]
                pe.wait_ge(s_oms, f * TILES + TILES)
                for b in range(4):
                    pe.matmul(bank(4 + b), zeros[:, :], cst[:, 0:512], start=True, stop=False, skip_group_check=True)
                wait_apart(pe, s_runs, f * 2 + 2)
                first = pe.value_load(runs_i[0:1, 0:1], min_val=0, max_val=1 << 20)
                end = pe.value_load(runs_i[0:1, 1:2], min_val=0, max_val=1 << 20)
                with pe.Fori(first, end) as it:
                    for j in range(CH):
                        pe.wait_ge(s_sval, it * CH + j + 1)
                        for b in range(4):
                            mm = pe.matmul(bank(4 + b), ident, placed_at[j][:, b * 512:(b + 1) * 512],
                                           start=False, stop=False, skip_group_check=True)
                        mm.then_inc(s_spsum, 1)
                for b in range(4):
                    mm = pe.matmul(bank(4 + b, 1), ident, zeros[:, 0:1], start=False, stop=True, skip_group_check=True)
                mm.then_inc(s_spend, 1)

            def window(n, u):
                v, w = u + 1, u - 1
                if 0 <= v < TAPS2:
                    at = n * TAPS2 + v
                    if v == 0:
                        wait_apart(pe, s_tap, n * TAPS2)
                    elif v >= 2:
                        pe.wait_ge(s_tap, at - 1)
                    pe.wait_ge(s_prod, at + 1)
                    points = points_of(v)
                    for p in points:
                        mm = pe.matmul(bank(v % 2, PIX), ident, prod[:, v % 3, p, :],
                                       start=(p == points[0]), stop=(p == points[-1]))
                    mm.then_inc(s_wd, 1)
                if 0 <= w < TAPS2 and not VLOW(w):
                    k = count(PLOW, w)
                    if k == 1:
                        wait_apart(pe, s_samp, n * 2)
                    pe.wait_ge(s_tap, n * TAPS2 + w + 1)
                    for b in range(2):
                        mm = pe.matmul(bank(2 + b), ident, tapped[:, w % 2, b * 512:(b + 1) * 512],
                                       start=(k == 1), stop=(k == NPLOW), skip_group_check=True)
                    mm.then_inc(s_psum, 1)

            run(pe, side, window)

        @block.vector
        def _(ve):
            vec = nc.vector
            vec.memset(img[:, :], 0.0).then_inc(s_zero, 1)
            vec.memset(xp[:, :, :, :], 0.0).then_inc(s_zero, 1)
            vec.memset(gat[:, :, :, :], 0.0).then_inc(s_zero, 1)
            vec.memset(rs[:, :], 0.0).then_inc(s_zero, 1)
            vec.memset(zeros[:, :], 0.0).then_inc(s_zero, 1)
            vec.memset(pacc[:, :], 0.0).then_inc(s_zero, 1)
            ve.wait_ge(s_load, 16 * N_LOAD)
            for i, bn in enumerate(("bn1", "bn2")):
                vec.tensor_scalar(col(bn + "_v", 0, K), col(bn + "_v", 0, K), BN_EPS, None, ALU.add)\
                    .then_inc(s_vset, 1)
            vec.tensor_tensor(rows[:, C:C + OM], rows[:, C:C + OM], cst_("grid"), ALU.add).then_inc(s_vset, 1)
            vec.memset(runs[:, :], 0.0).then_inc(s_vset, 1)
            ve.wait_ge(s_gset, 2)
            for i, (bn, bias) in enumerate((("bn1", "dw2_b"), ("bn2", "pw_b"))):
                at = 4 + 4 * i
                vec.tensor_tensor(col(bn + "_g", 0, K), col(bn + "_g", 0, K), col(bn + "_v", 0, K), ALU.mult)\
                    .then_inc(s_vset, 1)
                vec.tensor_tensor(col(bias, 0, K), col(bias, 0, K), col(bn + "_m", 0, K), ALU.subtract)\
                    .then_inc(s_vset, 1)
                ve.wait_ge(s_vset, at + 2)
                vec.tensor_tensor(col(bias, 0, K), col(bias, 0, K), col(bn + "_g", 0, K), ALU.mult)\
                    .then_inc(s_vset, 1)
                ve.wait_ge(s_vset, at + 3)
                vec.tensor_tensor(col(bias, 0, K), col(bias, 0, K), col(bn + "_b", 0, K), ALU.add)\
                    .then_inc(s_vset, 1)
            ve.wait_ge(s_vset, 12)
            ve.wait_ge(s_zero, 6)

            def side(f, m):
                chain = {"k": 0}

                def link(ins, alone=False):
                    chain["k"] += 1
                    ins.then_inc(s_v, 1)
                    if alone:
                        wait_apart(ve, s_v, f * VLINKS + chain["k"])
                    else:
                        ve.wait_ge(s_v, f * VLINKS + chain["k"])

                def moments(src, c, stat, start):
                    for k in range(c):
                        for h in range(2):
                            last = vec.bn_stats(stats[:, k, h, :], src(k, h))
                    link(last, alone=True)
                    for k in range(c):
                        last = vec.bn_aggr(small[:, 2 * k:2 * k + 2], stats[:, k, :, :].rearrange("p a b -> p (a b)"))
                    link(last)
                    mean, var = small[:, 0:2 * c:2], small[:, 1:2 * c:2]
                    link(vec.tensor_tensor(small[:, 8:8 + c], mean, mean, ALU.mult))
                    vec.tensor_tensor(var, var, small[:, 8:8 + c], ALU.add).then_inc(s_gstat, 1)
                    yield start + 2
                    ve.wait_ge(s_gsum, stat)
                    link(vec.tensor_copy(small[:, 12:12 + 2 * c], bank(7, 2 * c)))
                    mean, msq = small[:, 12:12 + 2 * c:2], small[:, 13:12 + 2 * c:2]
                    vec.tensor_scalar(small[:, 52:52 + c], mean, -1.0, None, ALU.mult)
                    link(vec.tensor_tensor(small[:, 20:20 + c], mean, mean, ALU.mult))
                    link(vec.tensor_tensor(small[:, 24:24 + c], msq, small[:, 20:20 + c], ALU.subtract))
                    vec.tensor_scalar(small[:, 24:24 + c], small[:, 24:24 + c], GN_EPS, None, ALU.add)\
                        .then_inc(s_var, 1)

                def group_norm(stat, start):
                    yield from moments(lambda k, h: x[:, k, h * HALF:(h + 1) * HALF], K, stat, start)

                def depthwise(dst, w, start, before):
                    ve.wait_ge(s_dw0, before + 2)
                    for tap in range(1, TAPS):
                        for k in range(K):
                            o = dst[:, k, :].rearrange("p (h w) -> p h w", h=H)
                            last = vec.scalar_tensor_tensor(out=o, in0=shifted(xp, k, tap // 3, tap % 3),
                                                            scalar=col(w, k * TAPS + tap), in1=o,
                                                            op0=ALU.mult, op1=ALU.add)
                            if tap == TAPS - 1:
                                last.then_inc(s_dw if w == "dw2" else s_dw3, 1)
                            else:
                                link(last)
                        if tap % 2 == 0:
                            yield start + tap // 2

                if f is not None:
                    yield STEP["gn0"]
                    ve.wait_ge(s_x, f * 16 + 16)
                    yield from group_norm(f * 5 + 1, STEP["gn0"])
                if m is not None:
                    yield STEP["finish"]
                    ve.wait_ge(s_back, (m + 1) * 16 * N_BACK)
                    vec.tensor_tensor(bigf, bigf, work[:, 0:K * N], ALU.add).then_inc(s_mixed, 1)
                    for j in range(4):
                        yield STEP["finish"] + 4 + j // 2
                        ve.wait_ge(s_fin, m * 4 + j + 1)
                        o = res[:, j // 2, j % 2 * HALF:(j % 2 + 1) * HALF]
                        last = vec.scalar_tensor_tensor(out=o, in0=bank(4 + j), scalar=col("out_b", j // 2),
                                                        in1=o, op0=ALU.add, op1=ALU.add)
                    last.then_inc(s_xdone, 1)
                if f is None:
                    return
                yield STEP["L0"] + 10
                ve.wait_ge(s_sc, f + 1)
                vec.tensor_reduce(small[:, 32:34], bank(4).rearrange("p (m d) -> p m d", m=K), AX.X, ALU.max,
                                  negate=True).then_inc(s_mx, 1)
                yield STEP["L0"] + 12
                ve.wait_ge(s_e, f * 2 + 2)
                link(vec.reciprocal(small[:, 36:38], small[:, 34:36]))
                for j in range(4):
                    yield STEP["L0"] + 14 + j // 2
                    ve.wait_ge(s_att, f * 4 + j + 1)
                    o = x[:, j // 2, j % 2 * HALF:(j % 2 + 1) * HALF]
                    last = vec.scalar_tensor_tensor(out=o, in0=bank(4 + j), scalar=small[:, 36 + j // 2:37 + j // 2],
                                                    in1=o, op0=ALU.mult, op1=ALU.add)
                last.then_inc(s_x1, 1)
                ve.wait_ge(s_x1, f + 1)
                yield STEP["L1"]
                yield from group_norm(f * 5 + 2, STEP["L1"])
                yield STEP["L1"] + 5
                ve.wait_ge(s_t1, f * 2 + 2)
                yield from moments(lambda k, h: bank(4 + h), 1, f * 5 + 3, STEP["L1"] + 5)
                yield STEP["L1"] + 8
                ve.wait_ge(s_rstd, f * 9 + 5)
                link(vec.tensor_tensor(small[:, 40:41], col("t_gamma"), small[:, 28:29], ALU.mult))
                link(vec.tensor_tensor(small[:, 42:43], small[:, 12:13], small[:, 40:41], ALU.mult))
                vec.tensor_tensor(small[:, 41:42], col("t_beta"), small[:, 42:43], ALU.subtract).then_inc(s_tsc, 1)
                yield STEP["dyn"]
                ve.wait_ge(s_xvz, f + 1)
                ve.wait_ge(s_xvs, f * 4 + 4)
                for i in range(K * TAPS * 2):
                    half, tap, h = i // (2 * TAPS), i // 2 % TAPS, i % 2
                    if i % 4 == 0:
                        yield STEP["dyn"] + i // 4 + 1
                    if i >= 2:
                        ve.wait_ge(s_v, f * VLINKS + chain["k"])
                    ve.wait_ge(s_w, f * 2 * K * TAPS + i + 1)
                    o = acc[:, half, h * HALF:(h + 1) * HALF]
                    t = o if tap == 0 else tmp[:, h, :]
                    vec.scalar_tensor_tensor(
                        out=t.rearrange("p (h w) -> p h w", w=W), in0=bank(4 + i % 4).rearrange("p (h w) -> p h w", w=W),
                        scalar=col("b2", half * TAPS + tap), in1=shifted(xvp, half, tap // 3, tap % 3, h * HR, HR),
                        op0=ALU.add, op1=ALU.mult).then_inc(s_wu, 1)
                    if h == 1 and tap > 0:
                        ve.wait_ge(s_wu, f * 2 * K * TAPS + i + 1)
                        o = acc[:, half, :]
                        chain["k"] += 1
                        vec.tensor_tensor(o, o, work[:, 3 * N:4 * N], ALU.add).then_inc(s_v, 1)
                yield STEP["dyn"] + 10
                ve.wait_ge(s_v, f * VLINKS + chain["k"])
                link(vec.tensor_tensor(xflat, xflat, work[:, 0:K * N], ALU.add))
                yield STEP["L2"]
                yield from group_norm(f * 5 + 4, STEP["L2"])
                yield STEP["L2"] + 4
                yield from depthwise(acc, "dw2", STEP["L2"] + 4, f * 4)
                yield STEP["pw"] - 1
                ve.wait_ge(s_h, f * 2 + 2)
                for k in range(K):
                    last = vec.tensor_reduce(small[:, 44 + k:45 + k], q[:, k, :], AX.X, ALU.max)
                link(last)
                link(vec.tensor_scalar(small[:, 46:48], small[:, 44:46], DW_THRESH, None, ALU.is_ge))
                for k in range(K):
                    vec.tensor_scalar(pwm[:, k, :], wt("pw", k), small[:, 46 + k:47 + k], None, ALU.mult)\
                        .then_inc(s_pwm, 1)
                yield STEP["pw"] + 3
                ve.wait_ge(s_h2, f * 4 + 4)
                for k in range(K):
                    last = vec.tensor_reduce(small[:, 48 + k:49 + k], acc[:, k, :], AX.X, ALU.max)
                link(last)
                link(vec.tensor_scalar(small[:, 50:52], small[:, 48:50], PW_THRESH, None, ALU.is_ge))
                for k in range(K):
                    last = vec.scalar_tensor_tensor(out=x[:, k, :], in0=acc[:, k, :], scalar=small[:, 50 + k:51 + k],
                                                    in1=x[:, k, :], op0=ALU.mult, op1=ALU.add)
                last.then_inc(s_xmid, 1)
                ve.wait_ge(s_xmid, f + 1)
                yield STEP["L3"]
                yield from group_norm(f * 5 + 5, STEP["L3"])
                yield STEP["L3"] + 4
                yield from depthwise(q, "dw3", STEP["L3"] + 4, f * 4 + 2)
                for t in range(TILES):
                    if t % 4 == 0:
                        yield STEP["L3"] + 8 + t // 4
                    if t % 2 == 0:
                        ve.wait_ge(s_xpr, f * 4 + t // 2 + 1)
                    vec.tensor_tensor(big[:, t, :], bank(4 + t // 2, C, t % 2 * C), rows[:, 0:C], ALU.add)\
                        .then_inc(s_xprs, 1)
                yield STEP["ln"] + 1
                ve.wait_ge(s_mean, f * 2 + 2)
                for k in range(K):
                    for h in range(2):
                        o = q[:, k, h * HALF:(h + 1) * HALF]
                        last = vec.tensor_tensor(o, o, bank(4 + h), ALU.subtract)
                    last.then_inc(s_cent, 1)
                yield STEP["ln"] + 4
                ve.wait_ge(s_sd, f * 2 + 2)
                link(vec.reciprocal(tr, tr))
                for k in range(K):
                    vec.tensor_tensor(q[:, k, :], q[:, k, :], tr, ALU.mult).then_inc(s_xhat, 1)
                for t in range(TILES):
                    yield STEP["om"] + (t + 1) // 2
                    ve.wait_ge(s_om, f * TILES + t + 1)
                    vec.tensor_tensor(om[:, t, :], bank(4 + t % 4, OM), rows[:, C:C + OM], ALU.add).then_inc(s_oms, 1)
                yield STEP["om"] + 5
                ve.wait_ge(s_oms, f * TILES + TILES)
                planes = om.rearrange("p t (g c m) -> p (t g) c m", g=G, c=3)
                tx, ty, mask = planes[:, :, 0, :], planes[:, :, 1, :], planes[:, :, 2, :]
                wide = red[:, :].rearrange("p (a o) -> p a o", o=1).broadcast_to([P, TILES * G, TAPS])
                link(vec.tensor_reduce(red[:, :], mask, AX.X, ALU.max))
                vec.tensor_tensor(mask, mask, wide, ALU.subtract).then_inc(s_msub, 1)
                by_tg = lambda ap: ap.rearrange("p (a m) -> p a m", m=TAPS)
                f3, m3, k3 = by_tg(flag), by_tg(mout[:, :]), by_tg(keys[:, :])
                yield STEP["om"] + 6
                ve.wait_ge(s_mexp, f + 1)
                link(vec.tensor_reduce(red[:, :], mask, AX.X, ALU.add))
                link(vec.reciprocal(red[:, :], red[:, :]))
                link(vec.tensor_tensor(mask, mask, wide, ALU.mult))
                yield STEP["om"] + 7
                ve.wait_ge(s_abs, f * 4 + 4)
                far = beyond[:, :, 0, :]
                link(vec.tensor_tensor(m3, m3, k3, ALU.min))
                ve.wait_ge(s_far, f * 2 + 2)
                link(vec.tensor_tensor(far, far, beyond[:, :, 1, :], ALU.max))
                link(vec.scalar_tensor_tensor(out=k3, in0=m3, scalar=float(1 - R), in1=far, op0=ALU.add, op1=ALU.max))
                vec.tensor_scalar(f3, k3, 0.0, None, ALU.is_gt).then_inc(s_flag, 1)
                ve.wait_ge(s_flag, f + 1)
                link(vec.tensor_tensor(m3, mask, f3, ALU.mult))
                vec.tensor_tensor(mask, mask, m3, ALU.subtract).then_inc(s_omr, 1)
                yield STEP["sparse"]
                link(vec.tensor_tensor(k3, cst_("code").rearrange("p (a o) -> p a o", o=1).broadcast_to(
                    [P, TILES * G, TAPS]), cst_("tap_code").rearrange("p (o m) -> p o m", o=1).broadcast_to(
                        [P, TILES * G, TAPS]), ALU.add))
                link(vec.tensor_tensor(k3, k3, f3, ALU.mult))
                ve.wait_ge(s_cntr, f + 1)
                link(vec.tensor_scalar(runs[:, 1:2], runs[:, 1:2], 1 / CH, 1 - 1 / (2 * CH), ALU.mult, ALU.add))
                link(vec.tensor_copy(fli[:, 0:1], runs[:, 1:2]))
                link(vec.tensor_copy(runs[:, 3:4], fli[:, 0:1]))
                link(vec.tensor_tensor(runs[:, 4:5], runs[:, 3:4], runs[:, 1:2], ALU.is_gt))
                link(vec.tensor_tensor(runs[:, 1:2], runs[:, 3:4], runs[:, 4:5], ALU.subtract))
                link(vec.tensor_scalar(runs[:, 1:2], runs[:, 1:2], 1.0, None, ALU.max))
                link(vec.tensor_tensor(runs[:, 1:2], runs[:, 2:3], runs[:, 1:2], ALU.add))
                vec.tensor_copy(runs_i[0:1, 0:1], runs[0:1, 2:3]).then_inc(s_runs, 1)
                vec.tensor_copy(runs_i[0:1, 1:2], runs[0:1, 1:2]).then_inc(s_runs, 1)
                ve.wait_ge(s_runs, f * 2 + 2)
                link(vec.tensor_copy(runs[:, 2:3], runs[:, 1:2]), alone=True)
                first = ve.value_load(runs_i[0:1, 0:1], min_val=0, max_val=1 << 20)
                end = ve.value_load(runs_i[0:1, 1:2], min_val=0, max_val=1 << 20)
                cells_of = lambda at, n: rs[:, at:at + n * CH].rearrange("p (c j) -> p c j", j=CH)
                top, key = rs[:, 0:8], rs[:, 0:CH]
                sel, pos, flr, up = cells_of(8, 5), cells_of(28, 2), cells_of(36, 2), cells_of(44, 2)
                lin, fx, my, w4 = rs[:, 52:56], cells_of(56, 2), cells_of(64, 2), cells_of(72, 4)
                val = rs[:, 88:152].rearrange("p (j c) -> p j c", c=CG)
                shifted_code, tgcode = rs[:, 152:156], rs[:, 156:160]

                def floor(dst, src, integer, larger, then):
                    then(vec.tensor_copy(integer, src))
                    then(vec.tensor_copy(dst, integer))
                    then(vec.tensor_tensor(larger, dst, src, ALU.is_gt))
                    then(vec.tensor_tensor(dst, dst, larger, ALU.subtract))

                def select(then):
                    then(vec.max(out=top, in_=keys[:, :]))
                    then(vec.tensor_scalar(key, key, 0.5, None, ALU.max))
                    then(vec.tensor_scalar(shifted_code, key, 1 / TAPS, (TAPS // 2) / TAPS + 0.5, ALU.mult, ALU.add))
                    floor(tgcode, shifted_code, fli[:, 0:CH], up[:, 0, :], then)
                    for j in range(CH):
                        last = vec.tensor_scalar(tg[:, j, :], cst_("tg_code"), tgcode[:, j:j + 1], None, ALU.is_equal)
                    then(last)
                    for j in range(CH):
                        for c, table in enumerate((tx, ty, m3)):
                            then(vec.scalar_tensor_tensor(out=by_tg(junk), in0=k3, scalar=key[:, j:j + 1], in1=table,
                                                          op0=ALU.is_equal, op1=ALU.mult, accum_out=sel[:, c, j:j + 1]))
                        for c, table in enumerate(("group_of", "row_of")):
                            then(vec.scalar_tensor_tensor(out=junk[:, 0:TILES * G], in0=tg[:, j, :], scalar=1.0,
                                                          in1=cst_(table), op0=ALU.mult, op1=ALU.mult,
                                                          accum_out=sel[:, 3 + c, j:j + 1]))
                    vec.tensor_scalar(pos[:, 0, :], sel[:, 0, :], cst_("pixel_xy")[:, 0:1], None, ALU.add)
                    then(vec.scalar_tensor_tensor(out=pos[:, 1, :], in0=sel[:, 1, :], scalar=cst_("pixel_xy")[:, 1:2],
                                                  in1=sel[:, 4, :], op0=ALU.add, op1=ALU.add))
                    then(vec.tensor_scalar(pos, pos, -2.0, float(H), ALU.max, ALU.min))
                    floor(flr, pos, fli[:, :].rearrange("p (c j) -> p c j", j=CH), up, then)
                    then(vec.scalar_tensor_tensor(out=lin, in0=flr[:, 1, :], scalar=float(PADW), in1=flr[:, 0, :],
                                                  op0=ALU.mult, op1=ALU.add))
                    then(vec.scalar_tensor_tensor(out=lin, in0=sel[:, 3, :], scalar=float(PADH * PADW), in1=lin,
                                                  op0=ALU.mult, op1=ALU.add))

                def ask():
                    for yk in range(2):
                        last = vec.tensor_scalar(idx[:, yk, :], lin, float(CG), float(((R + yk) * PADW + R) * CG), ALU.mult, ALU.add)
                    last.then_inc(s_idx, 1)

                def weights(then):
                    then(vec.tensor_tensor(up, pos, flr, ALU.subtract))
                    vec.tensor_copy(fx[:, 1, :], up[:, 0, :])
                    vec.tensor_scalar(fx[:, 0, :], up[:, 0, :], -1.0, 1.0, ALU.mult, ALU.add)
                    vec.tensor_tensor(my[:, 1, :], up[:, 1, :], sel[:, 2, :], ALU.mult)
                    then(vec.tensor_scalar(my[:, 0, :], up[:, 1, :], -1.0, 1.0, ALU.mult, ALU.add))
                    then(vec.tensor_tensor(my[:, 0, :], my[:, 0, :], sel[:, 2, :], ALU.mult))
                    for yk in range(2):
                        last = vec.tensor_tensor(w4[:, 2 * yk:2 * yk + 2, :], my[:, yk:yk + 1, :].broadcast_to([P, 2, CH]),
                                                 fx, ALU.mult)
                    then(last)

                def weigh(then):
                    for yk in range(2):
                        g = gat[:, :, yk, :].rearrange("p j (x c) -> p j x c", c=CG)
                        last = vec.tensor_tensor(g, g, w4[:, 2 * yk:2 * yk + 2, :].rearrange("p x (j o) -> p j x o", o=1)
                                                 .broadcast_to([P, CH, 2, CG]), ALU.mult)
                    then(last)
                    then(vec.tensor_reduce(val, gat[:, :, :, :].rearrange("p j y (x c) -> p j c (y x)", c=CG), AX.X, ALU.add))

                def place(it):
                    for j in range(CH):
                        ve.wait_ge(s_spsum, it * CH + CH + max(0, j - 2))
                        vec.tensor_tensor(placed_at[j].rearrange("p (a c) -> p a c", c=CG),
                                          tg[:, j, :].rearrange("p (a o) -> p a o", o=1).broadcast_to([P, TILES * G, CG]),
                                          val[:, j:j + 1, :].broadcast_to([P, TILES * G, CG]), ALU.mult).then_inc(s_sval, 1)

                def links_of(semaphore, passes, per):
                    k = [0]

                    def then(ins):
                        k[0] += 1
                        ins.then_inc(semaphore, 1)
                        ve.wait_ge(semaphore, passes * per + k[0])
                    return then

                ve.wait_ge(s_imgw, (f + 1) * 16 * TILES * TR)
                link(vec.tensor_copy(small[:, 60:61], runs[:, 1:2]), alone=True)
                with ve.Fori(first, end) as it:
                    then = links_of(s_rv, it, RLINKS)
                    select(then)
                    ask()
                    vec.scalar_tensor_tensor(out=keys[:, :], in0=keys[:, :], scalar=key[:, CH - 1:CH], in1=keys[:, :],
                                             op0=ALU.is_lt, op1=ALU.mult)
                    weights(then)
                    ve.wait_ge(s_gd, it + 1)
                    weigh(links_of(s_wg, it, 2))
                    place(it)
                    ve.wait_ge(s_sval, it * CH + CH)
                    vec.memset(small[0:1, 62:63], 0.0)
                assert chain["k"] == VLINKS, chain

            def window(n, u):
                at, w = n * TAPS2 + u, u - 1
                if u == -1:
                    ve.wait_ge(s_spend, n + 1)
                    ve.wait_ge(s_az, (n + 1) * 2)
                    ve.wait_ge(s_img, (n + 1) * 16 * G)
                    vec.memset(small[0:1, 61:62], 0.0)
                if 0 <= u < TAPS2:
                    dy, d = TAP[u]
                    if u >= 2:
                        for semaphore, whose, total in ((s_psum, PLOW, NPLOW), (s_vacc, VSUM, NVSUM), (s_pacc, PUP, NPUP)):
                            if whose(u - 2):
                                ve.wait_ge(semaphore, n * total + count(whose, u - 2))
                    ve.wait_ge(s_wd, at + 1)
                    wtap = bank(u % 2, PIX).rearrange("p (r x o) -> p r x o", r=TR, o=1).broadcast_to([P, TR, W, CG])
                    src = img[:, :].rearrange("p (y x) -> p y x", y=IMGR)[:, dy:dy + TR, d * CG:(d + W) * CG]\
                        .rearrange("p r (x c) -> p r x c", c=CG)
                    dst = tapped[:, u % 2, :].rearrange("p (r x c) -> p r x c", r=TR, c=CG)
                    vec.tensor_tensor(dst, wtap, src, ALU.mult).then_inc(s_tap, 1)
                if 0 <= w < TAPS2 and VSUM(w):
                    ve.wait_ge(s_tap, n * TAPS2 + w + 1)
                    if count(VSUM, w) > 1:
                        ve.wait_ge(s_vacc, n * NVSUM + count(VSUM, w) - 1)
                    a, z = 0 if VLOW(w) else UP, PIX * CG if VUP(w) else UP
                    vec.tensor_tensor(samp[:, a:z], samp[:, a:z], tapped[:, w % 2, a:z], ALU.add).then_inc(s_vacc, 1)
                if u == TAPS2 + 1:
                    ve.wait_ge(s_vacc, (n + 1) * NVSUM)
                    ve.wait_ge(s_psum, (n + 1) * NPLOW)
                    vec.tensor_tensor(samp[:, 0:UP], samp[:, 0:UP], ps[:, 2:4, :].rearrange("p b n -> p (b n)"), ALU.add)\
                        .then_inc(s_samp, 1)
                    ve.wait_ge(s_pacc, (n + 1) * NPUP)
                    vec.tensor_tensor(samp[:, UP:], samp[:, UP:], pacc[:, :], ALU.add).then_inc(s_samp, 1)

            run(ve, side, window)

        @block.scalar
        def _(ac):
            act = nc.scalar
            ac.wait_ge(s_load, 16 * N_LOAD)
            ac.wait_ge(s_vset, 12)

            def side(f, m):
                def group_norm(i, start):
                    yield start + 3
                    ac.wait_ge(s_rstd, f * 9 + (2, 4, 7, 9)[i])
                    for k in range(K):
                        last = act.activation(xp[:, k, 1:1 + H, 1:1 + W], x[:, k, :].rearrange("p (h w) -> p h w", h=H),
                                              ACT.Identity, bias=small[:, 54 + k:55 + k], scale=small[:, 28 + k:29 + k])
                    last.then_inc(s_norm, 1)

                def first_tap(dst, w, bias, i):
                    ac.wait_ge(s_norm, f * 4 + i)
                    for k in range(K):
                        act.activation(dst[:, k, :].rearrange("p (h w) -> p h w", h=H), shifted(xp, k, 0, 0), ACT.Identity,
                                       bias=0.0 if bias is None else col(bias, k), scale=col(w, k * TAPS)).then_inc(s_dw0, 1)

                if f is not None:
                    yield from group_norm(0, STEP["gn0"] - 1)
                if m is not None:
                    yield STEP["finish"] + 2
                    for j in range(4):
                        ac.wait_ge(s_oT, m * 2 + j // 2 + 1)
                        act.activation(q[:, j // 2, j % 2 * HALF:(j % 2 + 1) * HALF], bank(4 + j), ACT.Copy)\
                            .then_inc(s_oTs, 1)
                if f is None:
                    return
                for j in range(4):
                    yield STEP["L0"] + 1 + j
                    ac.wait_ge(s_q, f * 4 + j + 1)
                    act.activation(q[:, j // 2, j % 2 * HALF:(j % 2 + 1) * HALF], bank(4 + j), ACT.Identity,
                                   bias=col("q_bias", j // 2)).then_inc(s_qs, 1)
                yield STEP["L0"] + 5
                wait(ac, s_spbw, f * 16)
                wait(ac, s_omw, f * 16 * TILES)
                for j in range(4):
                    ac.wait_ge(s_qt, f * 4 + j + 1)
                    act.activation(qT[:, 2 * j:2 * j + 2, :].rearrange("p t c -> p (t c)"), bank(4 + j), ACT.Copy)\
                        .then_inc(s_qta, 1)
                yield STEP["L0"] + 10
                if m is not None:
                    ac.wait_ge(s_stored, (m + 1) * 16)
                ac.wait_ge(s_mx, f + 1)
                for k in range(K):
                    act.activation(e[:, k, :], bank(4, C, k * C), ACT.Exp, bias=small[:, 32 + k:33 + k],
                                   accum_out=small[:, 34 + k:35 + k]).then_inc(s_e, 1)
                yield STEP["L0"] + 12
                ac.wait_ge(s_et, f + 1)
                act.activation(et[:, :, :].rearrange("p k n -> p (k n)"), bank(5), ACT.Copy).then_inc(s_ets, 1)
                yield from group_norm(1, STEP["L1"])
                yield STEP["L1"] + 6
                ac.wait_ge(s_xvz, f + 1)

                def keep_xv(j, b):
                    ac.wait_ge(s_xv, f * 4 + j + 1)
                    act.activation(rows_of(xvp, j // 2, j % 2), bank(b).rearrange("p (h w) -> p h w", w=W),
                                   ACT.Copy).then_inc(s_xvs, 1)

                keep_xv(0, 6)
                keep_xv(1, 7)
                yield STEP["L1"] + 7
                keep_xv(2, 6)
                yield STEP["L1"] + 8
                ac.wait_ge(s_tsc, f + 1)
                act.activation(tr, ps[:, 4:6, :].rearrange("p b n -> p (b n)"), ACT.Relu, bias=small[:, 41:42],
                               scale=small[:, 40:41]).then_inc(s_tr, 1)
                yield STEP["dyn"]
                keep_xv(3, 4)
                yield from group_norm(2, STEP["L2"])
                first_tap(acc, "dw2", None, 3)
                yield STEP["pw"] - 2
                for k in range(K):
                    ac.wait_ge(s_dw, f * 2 + k + 1)
                    act.activation(q[:, k, :], acc[:, k, :], ACT.Relu, bias=col("dw2_b", k), scale=col("bn1_g", k))\
                        .then_inc(s_h, 1)
                for j in range(4):
                    yield STEP["pw"] + 1 + j // 2
                    ac.wait_ge(s_pw, f * 4 + j + 1)
                    act.activation(acc[:, j // 2, j % 2 * HALF:(j % 2 + 1) * HALF], bank(4 + j), ACT.Relu,
                                   bias=col("pw_b", j // 2), scale=col("bn2_g", j // 2)).then_inc(s_h2, 1)
                yield from group_norm(3, STEP["L3"])
                first_tap(q, "dw3", "dw3_b", 4)
                for k in range(K):
                    act.activation(acc[:, k, :].rearrange("p (h w) -> p h w", h=H), xp[:, k, 1:1 + H, 1:1 + W], ACT.Copy)\
                        .then_inc(s_flat, 1)
                yield STEP["ln"] + 1
                ac.wait_ge(s_xpr, f * 4 + 4)
                for k in range(K):
                    ac.wait_ge(s_cent, f * 2 + k + 1)
                    act.activation(acc[:, k, :], q[:, k, :], ACT.Square).then_inc(s_sq, 1)
                yield STEP["ln"] + 3
                for h in range(2):
                    ac.wait_ge(s_lvar, f * 2 + h + 1)
                    act.activation(tr[:, h * HALF:(h + 1) * HALF], bank(4 + h), ACT.Sqrt, bias=cst_("eps"))\
                        .then_inc(s_sd, 1)
                yield STEP["ln"] + 4
                for k in range(K):
                    ac.wait_ge(s_xhat, f * 2 + k + 1)
                    act.activation(q[:, k, :], q[:, k, :], ACT.Gelu, bias=col("ln_b", k), scale=col("ln_g", k))\
                        .then_inc(s_gelu, 1)
                yield STEP["om"] + 6
                ac.wait_ge(s_msub, f + 1)
                mask = om.rearrange("p t (g c m) -> p (t g) c m", g=G, c=3)[:, :, 2, :]
                act.activation(mask, mask, ACT.Exp).then_inc(s_mexp, 1)
                ac.wait_ge(s_ctr, f * 2 + 2)
                planes = om.rearrange("p t (g c m) -> p (t g) c m", g=G, c=3)
                for c, o in enumerate((mout, keys)):
                    act.activation(beyond[:, :, c, :], beyond[:, :, c, :], ACT.Abs).then_inc(s_abs, 1)
                    act.activation(o[:, :].rearrange("p (a m) -> p a m", m=TAPS), planes[:, :, c, :], ACT.Abs)\
                        .then_inc(s_abs, 1)
                yield STEP["om"] + 7
                ac.wait_ge(s_flag, f + 1)
                act.activation(junk, flag, ACT.Copy, accum_out=runs[:, 0:1]).then_inc(s_cnt, 1)

            def window(n, u):
                v = u + 3
                if v >= TAPS2:
                    return
                dy, d = TAP[v]
                hats = TAPS2 + D
                first = v == 0 or TAP[v - 1][0] != dy
                xs, ys = span(d - R), span(dy - R)
                of = lambda ap, a: ap.rearrange("p (i j) n -> p i j n", j=3)[:, a, ys]
                tv = tb[:, :, :].rearrange("p n (c m) -> p c m n", c=3)
                k = n * hats + v + dy
                if first:
                    every = slice(0, 3)
                    o = of(haty[:, dy % 2], every)
                    if v == 0:
                        ac.wait_ge(s_tb, (n + 1) * 16)
                    elif dy >= 2:
                        ac.wait_ge(s_wyd, n * D + dy - 1)
                    act.activation(o, of(tv[:, 1], every), ACT.Abs, bias=cst_("minus_d")[:, dy:dy + 1]).then_inc(s_a, 1)
                    ac.wait_ge(s_a, k + 1)
                    act.activation(o, o, ACT.Relu, bias=1.0, scale=-1.0).then_inc(s_hy, 1)
                if v >= 3:
                    ac.wait_ge(s_prod, n * TAPS2 + v - 2)
                o = of(hatx[:, v % 3], xs)
                act.activation(o, of(tv[:, 0], xs), ACT.Abs, bias=cst_("minus_d")[:, d:d + 1]).then_inc(s_a, 1)
                ac.wait_ge(s_a, k + 2)
                act.activation(o, o, ACT.Relu, bias=1.0, scale=-1.0).then_inc(s_hx, 1)
                if u == -1:
                    ac.wait_ge(s_spend, n + 1)
                    act.activation(bigf, ps[:, 4:8, :].rearrange("p b n -> p (b n)"), ACT.Copy).then_inc(s_spb, 1)

            run(ac, side, window)

        @block.gpsimd
        def _(po):
            pool = nc.gpsimd
            po.wait_ge(s_vset, 2)
            po.wait_ge(s_load, 16 * N_LOAD)
            for bn in ("bn1", "bn2"):
                pool.tensor_tensor(col(bn + "_v", 0, K), col(bn + "_v", 0, K), cst_("half")[:, 0:K], ALU.pow)\
                    .then_inc(s_gset, 1)
            po.wait_ge(s_vset, 12)
            def side(f, m):
                if f is None:
                    return

                def rstd(stat, c):
                    done = f * 9 + {1: 0, 2: 2, 3: 4, 4: 5, 5: 7}[stat]
                    po.wait_ge(s_var, f * 5 + stat)
                    pool.tensor_tensor(small[:, 28:28 + c], small[:, 24:24 + c], cst_("half")[:, 0:c], ALU.pow)\
                        .then_inc(s_rstd, 1)
                    if stat != 3:
                        po.wait_ge(s_rstd, done + 1)
                        pool.tensor_tensor(small[:, 54:54 + c], small[:, 52:52 + c], small[:, 28:28 + c], ALU.mult)\
                            .then_inc(s_rstd, 1)

                yield STEP["gn0"] + 2
                rstd(1, K)
                yield STEP["L1"]
                wait_apart(po, s_x1, f + 1)
                pool.memset(qx[:, :], 0.0).then_inc(s_xvz, 1)
                yield STEP["L1"] + 2
                rstd(2, K)
                yield STEP["L1"] + 7
                rstd(3, 1)
                yield STEP["L2"] + 2
                rstd(4, K)
                yield STEP["L3"] + 2
                rstd(5, K)
                yield STEP["om"] + 5
                xy = om.rearrange("p t (g c m) -> p (t g) c m", g=G, c=3)
                by_point = lambda name, c: cst_(name)[:, c * TAPS:(c + 1) * TAPS].rearrange("p (o m) -> p o m", o=1)\
                    .broadcast_to([P, TILES * G, TAPS])
                wait_apart(po, s_oms, f * TILES + TILES)
                for c in range(2):
                    pool.tensor_tensor(beyond[:, :, c, :], xy[:, :, c, :], by_point("middle", c), ALU.subtract)\
                        .then_inc(s_ctr, 1)
                yield STEP["om"] + 6
                wait_apart(po, s_abs, f * 4 + 4)
                for c in range(2):
                    o = beyond[:, :, c, :]
                    pool.tensor_tensor(o, o, by_point("reach", c), ALU.subtract).then_inc(s_far, 1)
                yield STEP["sparse"] - 1
                wait_apart(po, s_cnt, f + 1)
                pool.partition_all_reduce(runs[:, 1:2], runs[:, 0:1], P, bass.bass_isa.ReduceOp.max).then_inc(s_cntr, 1)
                yield STEP["sparse"]
                wait_apart(po, s_imgw, (f + 1) * 16 * TILES * TR)
                wait_apart(po, s_runs, f * 2 + 2)
                first = po.value_load(runs_i[0:1, 0:1], min_val=0, max_val=1 << 20)
                end = po.value_load(runs_i[0:1, 1:2], min_val=0, max_val=1 << 20)
                with po.Fori(first, end) as it:
                    wait_apart(po, s_idx, it + 1)
                    pairs = img_dram.rearrange("n (c o) -> (n c) o", o=1)
                    for j in range(CH):
                        for yk in range(2):
                            pool.indirect_dma_start(
                                out=gat[:, j, yk, :], out_offset=None, in_=pairs,
                                in_offset=bass.IndirectOffsetOnAxis(ap=idx[:, yk, j:j + 1], axis=0)).then_inc(s_gat, 16)
                    po.wait_ge(s_gat, 16 * 2 * CH)
                    pool.memset(pdone[:, :], 0.0).then_inc(s_gd, 1)
                    po.inc_swdge_sem([s_gat], [16 * 2 * CH], mode="sub")
                    po.wait_ge(s_gd, it + 1)

            def window(n, u):
                v, w = u + 2, u - 1
                if u == -LEAD:
                    wait_apart(po, s_samp, n * 2)
                    pool.memset(pacc[:, :], 0.0).then_inc(s_az, 1)
                    wait_apart(po, s_sampw, n * 16)
                    pool.memset(samp[:, :], 0.0).then_inc(s_az, 1)
                if 0 <= v < TAPS2:
                    dy, d = TAP[v]
                    at = n * TAPS2 + v
                    xs, ys = span(d - R), span(dy - R)
                    of = lambda ap, a: ap.rearrange("p (i j) n -> p i j n", j=3)[:, a, ys]
                    if v == 0 or TAP[v - 1][0] != dy:
                        every = slice(0, 3)
                        po.wait_ge(s_hy, n * D + dy + 1)
                        if v > 0:
                            po.wait_ge(s_prod, at)
                        mk = tb[:, :, :].rearrange("p n (c m) -> p c m n", c=3)[:, 2]
                        pool.tensor_tensor(of(wy[:, :, :], every), of(haty[:, dy % 2], every), of(mk, every), ALU.mult).then_inc(s_wyd, 1)
                        po.wait_ge(s_wyd, n * D + dy + 1)
                    po.wait_ge(s_hx, at + 1)
                    if v >= 3:
                        po.wait_ge(s_wd, at - 2)
                    pool.tensor_tensor(of(prod[:, v % 3], xs), of(wy[:, :, :], xs), of(hatx[:, v % 3], xs), ALU.mult).then_inc(s_prod, 1)
                if 0 <= w < TAPS2 and PUP(w):
                    k = n * NPUP + count(PUP, w)
                    po.wait_ge(s_tap, n * TAPS2 + w + 1)
                    if count(PUP, w) == 1:
                        po.wait_ge(s_az, n * 2 + 2)
                    else:
                        po.wait_ge(s_pacc, k - 1)
                    pool.tensor_tensor(pacc[:, :], pacc[:, :], tapped[:, w % 2, UP:], ALU.add).then_inc(s_pacc, 1)

            run(po, side, window)


VLINKS = 102
RLINKS = 40


def span(d):
    near = [g for g in range(3) if max(-R, g - 1 - REACH) <= d <= min(R, g - 1 + REACH)]
    return slice(near[0], near[-1] + 1)


def points_of(u):
    dy, d = TAP[u]
    return [i * 3 + j for i in range(3)[span(d - R)] for j in range(3)[span(dy - R)]]


def heavy(u):
    return any(tap_of(a) <= u < tap_of(z) for a, z in (
        (STEP["dyn"] + 1, STEP["L2"] - 1), (STEP["L2"] + 4, STEP["L2"] + 8), (STEP["L3"] + 4, STEP["L3"] + 8)))


def VLOW(u):
    return u % 2 == 1 and not heavy(u)


def VUP(u):
    return u % 2 == 0 and not heavy(u)


def PLOW(u):
    return not VLOW(u)


def PUP(u):
    return not VUP(u)


def VSUM(u):
    return VLOW(u) or VUP(u)


def count(whose, u):
    return sum(bool(whose(i)) for i in range(u + 1))


NPLOW, NPUP, NVSUM = (count(whose, TAPS2 - 1) for whose in (PLOW, PUP, VSUM))


def consts():
    out = np.zeros((P, NCST), np.float32)

    def put(name, value):
        a, n = CST[name]
        out[:, a:a + n] = value

    put("ident", np.eye(P))
    put("group8", np.kron(np.eye(P // 8), np.full((8, 8), 1 / 8)))
    put("mean256", 1 / C)
    tile_group = np.arange(TILES * G)
    put("code", (TILES * G - tile_group) * TAPS)
    put("tap_code", -np.arange(TAPS))
    put("group_of", tile_group % G)
    put("tg_code", TILES * G - tile_group)
    put("row_of", tile_group // G * TR)
    tap = np.arange(TAPS)
    at = np.stack([tap // 3 - 1, tap % 3 - 1])
    low, high = np.maximum(-R, at - REACH), np.minimum(R, at + REACH)
    put("middle", ((low + high) / 2).reshape(-1))
    put("reach", ((high - low) / 2).reshape(-1))
    pix = np.arange(P)
    put("pixel_xy", np.stack([pix % W, pix // W], 1))
    put("minus_d", R - np.arange(D))
    grid = np.zeros((G, 3, TAPS))
    grid[:, 0], grid[:, 1] = np.arange(TAPS) // 3 - 1, np.arange(TAPS) % 3 - 1
    put("grid", grid.reshape(-1))
    put("half", -0.5)
    put("eps", LN_EPS)
    return out


PERMS = ((0, 1, 2, 3, 4, 5, 6, 7), (3, 0, 1, 2, 5, 6, 7, 4), (2, 3, 0, 1, 6, 7, 4, 5), (1, 2, 3, 0, 7, 4, 5, 6),
         (4, 5, 6, 7, 0, 1, 2, 3), (5, 6, 7, 4, 3, 0, 1, 2), (6, 7, 4, 5, 2, 3, 0, 1), (7, 4, 5, 6, 1, 2, 3, 0))


def tap_perms():
    a = np.arange(TAPS).reshape(3, 3)
    turned = [a, np.rot90(a, 1), np.rot90(a, 2), np.rot90(a, 3),
              np.rot90(a.T, 3), np.rot90(a.T, 2), np.rot90(a.T, 1), a.T]
    return np.stack([t.reshape(-1) for t in turned])


def lay_out(inp):
    a = {k: np.asarray(v) for k, v in inp.items()}

    def chunks(w):
        return w.reshape(K, P, -1)

    def d4(w):
        perms = np.array(PERMS)
        full = w[:, :, perms]
        return full.transpose(1, 3, 0, 2).reshape(w.shape[1] * 8, w.shape[0] * 8)

    off = a["L3_conv_off_w"].reshape(C, G, TAPS, 2)
    offb = a["L3_conv_off_b"].reshape(G, TAPS, 2)
    om_w = np.stack([off[..., 0], off[..., 1], a["L3_conv_mask_w"].reshape(C, G, TAPS)], 2).reshape(C, OM)
    om_b = np.stack([offb[..., 0], offb[..., 1], a["L3_conv_mask_b"].reshape(G, TAPS)], 1).reshape(OM)
    parts = {"w0": a["L0_conv_w"].T, "wv": d4(a["L1_conv_w_v"]), "w1": d4(a["L1_conv_w1"]),
             "pw": a["L2_conv_pw_w"].reshape(C, C).T, "in_w": a["L3_conv_in_w"], "om_w": om_w, "out_w": a["L3_conv_out_w"]}
    weights = np.concatenate([chunks(parts[name]) for name in WTS], 2)

    perm = tap_perms()
    w2 = a["L1_conv_w2"].reshape(K, TAPS, P // 8)
    w2x = np.zeros((P // 8, 8, K, TAPS, P // 8, 8), np.float32)
    for g in range(8):
        for c in range(P // 8):
            w2x[:, g, :, :, c, g] = w2[:, perm[g], :].transpose(2, 0, 1)
    b2 = a["L1_conv_b2"].reshape(K, TAPS)[:, perm]
    b2 = np.tile(b2.transpose(1, 0, 2).reshape(8, K * TAPS), (P // 8, 1))

    def two(v):
        return v.reshape(K, P).T

    def taps(w):
        return w.reshape(K, P, TAPS).transpose(1, 0, 2).reshape(P, K * TAPS)

    c = {"q_bias": two(a["L0_conv_bias"]), "dw2_b": two(a["L2_conv_dw_b"]), "pw_b": two(a["L2_conv_pw_b"]),
         "dw3_b": two(a["L3_conv_dw_b"]), "ln_g": two(a["L3_conv_ln_g"]), "ln_b": two(a["L3_conv_ln_b"]),
         "out_b": two(a["L3_conv_out_b"]), "t_gamma": a["L1_conv_gn_gamma"].reshape(P, 1),
         "t_beta": a["L1_conv_gn_beta"].reshape(P, 1), "dw2": taps(a["L2_conv_dw_w"]), "dw3": taps(a["L3_conv_dw_w"]),
         "b2": b2}
    for bn in ("bn1", "bn2"):
        for v in "gbmv":
            c[f"{bn}_{v}"] = two(a[f"L2_conv_{bn}_{v}"])
    cols = np.concatenate([c[name] for name in COLS], 1)
    rows = np.tile(np.concatenate([a["L3_conv_in_b"], om_b])[None], (P, 1))
    arrays = {"x_in": a["x"].reshape(B, C, N), "weights_in": weights, "w2x_in": w2x.reshape(P, K * TAPS * P),
              "cols_in": cols, "rows_in": rows, "consts_in": consts()}
    return {k: np.ascontiguousarray(v) for k, v in arrays.items()}


def kernel(**inputs):
    import concourse.bacc as bacc
    from concourse.bass_utils import run_bass_kernel_spmd as run

    arrays = lay_out(inputs)
    nc = bacc.Bacc("TRN2", target_bir_lowering=False, num_devices=1)
    args = {k: nc.dram_tensor(k, v.shape, F32, kind="ExternalInput").ap() for k, v in arrays.items()}
    out = nc.dram_tensor("out", (B, C, N), F32, kind="ExternalOutput").ap()
    build(nc, out=out, **args)
    r = run(nc, [arrays], core_ids=[0])
    return r.results[0]["out"].reshape(B, C, H, W)
```
